# Optimizing a Trainium2 kernel written in Bass

```python
import numpy as np
import jax
import jax.numpy as jnp

def _softmax(x, axis=-1):
    return jax.nn.softmax(x, axis=axis)

def _gelu(x):
    return jax.nn.gelu(x, approximate=True)

def _silu(x):
    return jax.nn.silu(x)

def _sigmoid(x):
    return jax.nn.sigmoid(x)

def _layernorm(x, axis=-1, eps=1e-05):
    m = jnp.mean(x, axis=axis, keepdims=True)
    v = jnp.var(x, axis=axis, keepdims=True)
    return (x - m) / jnp.sqrt(v + eps)

def _scatter_add(tgt, idx, src, axis=0):
    return tgt.at[idx].add(src)

def _segment_sum(src, seg, n):
    return jax.ops.segment_sum(src, seg, n)
kernel_name = 'mk_gnn_preln_d2_gnn_r8_18cc71'

def setup_inputs(seed: int=0):
    np.random.seed(seed)
    _w = jnp.asarray

    def _rec_inputs():
        import jax
        import jax.numpy as jnp
        _gk = jax.random.key(seed)
        x = -0.0005121 + 1.001 * jax.random.normal(jax.random.fold_in(_gk, 1), (6250, 64), jnp.float32)
        _s = jax.random.randint(jax.random.fold_in(_gk, 2), (100000,), 0, 6250, jnp.int32)
        _d = jax.random.randint(jax.random.fold_in(_gk, 3), (100000,), 0, 6250, jnp.int32)
        _loop = jnp.arange(6250, dtype=jnp.int32)
        src = jnp.concatenate([_s, _d, _loop])
        dst = jnp.concatenate([_d, _s, _loop])
        _o = jnp.argsort(dst, stable=True)
        src = src[_o]
        dst = dst[_o]
        edge_attr_128 = -8.16379e-05 + 0.999858 * jax.random.normal(jax.random.fold_in(_gk, 12), (206250, 128), jnp.float32)
        edge_attr_64 = 0.000189758 + 1.00013 * jax.random.normal(jax.random.fold_in(_gk, 13), (206250, 64), jnp.float32)
        return (x, src, dst, edge_attr_128, edge_attr_64)
    x, src, dst, edge_attr_128, edge_attr_64 = _rec_inputs()

    def _L0_gnn_setup():
        import jax, jax.numpy as jnp
        import numpy as np
        N, E, RBF_DIM, DIM = (6250, 100000, 128, 64)
        BETA, THRESH = (0.5, 14.0)

        def softplus_b05(x):
            z = BETA * x
            safe = jnp.where(z > THRESH, 0.0, z)
            return jnp.where(z > THRESH, x, 1.0 / BETA * jnp.log1p(jnp.exp(safe)))
        key = jax.random.key(seed)
        ks = jax.random.split(key, 10)
        s = 0.02
        return {'new_node': jax.random.normal(ks[0], (N, DIM), jnp.float32), 'rbf': jax.random.normal(ks[1], (E, RBF_DIM), jnp.float32), 'edge_f': jax.random.normal(ks[2], (E, DIM), jnp.float32), 'src': jax.random.randint(ks[3], (E,), 0, N, jnp.int32), 'dst': jax.random.randint(ks[4], (E,), 0, N, jnp.int32), 'W1': jax.random.normal(ks[5], (RBF_DIM, DIM), jnp.float32) * s, 'b1': jnp.zeros((DIM,), jnp.float32), 'W2': jax.random.normal(ks[6], (DIM, DIM), jnp.float32) * s, 'b2': jnp.zeros((DIM,), jnp.float32), 'W3': jax.random.normal(ks[7], (DIM, DIM), jnp.float32) * s, 'b3': jnp.zeros((DIM,), jnp.float32)}
    _L0_gnn_all = _L0_gnn_setup()
    _L0_gnn_in = {k: v for k, v in _L0_gnn_all.items() if k in ('W1', 'b1', 'W2', 'b2', 'W3', 'b3')}
    del _L0_gnn_all

    def _L1_gnn_setup():
        import jax, jax.numpy as jnp
        import numpy as np
        N_NODES = 6250
        N_EDGES = 100000
        IN_C = 64
        key = jax.random.key(seed)
        ks = jax.random.split(key, 7)
        c2 = 2 * IN_C
        return {'features': jax.random.normal(ks[0], (N_NODES, IN_C), dtype=jnp.float32), 'W_lin': jax.random.normal(ks[1], (c2, c2), dtype=jnp.float32) / np.sqrt(c2), 'b_lin': jax.random.normal(ks[2], (c2,), dtype=jnp.float32) * 0.01, 'W_out': jax.random.normal(ks[3], (IN_C, c2), dtype=jnp.float32) / np.sqrt(c2), 'b_out': jax.random.normal(ks[4], (IN_C,), dtype=jnp.float32) * 0.01, 'src': jax.random.randint(ks[5], (N_EDGES,), 0, N_NODES, dtype=jnp.int32), 'dst': jax.random.randint(ks[6], (N_EDGES,), 0, N_NODES, dtype=jnp.int32)}
    _L1_gnn_all = _L1_gnn_setup()
    _L1_gnn_in = {k: v for k, v in _L1_gnn_all.items() if k in ('W_lin', 'b_lin', 'W_out', 'b_out')}
    del _L1_gnn_all
    return {'x': x, 'src': src, 'dst': dst, 'edge_attr_128': edge_attr_128, 'edge_attr_64': edge_attr_64, 'L0_gnn_W1': _L0_gnn_in['W1'], 'L0_gnn_b1': _L0_gnn_in['b1'], 'L0_gnn_W2': _L0_gnn_in['W2'], 'L0_gnn_b2': _L0_gnn_in['b2'], 'L0_gnn_W3': _L0_gnn_in['W3'], 'L0_gnn_b3': _L0_gnn_in['b3'], 'L1_gnn_W_lin': _L1_gnn_in['W_lin'], 'L1_gnn_b_lin': _L1_gnn_in['b_lin'], 'L1_gnn_W_out': _L1_gnn_in['W_out'], 'L1_gnn_b_out': _L1_gnn_in['b_out']}

def reference(x, src, dst, edge_attr_128, edge_attr_64, L0_gnn_W1, L0_gnn_b1, L0_gnn_W2, L0_gnn_b2, L0_gnn_W3, L0_gnn_b3, L1_gnn_W_lin, L1_gnn_b_lin, L1_gnn_W_out, L1_gnn_b_out):
    import jax
    import jax.numpy as jnp

    def _L0_gnn_ref(new_node, rbf, edge_f, src, dst, W1, b1, W2, b2, W3, b3):
        import jax, jax.numpy as jnp
        import numpy as np
        N, E, RBF_DIM, DIM = (6250, 100000, 128, 64)
        BETA, THRESH = (0.5, 14.0)

        def softplus_b05(x):
            z = BETA * x
            safe = jnp.where(z > THRESH, 0.0, z)
            return jnp.where(z > THRESH, x, 1.0 / BETA * jnp.log1p(jnp.exp(safe)))
        h = softplus_b05(rbf @ W1 + b1) @ W2 + b2
        edge_f_new = edge_f @ W3 + b3
        m = new_node[src] * h + edge_f_new
        out = jax.ops.segment_sum(m, dst, num_segments=N)
        return out

    def _L1_gnn_ref(features, W_lin, b_lin, W_out, b_out, src, dst):
        import jax, jax.numpy as jnp
        import numpy as np
        N_NODES = 6250
        N_EDGES = 100000
        IN_C = 64
        n_nodes = features.shape[0]
        ef = jnp.concatenate([features[src], features[dst]], axis=-1)
        att = jax.nn.relu(ef @ W_lin.T + b_lin)
        mx = jax.ops.segment_max(att, dst, num_segments=n_nodes)
        ex = jnp.exp(att - mx[dst])
        den = jax.ops.segment_sum(ex, dst, num_segments=n_nodes)
        alpha = ex / den[dst]
        new_features = jax.ops.segment_sum(alpha * ef, dst, num_segments=n_nodes)
        return new_features @ W_out.T + b_out
    h = jnp.maximum(_layernorm(x, axis=-1), 0.0)
    x = x + _L0_gnn_ref(h, edge_attr_128, edge_attr_64, src, dst, L0_gnn_W1, L0_gnn_b1, L0_gnn_W2, L0_gnn_b2, L0_gnn_W3, L0_gnn_b3)
    h = jnp.maximum(_layernorm(x, axis=-1), 0.0)
    x = x + _L1_gnn_ref(h, L1_gnn_W_lin, L1_gnn_b_lin, L1_gnn_W_out, L1_gnn_b_out, src, dst)
    return x

_drawn_inputs = setup_inputs


def setup_inputs(seed=0):
    import zlib

    import numpy as np

    out = dict(_drawn_inputs(seed))
    spreads = {'L0_gnn_b1': (0.0, 0.352), 'L0_gnn_b2': (0.0, 0.1), 'L0_gnn_b3': (0.0, 0.1)}
    factors = {'edge_attr_128': 3.826,
     'L0_gnn_W1': 3.846,
     'L1_gnn_W_lin': 48.051,
     'L1_gnn_b_lin': 64.0,
     'L1_gnn_b_out': 34.852}
    for name, (base, spread) in spreads.items():
        noise = np.random.default_rng([zlib.crc32(name.encode()), seed]).standard_normal(out[name].shape)
        drawn = base * np.exp(spread * noise) if base else spread * noise
        out[name] = jnp.asarray(drawn.astype(out[name].dtype))
    for name, factor in factors.items():
        out[name] = (out[name] * factor).astype(out[name].dtype)
    return out
```

```python
import concourse.bass as bass
from concourse import mybir
from contextlib import ExitStack

P = 128
NODES, EDGES = 6250, 206250
C = 64
RBF = 128
K = 28
CHUNKS = 58
T = K * CHUNKS
EDGES_PAD = P * T
NB = 49
NODES_PAD = P * NB
GROUP = 4
GROUPS = K // GROUP
PAIR_G = 2 * GROUPS
ROW = 406
ROWS = EDGES_PAD // ROW
U = C * (K + 1)
SKIP = EDGES_PAD + 1
EPS = 1e-5
BANK = 512
assert EDGES <= EDGES_PAD and NODES < NODES_PAD and ROWS * ROW == EDGES_PAD and CHUNKS % 2 == 0

fp32 = mybir.dt.float32
bf16 = mybir.dt.bfloat16
i32 = mybir.dt.int32
ALU = mybir.AluOpType
ACT = mybir.ActivationFunctionType
AX = mybir.AxisListType


class Chain:

    def __init__(self, eng, sem):
        self.eng, self.sem, self.n = eng, sem, 0

    def step(self, ins):
        self.n += 1
        ins.then_inc(self.sem, 1)
        return self.n

    def then_wait(self, ins):
        self.eng.wait_ge(self.sem, self.step(ins))


def over_channels(ap, n=C):
    return ap.unsqueeze(1).to_broadcast([ap.shape[0], n, ap.shape[1]])


def over_last(ap, n=C):
    return ap.unsqueeze(2).to_broadcast([ap.shape[0], ap.shape[1], n])


def flat(ap):
    return ap.rearrange("p c t -> p (c t)")


def layer_norm_relu(nc, chain, act_asks, act_answers, asked, x, out, xc, stat):
    mean, var = stat[:, 0:NB], stat[:, NB:2 * NB]
    sq = out
    chain.then_wait(nc.vector.tensor_reduce(mean, x, AX.X, ALU.add))
    chain.then_wait(nc.vector.tensor_scalar(mean, mean, 1.0 / C, None, ALU.mult))
    chain.then_wait(nc.vector.tensor_tensor(xc, x, over_last(mean), ALU.subtract))
    chain.then_wait(nc.vector.tensor_tensor(sq, xc, xc, ALU.mult))
    chain.then_wait(nc.vector.tensor_reduce(var, sq, AX.X, ALU.add))
    nc.vector.tensor_scalar(var, var, 1.0 / C, EPS, ALU.mult, ALU.add).then_inc(act_asks, 1)
    chain.eng.wait_ge(act_answers, asked)
    chain.then_wait(nc.vector.reciprocal(var, var))
    return nc.vector.scalar_tensor_tensor(out, xc, 0.0, over_last(var), ALU.max, ALU.mult)


def setup_phase(nc, d, s, m):
    with ExitStack() as ctx:
        sb = lambda name, shape, dt=fp32: ctx.enter_context(nc.sbuf_tensor(name, shape, dt))
        dst_i = sb("dst_i", [P, T + 1], i32)
        dst_f = sb("dst_f", [P, T + 1])
        first_i = sb("first_i", [P, ROWS], i32)
        first_f = sb("first_f", [P, ROWS])
        hit = sb("hit", [P, ROWS])
        h1 = sb("h1", [P, NB, C])
        xc = sb("xc1", [P, NB, C])
        stat = sb("stat1", [P, 2 * NB])
        node_i = sb("node_i", [P, NB], i32)
        w1_raw = sb("w1_raw", [RBF, C])
        w2_raw = sb("w2_raw", [C, C])
        b1_raw = sb("b1_raw", [C, 1])
        b23_f = sb("b23_f", [3, 2 * C])
        b23_hi = sb("b23_hi", [3, 2 * C], bf16)
        b23_mid = sb("b23_mid", [3, 2 * C], bf16)
        b23_lo = sb("b23_lo", [3, 2 * C], bf16)
        b23_r = sb("b23_r", [3, 2 * C])
        b23_s = sb("b23_s", [3, 2 * C])
        block = ctx.enter_context(nc.Block())

        @block.sync
        def _(sp):
            sp.dma_start(first_i[:, :], d.dst_first.unsqueeze(0).to_broadcast([P, ROWS])).then_inc(s.first_in, 16)
            sp.dma_start(m.x[:, :, :], d.x.rearrange("(p b) c -> p b c", b=NB)).then_inc(s.x_in, 16)
            sp.dma_start(dst_i[:, :], d.dst_ext).then_inc(s.dst_in, 16)
            sp.dma_start(m.src[:, :], d.src.rearrange("(p t) -> p t", t=T)).then_inc(s.src_in, 16)
            sp.wait_ge(s.h1_ready, 1)
            sp.dma_start(d.h1_tab.rearrange("(p b) c -> p b c", b=NB), h1[:, :, :]).then_inc(s.h1_stored, 16)
            sp.wait_ge(s.h1_stored, 16)

        @block.gpsimd
        def _(pool):
            nc.gpsimd.iota(node_i[:, :], [[1, NB]], base=0, channel_multiplier=NB).then_inc(s.node_iota, 1)
            nc.gpsimd.iota(m.ident_i[:, :], [[1, P]], base=0, channel_multiplier=-1).then_inc(s.node_iota, 1)
            nc.gpsimd.iota(m.pstart_i[:, :], [[0, 1]], base=0, channel_multiplier=T).then_inc(s.node_iota, 1)
            nc.gpsimd.iota(m.kstart_i[:, :], [[K, CHUNKS]], base=0, channel_multiplier=0).then_inc(s.node_iota, 1)
            nc.gpsimd.iota(m.slot_i[:, :], [[1, K + 1]], base=-1, channel_multiplier=0).then_inc(s.node_iota, 1)
            pool.wait_ge(s.row_ready, 1)
            for b in range(NB):
                nc.gpsimd.indirect_dma_start(m.search[:, b, :], None, d.dst_rows,
                                             bass.IndirectOffsetOnAxis(m.row_i[:, b:b + 1], 0)).then_inc(s.search_in, 16)

        @block.scalar
        def _(act):
            act.dma_start(w1_raw[:, :], d.W1).then_inc(s.w_in, 16)
            act.dma_start(w2_raw[:, :], d.W2).then_inc(s.w_in, 16)
            act.dma_start(b1_raw[:, :], d.b1.rearrange("(c o) -> c o", o=1)).then_inc(s.w_in, 16)
            act.dma_start(b23_f[:, 0:C], d.b2.unsqueeze(0).to_broadcast([3, C])).then_inc(s.w_in, 16)
            act.dma_start(b23_f[:, C:2 * C], d.b3.unsqueeze(0).to_broadcast([3, C])).then_inc(s.w_in, 16)
            act.wait_ge(s.var1_ready, 1)
            nc.scalar.activation(stat[:, NB:2 * NB], stat[:, NB:2 * NB], ACT.Sqrt).then_inc(s.std1_ready, 1)

        @block.vector
        def _(dve):
            ch = Chain(dve, s.setup_dve)
            dve.wait_ge(s.node_iota, 5)
            ch.then_wait(nc.vector.tensor_copy(m.node[:, :], node_i[:, :]))
            ch.then_wait(nc.vector.tensor_scalar(m.ident[:, :], m.ident_i[:, :], 0.0, None, ALU.is_equal))
            dve.wait_ge(s.first_in, 16)
            ch.then_wait(nc.vector.tensor_copy(first_f[:, :], first_i[:, :]))
            for b in range(NB):
                ch.then_wait(nc.vector.tensor_scalar(hit[:, :], first_f[:, :], m.node[:, b:b + 1], 0.0, ALU.is_le, ALU.add,
                                                accum_out=m.row[:, b:b + 1]))
            dve.wait_ge(s.setup_dve, ch.n)
            ch.then_wait(nc.vector.tensor_scalar(m.row[:, :], m.row[:, :], -1.0, 0.0, ALU.add, ALU.max))
            nc.vector.tensor_copy(m.row_i[:, :], m.row[:, :]).then_inc(s.row_ready, 1)
            dve.wait_ge(s.x_in, 16)
            layer_norm_relu(nc, ch, s.var1_ready, s.std1_ready, 1, m.x[:, :, :], h1[:, :, :], xc[:, :, :],
                            stat).then_inc(s.h1_ready, 1)
            dve.wait_ge(s.dst_in, 16)
            ch.then_wait(nc.vector.tensor_copy(dst_f[:, :], dst_i[:, :]))
            ch.then_wait(nc.vector.tensor_tensor(m.same[:, :], dst_f[:, 1:T + 1], dst_f[:, 0:T], ALU.is_equal))
            ch.then_wait(nc.vector.tensor_copy(m.d0[:, :], dst_f[:, 1:2]))
            ch.then_wait(nc.vector.tensor_tensor(m.link[:, :], dst_f[:, 1:2], dst_f[:, T:T + 1], ALU.is_equal))
            ch.then_wait(nc.vector.tensor_tensor(m.link[:, :], m.link[:, :], m.same[:, 0:1], ALU.mult))
            ch.then_wait(nc.vector.tensor_copy(m.d0_i[:, :], m.d0[:, :]))
            ch.then_wait(nc.vector.tensor_copy(m.pstart[:, :], m.pstart_i[:, :]))
            ch.then_wait(nc.vector.tensor_copy(m.kstart[:, :], m.kstart_i[:, :]))
            ch.then_wait(nc.vector.tensor_copy(m.slot[:, :], m.slot_i[:, :]))
            dve.wait_ge(s.w_in, 80)
            ch.then_wait(nc.vector.tensor_scalar(m.w1h[:, :], w1_raw[:, :], 0.5, None, ALU.mult))
            ch.then_wait(nc.vector.tensor_scalar(m.b1h[:, :], b1_raw[:, :], 0.5, None, ALU.mult))
            dve.wait_ge(s.w3_in, 16)
            ch.then_wait(nc.vector.tensor_scalar(m.w23[0:C, 0:C], w2_raw[:, :], 2.0, None, ALU.mult))
            ch.then_wait(nc.vector.tensor_copy(b23_hi[:, :], b23_f[:, :]))
            ch.then_wait(nc.vector.tensor_tensor(b23_r[:, :], b23_f[:, :], b23_hi[:, :], ALU.subtract))
            ch.then_wait(nc.vector.tensor_copy(b23_mid[:, :], b23_r[:, :]))
            ch.then_wait(nc.vector.tensor_tensor(b23_r[:, :], b23_r[:, :], b23_mid[:, :], ALU.subtract))
            ch.then_wait(nc.vector.tensor_copy(b23_lo[:, :], b23_r[:, :]))
            ch.then_wait(nc.vector.tensor_scalar(b23_s[:, :], b23_hi[:, :], m.ident[0:3, 0:1], None, ALU.mult))
            ch.then_wait(nc.vector.scalar_tensor_tensor(b23_s[:, :], b23_mid[:, :], m.ident[0:3, 1:2], b23_s[:, :],
                                                        ALU.mult, ALU.add))
            ch.then_wait(nc.vector.scalar_tensor_tensor(b23_s[:, :], b23_lo[:, :], m.ident[0:3, 2:3], b23_s[:, :],
                                                        ALU.mult, ALU.add))
            for j in range(GROUP):
                ch.step(nc.vector.tensor_copy(m.bias_rows[:, j * 2 * C:(j + 1) * 2 * C], b23_s[:, :]))
            ch.step(nc.vector.memset(m.bias_ones[:, :], 1.0))
            dve.wait_ge(s.setup_dve, ch.n)

        @block.tensor
        def _(pe):
            pe.wait_ge(s.h1_ready, 1)


def sum_phase(nc, d, s, m):
    with ExitStack() as ctx:
        sb = lambda name, shape, dt=fp32: ctx.enter_context(nc.sbuf_tensor(name, shape, dt))
        pb = lambda name, shape: ctx.enter_context(nc.psum_tensor(name, shape, fp32))
        GC = GROUP * P
        arena = m.search[:, :, :].rearrange("p b r -> p (b r)").bitcast(fp32)
        KP = K * P
        rbf = [arena[:, q * KP:(q + 1) * KP] for q in range(2)]
        spef = [arena[:, (2 + q) * KP:(3 + q) * KP] for q in range(2)]
        rows = [arena[:, 4 * KP + q * K * C:4 * KP + (q + 1) * K * C].rearrange("p (t c) -> p t c", c=C) for q in range(2)]
        g = [sb(f"h_src{q}", [P, K, C]) for q in range(2)]
        idx = [sb(f"idx1_{q}", [P, K], i32) for q in range(2)]
        mask = [sb(f"mask1_{q}", [P, C, K + 1]) for q in range(2)]
        msg = sb("msg", [P, C, K + 1])
        run = sb("run", [P, C, K + 1])
        zeros = sb("zeros", [P, K, C])
        zc = [sb(f"zc{q}", [C, GC]) for q in range(2)]
        lg = [sb(f"lg{q}", [C, GC]) for q in range(2)]
        hit2 = sb("hit2", [P, ROW])
        z = [pb(f"z{q}", [C, GC]) for q in range(2)]
        hw = [pb(f"hw{q}", [P, GROUP, 2 * C]) for q in range(2)]
        tail_ps = pb("tail_ps", [C, BANK])[:, 0:P]
        link_ps = pb("link_ps", [C, BANK])[:, 0:P]
        carry_ps = pb("carry_ps", [P, BANK])[:, 0:C]
        tail_t = sb("tail_t", [C, P])
        link_t = sb("link_t", [C, P])
        open_t = sb("open_t", [C, P + 1])
        tail = sb("tail1", [P, C])
        seg_row = sb("seg_row", [P, C])
        block = ctx.enter_context(nc.Block())
        s1_rows = d.s1.rearrange("(p t) c -> p t c", t=T)
        v_rows = d.v.rearrange("(p t) c -> p t c", t=T)

        @block.sync
        def _(sp):
            def load(i, q, first):
                if not first:
                    sp.wait_ge(s.z_ready, i * PAIR_G + (q - 1) * GROUPS)
                    sp.wait_ge(s.hw_ready, i * PAIR_G + (q - 1) * GROUPS)
                k = i * 2 + q
                sp.dma_start(rbf[q], d.rbf_t[:, bass.ds(k * KP, KP)]).then_inc(s.edge_in[q], 16)
                sp.dma_start(spef[q][C:2 * C, :], d.ef_t[:, bass.ds(k * KP, KP)]).then_inc(s.edge_in[q], 16)
                sp.dma_start(v_rows[:, bass.ds(k * K, K), :], zeros[:, :, :]).then_inc(s.v_zeroed, 16)

            def store(i, q):
                k = i * 2 + q
                sp.wait_ge(s.rows1_ready, k + 1)
                sp.dma_start(s1_rows[:, bass.ds(k * K, K), :], rows[q]).then_inc(s.rows1_stored[q], 16)

            sp.wait_ge(s.cnt_ready, 1)
            sp.dma_start(d.cnt_tab[1:1 + NODES_PAD, :].rearrange("(p b) o -> p (b o)", b=NB), m.cnt[:, :]).then_inc(s.cnt_stored, 16)
            sp.dma_start(d.cnt_tab[0:1, :], zeros[0:1, 0, 0:1]).then_inc(s.cnt_stored, 16)
            sp.wait_ge(s.cnt_stored, 32)
            sp.dma_start(m.start[:, :], d.cnt_tab[0:NODES_PAD, :].rearrange("(p b) o -> p (b o)", b=NB)).then_inc(s.start_in, 16)
            load(0, 0, True)
            load(0, 1, True)
            with sp.Fori(1, CHUNKS // 2) as i:
                load(i, 0, False)
                store(i - 1, 0)
                load(i, 1, False)
                store(i - 1, 1)
            store(CHUNKS // 2 - 1, 0)
            store(CHUNKS // 2 - 1, 1)
            sp.wait_ge(s.rows1_stored[0], 16 * (CHUNKS // 2))
            sp.wait_ge(s.rows1_stored[1], 16 * (CHUNKS // 2))
            sp.wait_ge(s.v_zeroed, 16 * CHUNKS)

        @block.gpsimd
        def _(pool):
            def gather(i, q, first):
                if not first:
                    pool.wait_ge(s.msg_ready, i * PAIR_G + (q - 1) * GROUPS)
                nc.gpsimd.tensor_copy(idx[q][:, :], m.src[:, bass.ds((i * 2 + q) * K, K)]).then_inc(s.idx1_ready, 1)
                pool.wait_ge(s.idx1_ready, i * 2 + q + 1)
                pool.sem_inc(s.idx1_seen, 1)
                for t in range(K):
                    nc.gpsimd.indirect_dma_start(g[q][:, t, :], None, d.h1_tab,
                                                 bass.IndirectOffsetOnAxis(idx[q][:, t:t + 1], 0)).then_inc(s.gather1_in[q], 16)

            pool.wait_ge(s.src_in, 16)
            gather(0, 0, True)
            gather(0, 1, True)
            with pool.Fori(1, CHUNKS // 2) as i:
                gather(i, 0, False)
                gather(i, 1, False)
            pool.wait_ge(s.cnt_stored, 32)
            pool.wait_ge(s.d0_ready, 1)
            nc.gpsimd.indirect_dma_start(m.d0_cnt[:, :], None, d.cnt_tab,
                                         bass.IndirectOffsetOnAxis(m.d0_i[:, 0:1], 0)).then_inc(s.d0_cnt_in, 16)
            pool.wait_ge(s.seg_idx_ready, 1)
            pool.wait_ge(s.rows1_stored[0], 16 * (CHUNKS // 2))
            pool.wait_ge(s.rows1_stored[1], 16 * (CHUNKS // 2))
            nc.gpsimd.indirect_dma_start(seg_row[:, :], None, d.s1,
                                         bass.IndirectOffsetOnAxis(m.seg_read_i[:, 0:1], 0)).then_inc(s.seg1_in, 16)
            pool.wait_ge(s.seg1_ready, 1)
            nc.gpsimd.indirect_dma_start(d.s1, bass.IndirectOffsetOnAxis(m.seg_write_i[:, 0:1], 0), seg_row[:, :], None,
                                         bounds_check=EDGES_PAD - 1, oob_is_err=False).then_inc(s.seg1_stored, 16)
            pool.wait_ge(s.seg1_stored, 16)

        @block.tensor
        def _(pe):
            def hidden(i, j, first):
                q, gi = j // GROUPS % 2, i * PAIR_G + j
                if j % GROUPS == 0:
                    pe.wait_ge(s.edge_in[q], 32 * (i + 1))
                if not (first and j < 2):
                    pe.wait_ge(s.sp_ready, gi - 1)
                col = (j % GROUPS) * GC
                nc.tensor.matmul(z[j % 2][:, :], m.w1h[:, :], rbf[q][:, col:col + GC], start=True, stop=True).then_inc(s.z_ready, 1)

            def messages(i, j, first):
                q, gi = j // GROUPS % 2, i * PAIR_G + j
                pe.wait_ge(s.sp_ready, gi + 1)
                if not (first and j < 2):
                    pe.wait_ge(s.msg_ready, gi - 1)
                out = hw[j % 2]
                for t in range(GROUP):
                    col = (j % GROUPS) * GC + t * P
                    nc.tensor.matmul(out[:, t, :], spef[q][:, col:col + P], m.w23[:, :], start=(t == 0), stop=False,
                                     skip_group_check=True)
                nc.tensor.matmul(out[:, :, :].rearrange("p t c -> p (t c)"), m.bias_ones[:, :], m.bias_rows[:, :],
                                 start=False, stop=True, skip_group_check=True).then_inc(s.hw_ready, 1)

            def pair(i, first):
                for j in range(PAIR_G):
                    hidden(i, j, first)
                    if j > 0:
                        messages(i, j - 1, first)
                    elif not first:
                        messages(i - 1, PAIR_G - 1, False)

            pair(0, True)
            with pe.Fori(1, CHUNKS // 2) as i:
                pair(i, False)
            messages(CHUNKS // 2 - 1, PAIR_G - 1, False)
            pe.wait_ge(s.tail1_ready, 1)
            nc.tensor.transpose(tail_ps[:, :], tail[:, :], m.ident[:, :])
            nc.tensor.transpose(link_ps[:, :], m.link[:, 0:1].to_broadcast([P, C]), m.ident[:, :]).then_inc(s.tail1_turned, 1)
            pe.wait_ge(s.open1_ready, 1)
            nc.tensor.transpose(carry_ps[:, :], open_t[:, 0:P], m.ident[0:C, 0:C]).then_inc(s.carry1_ready, 1)

        @block.scalar
        def _(act):
            def softplus(i, j):
                gi = i * PAIR_G + j
                act.wait_ge(s.z_clamped, gi + 1)
                nc.scalar.activation(lg[j % 2][:, :], zc[j % 2][:, :], ACT.Exp).then_inc(s.exp_ready, 1)
                act.wait_ge(s.exp_ready, gi + 1)
                nc.scalar.activation(lg[j % 2][:, :], lg[j % 2][:, :], ACT.Ln, bias=1.0).then_inc(s.log_ready, 1)

            def spread_mask(k, q, first):
                if not first:
                    act.wait_ge(s.scan1_ready, k - 1)
                nc.scalar.copy(mask[q][:, :, 1:], over_channels(m.same[:, bass.ds(k * K, K)])).then_inc(s.mask1_ready, 1)

            def to_rows(k, q, first):
                act.wait_ge(s.scan1_ready, k + 1)
                if not first:
                    act.wait_ge(s.rows1_stored[q], 16 * (first_half(k)))
                nc.scalar.copy(rows[q], run[:, :, 1:].rearrange("p c t -> p t c")).then_inc(s.rows1_ready, 1)

            half = {}

            def first_half(k):
                return half["stores"]

            def pair(i, first):
                for j in range(PAIR_G):
                    softplus(i, j)
                    q = j // GROUPS
                    if j % GROUPS == 3 and not (first and q == 0):
                        half["stores"] = i - 1 if q == 0 else i
                        to_rows(i * 2 + q - 1, 1 - q, first or False)
                    if j % GROUPS == 5:
                        if q == 0:
                            spread_mask(i * 2 + 1, 1, first)
                        else:
                            spread_mask(i * 2 + 2, 0, False)

            nc.scalar.preload_act_table_set("natural_log_exp_and_others")
            act.wait_ge(s.mask1_zero, 2)
            spread_mask(0, 0, True)
            pair(0, True)
            with act.Fori(1, CHUNKS // 2 - 1) as i:
                pair(i, False)
            i = CHUNKS // 2 - 1
            for j in range(PAIR_G):
                softplus(i, j)
                q = j // GROUPS
                if j % GROUPS == 3:
                    half["stores"] = i - 1 if q == 0 else i
                    to_rows(i * 2 + q - 1, 1 - q, False)
                if j == 5:
                    spread_mask(i * 2 + 1, 1, False)
            half["stores"] = CHUNKS // 2 - 1
            to_rows(CHUNKS - 1, 1, False)

        @block.vector
        def _(dve):
            ch = Chain(dve, s.sum_dve)
            ch.step(nc.vector.memset(zeros[:, :, :], 0.0))
            ch.step(nc.vector.memset(run[:, :, :], 0.0))
            ch.step(nc.vector.memset(open_t[:, :], 0.0))
            nc.vector.memset(mask[0][:, :, 0:1], 0.0).then_inc(s.mask1_zero, 1)
            nc.vector.memset(mask[1][:, :, 0:1], 0.0).then_inc(s.mask1_zero, 1)
            dve.wait_ge(s.search_in, 16 * NB)
            for b in range(NB):
                ch.then_wait(nc.vector.tensor_scalar(hit2[:, :], m.search[:, b, :], m.node[:, b:b + 1], 0.0, ALU.is_le, ALU.add,
                                                accum_out=m.cnt[:, b:b + 1]))
            dve.wait_ge(s.sum_dve, ch.n)
            nc.vector.scalar_tensor_tensor(m.cnt[:, :], m.row[:, :], float(ROW), m.cnt[:, :], ALU.mult, ALU.add).then_inc(s.cnt_ready, 1)
            dve.wait_ge(s.cnt_ready, 1)
            dve.wait_ge(s.start_in, 16)
            ch.then_wait(nc.vector.tensor_tensor(m.has[:, :], m.cnt[:, :], m.start[:, :], ALU.is_gt))
            ch.then_wait(nc.vector.tensor_scalar(m.tmp[:, :], m.cnt[:, :], -1.0, 0.0, ALU.add, ALU.max))
            ch.then_wait(nc.vector.tensor_copy(m.last_i[:, :], m.tmp[:, :]))
            ch.then_wait(nc.vector.scalar_tensor_tensor(m.tmp[:, :], m.start[:, :], float(-SKIP), m.has[:, :], ALU.add, ALU.mult))
            ch.then_wait(nc.vector.tensor_scalar(m.tmp[:, :], m.tmp[:, :], float(SKIP), None, ALU.add))
            ch.then_wait(nc.vector.tensor_copy(m.start_i[:, :], m.tmp[:, :]))
            ch.then_wait(nc.vector.tensor_scalar(m.d0_t[:, :], m.d0[:, :], 1.0, None, ALU.add))
            nc.vector.tensor_copy(m.d0_i[:, :], m.d0_t[:, :]).then_inc(s.d0_ready, 1)

            def clamp(i, j):
                gi = i * PAIR_G + j
                dve.wait_ge(s.z_ready, gi + 1)
                nc.vector.tensor_scalar(zc[j % 2][:, :], z[j % 2][:, :], m.b1h[:, 0:1], 14.0, ALU.add, ALU.min).then_inc(s.z_clamped, 1)

            def softplus_max(i, j, first):
                q, gi = j // GROUPS % 2, i * PAIR_G + j
                dve.wait_ge(s.log_ready, gi + 1)
                col = (j % GROUPS) * GC
                nc.vector.scalar_tensor_tensor(spef[q][0:C, col:col + GC], z[j % 2][:, :], m.b1h[:, 0:1], lg[j % 2][:, :],
                                               ALU.add, ALU.max).then_inc(s.sp_ready, 1)

            def message(i, j):
                q, gi = j // GROUPS % 2, i * PAIR_G + j
                t0 = (j % GROUPS) * GROUP
                if j % GROUPS == 0:
                    dve.wait_ge(s.gather1_in[q], 16 * K * (i + 1))
                dve.wait_ge(s.hw_ready, gi + 1)
                out = msg[:, :, 1 + t0:1 + t0 + GROUP]
                nc.vector.tensor_tensor(out, g[q][:, t0:t0 + GROUP, :].rearrange("p t c -> p c t"),
                                        hw[j % 2][:, :, 0:C].rearrange("p t c -> p c t"), ALU.mult).then_inc(s.msg_scaled, 1)
                dve.wait_ge(s.msg_scaled, gi + 1)
                nc.vector.tensor_tensor(out, out, hw[j % 2][:, :, C:2 * C].rearrange("p t c -> p c t"), ALU.add).then_inc(s.msg_ready, 1)
                if j % GROUPS == GROUPS - 1:
                    k = i * 2 + q
                    nc.vector.tensor_copy(msg[:, :, 0:1], run[:, :, K:K + 1]).then_inc(s.carry1_in, 1)
                    dve.wait_ge(s.carry1_in, k + 1)
                    dve.wait_ge(s.msg_ready, gi + 1)
                    dve.wait_ge(s.mask1_ready, k + 1)
                    dve.wait_ge(s.rows1_ready, k)
                    nc.vector.tensor_tensor_scan(flat(run[:, :, :]), flat(mask[q][:, :, :]), flat(msg[:, :, :]), 0.0,
                                                 ALU.mult, ALU.add).then_inc(s.scan1_ready, 1)
                    dve.wait_ge(s.scan1_ready, k + 1)

            def pair(i, first):
                for j in range(PAIR_G):
                    clamp(i, j)
                    for lag, work in ((1, softplus_max), (2, message)):
                        if j >= lag:
                            work(i, j - lag) if work is message else work(i, j - lag, first)
                        elif not first:
                            work(i - 1, j - lag + PAIR_G) if work is message else work(i - 1, j - lag + PAIR_G, False)

            pair(0, True)
            with dve.Fori(1, CHUNKS // 2) as i:
                pair(i, False)
            i = CHUNKS // 2 - 1
            message(i, PAIR_G - 2)
            softplus_max(i, PAIR_G - 1, False)
            message(i, PAIR_G - 1)

            nc.vector.tensor_copy(tail[:, :], run[:, :, K]).then_inc(s.tail1_ready, 1)
            dve.wait_ge(s.tail1_turned, 1)
            ch.then_wait(nc.vector.tensor_copy(tail_t[:, :], tail_ps[:, :]))
            ch.then_wait(nc.vector.tensor_copy(link_t[:, :], link_ps[:, :]))
            nc.vector.tensor_tensor_scan(open_t[:, 1:P + 1], link_t[:, :], tail_t[:, :], 0.0, ALU.mult, ALU.add).then_inc(s.open1_ready, 1)
            dve.wait_ge(s.d0_cnt_in, 16)
            seg_t, ok = m.seg_t[:, :], m.seg_ok[:, :]
            ch.then_wait(nc.vector.scalar_tensor_tensor(seg_t, m.d0_cnt[:, :], -1.0, m.pstart[:, :], ALU.add, ALU.subtract))
            ch.then_wait(nc.vector.scalar_tensor_tensor(ok, seg_t, float(T), m.same[:, 0:1], ALU.is_lt, ALU.mult))
            ch.then_wait(nc.vector.tensor_scalar(seg_t, seg_t, float(T - 1), 0.0, ALU.min, ALU.max))
            ch.then_wait(nc.vector.tensor_tensor(m.d0_t[:, :], seg_t, m.pstart[:, :], ALU.add))
            ch.then_wait(nc.vector.tensor_copy(m.seg_read_i[:, :], m.d0_t[:, :]))
            ch.then_wait(nc.vector.scalar_tensor_tensor(m.d0_t[:, :], m.d0_t[:, :], float(-SKIP), ok, ALU.add, ALU.mult))
            ch.then_wait(nc.vector.tensor_scalar(m.d0_t[:, :], m.d0_t[:, :], float(SKIP), None, ALU.add))
            nc.vector.tensor_copy(m.seg_write_i[:, :], m.d0_t[:, :]).then_inc(s.seg_idx_ready, 1)
            dve.wait_ge(s.seg1_in, 16)
            dve.wait_ge(s.carry1_ready, 1)
            nc.vector.tensor_tensor(seg_row[:, :], seg_row[:, :], carry_ps[:, :], ALU.add).then_inc(s.seg1_ready, 1)


def node_phase(nc, d, s, m):
    with ExitStack() as ctx:
        sb = lambda name, shape, dt=fp32: ctx.enter_context(nc.sbuf_tensor(name, shape, dt))
        pb = lambda name, shape: ctx.enter_context(nc.psum_tensor(name, shape, fp32))
        agg = sb("agg", [P, NB, C])
        tab = sb("tab", [P, NB, 2 * C])
        h2 = sb("h2", [P, NB, C])
        bd = sb("bd", [P, NB, C])
        xc = sb("xc2", [P, NB, C])
        stat = sb("stat2", [P, 2 * NB])
        wab = sb("wab", [C + 1, 2 * C])
        h2t = [sb(f"h2t{q}", [C + 1, P]) for q in range(2)]
        turn = [pb(f"turn{q}", [C, BANK])[:, 0:P] for q in range(2)]
        ab = [pb(f"ab{q}", [P, BANK])[:, 0:2 * C] for q in range(2)]
        block = ctx.enter_context(nc.Block())

        @block.gpsimd
        def _(pool):
            for b in range(NB):
                nc.gpsimd.indirect_dma_start(agg[:, b, :], None, d.s1,
                                             bass.IndirectOffsetOnAxis(m.last_i[:, b:b + 1], 0)).then_inc(s.agg_in, 16)
            pool.wait_ge(s.bd_ready, 1)
            for b in range(NB):
                nc.gpsimd.indirect_dma_start(d.v, bass.IndirectOffsetOnAxis(m.start_i[:, b:b + 1], 0), bd[:, b, :], None,
                                             bounds_check=EDGES_PAD - 1, oob_is_err=False).then_inc(s.v_stored, 16)
            pool.wait_ge(s.bd_stored, 16)
            pool.wait_ge(s.d0n_ready, 1)
            nc.gpsimd.indirect_dma_start(m.b_open[:, :], None, d.b_tab,
                                         bass.IndirectOffsetOnAxis(m.d0_i[:, 0:1], 0)).then_inc(s.b_open_in, 16)
            pool.wait_ge(s.v_stored, 16 * NB)
            pool.wait_ge(s.b_open_in, 16)

        @block.sync
        def _(sp):
            sp.dma_start(wab[0:C, 0:C], d.wlin_t[0:C, 0:C]).then_inc(s.wab_in, 16)
            sp.dma_start(wab[0:C, C:2 * C], d.wlin_t[C:2 * C, 0:C]).then_inc(s.wab_in, 16)
            sp.wait_ge(s.wab_zero, 1)
            sp.dma_start(wab[C:C + 1, C:2 * C], d.b_lin[0:C].unsqueeze(0)).then_inc(s.wab_in, 16)
            sp.wait_ge(s.tab_ready, 1)
            sp.dma_start(d.tab2.rearrange("(p b) c -> p b c", b=NB), tab[:, :, :]).then_inc(s.tab_stored, 16)
            sp.wait_ge(s.bd_ready, 1)
            sp.dma_start(d.b_tab.rearrange("(p b) c -> p b c", b=NB), bd[:, :, :]).then_inc(s.bd_stored, 16)
            sp.wait_ge(s.tab_stored, 16)
            sp.wait_ge(s.bd_stored, 16)

        @block.scalar
        def _(act):
            act.wait_ge(s.var2_ready, 1)
            nc.scalar.activation(stat[:, NB:2 * NB], stat[:, NB:2 * NB], ACT.Sqrt).then_inc(s.std2_ready, 1)
            act.wait_ge(s.h2_ready, 1)
            nc.scalar.copy(tab[:, :, C:2 * C], h2[:, :, :]).then_inc(s.tab_h2, 1)
            for b in range(NB):
                act.wait_ge(s.turned2, b + 1)
                if b >= 2:
                    act.wait_ge(s.ab_ready, b - 1)
                else:
                    act.wait_ge(s.h2t_ones, 2)
                nc.scalar.copy(h2t[b % 2][0:C, :], turn[b % 2][:, :]).then_inc(s.h2t_ready, 1)

        @block.tensor
        def _(pe):
            pe.wait_ge(s.h2_ready, 1)
            pe.wait_ge(s.wab_in, 48)

            def turn_block(b):
                if b >= 2:
                    pe.wait_ge(s.h2t_ready, b - 1)
                nc.tensor.transpose(turn[b % 2][:, :], h2[:, b, :], m.ident[:, :]).then_inc(s.turned2, 1)

            turn_block(0)
            for b in range(NB):
                if b + 1 < NB:
                    turn_block(b + 1)
                pe.wait_ge(s.h2t_ready, b + 1)
                if b >= 2:
                    pe.wait_ge(s.ab_out, b - 1)
                nc.tensor.matmul(ab[b % 2][:, :], h2t[b % 2][:, :], wab[:, :], start=True, stop=True).then_inc(s.ab_ready, 1)

        @block.vector
        def _(dve):
            ch = Chain(dve, s.node_dve)
            nc.vector.memset(wab[C:C + 1, :], 0.0).then_inc(s.wab_zero, 1)
            for q in range(2):
                nc.vector.memset(h2t[q][C:C + 1, :], 1.0).then_inc(s.h2t_ones, 1)
            ch.then_wait(nc.vector.tensor_copy(m.d0_i[:, :], m.d0[:, :]))
            ch.eng.wait_ge(s.agg_in, 16 * NB)
            ch.then_wait(nc.vector.tensor_tensor(agg[:, :, :], agg[:, :, :], over_last(m.has[:, :]), ALU.mult))
            ch.then_wait(nc.vector.tensor_tensor(m.x[:, :, :], m.x[:, :, :], agg[:, :, :], ALU.add))
            layer_norm_relu(nc, ch, s.var2_ready, s.std2_ready, 1, m.x[:, :, :], h2[:, :, :], xc[:, :, :],
                            stat).then_inc(s.h2_ready, 1)
            for b in range(NB):
                dve.wait_ge(s.ab_ready, b + 1)
                ch.step(nc.vector.tensor_copy(tab[:, b, 0:C], ab[b % 2][:, 0:C]))
                nc.vector.tensor_copy(bd[:, b, :], ab[b % 2][:, C:2 * C]).then_inc(s.ab_out, 1)
            dve.wait_ge(s.node_dve, ch.n)
            dve.wait_ge(s.ab_out, NB)
            dve.wait_ge(s.tab_h2, 1)
            nc.vector.memset(stat[:, 0:1], 0.0).then_inc(s.tab_ready, 1)
            nc.vector.memset(stat[:, 1:2], 0.0).then_inc(s.bd_ready, 1)
            nc.vector.memset(stat[:, 2:3], 0.0).then_inc(s.d0n_ready, 1)


def softmax_phase(nc, d, s, m):
    with ExitStack() as ctx:
        sb = lambda name, shape, dt=fp32: ctx.enter_context(nc.sbuf_tensor(name, shape, dt))
        pb = lambda name, shape: ctx.enter_context(nc.psum_tensor(name, shape, fp32))
        g = [sb(f"ah_src{q}", [P, K, 2 * C]) for q in range(2)]
        idx = [sb(f"idx2_{q}", [P, K], i32) for q in range(2)]
        vin = sb("vin", [P, K, C])
        rows = sb("rows2", [P, K, 2 * C])
        unit = lambda name: sb(name, [P, C, K + 1])
        mask = [unit(f"mask2_{q}") for q in range(2)]
        vct = [unit(f"vct{q}") for q in range(2)]
        bexp, zb = unit("bexp"), unit("zb")
        mx = [unit(f"mx{q}") for q in range(2)]
        pw = [unit(f"pw{q}") for q in range(2)]
        wt = [unit(f"wt{q}") for q in range(2)]
        qs, den, num = unit("qs"), unit("den"), unit("num")
        block = ctx.enter_context(nc.Block())
        s2_rows = d.s2.rearrange("(p t) c -> p t c", t=T)
        m2_rows = d.m2.rearrange("(p k) u -> p k u", k=CHUNKS)
        v_rows = d.v.rearrange("(p t) c -> p t c", t=T)
        LASTP = CHUNKS // 2 - 1

        @block.sync
        def _(sp):
            def load(k, first):
                if not first:
                    sp.wait_ge(s.vct_ready, k)
                sp.dma_start(vin[:, :, :], v_rows[:, bass.ds(k * K, K), :]).then_inc(s.v_in, 16)

            def store_max(k, q):
                sp.wait_ge(s.mx_ready, k + 1)
                sp.dma_start(m2_rows[:, bass.ds(k, 1), :], mx[q][:, :, :].rearrange("p c t -> p (c t)").unsqueeze(1)).then_inc(s.mx_stored[q], 16)

            def store_rows(k):
                sp.wait_ge(s.rows2_ready, k + 1)
                sp.dma_start(s2_rows[:, bass.ds(k * K, K), :], rows[:, :, :]).then_inc(s.rows2_stored, 16)

            load(0, True)
            load(1, False)
            store_max(0, 0)
            with sp.Fori(0, LASTP) as i:
                for q in range(2):
                    k = i * 2 + q
                    load(k + 2, False)
                    store_max(k + 1, 1 - q)
                    store_rows(k)
            store_max(CHUNKS - 1, 1)
            store_rows(CHUNKS - 2)
            store_rows(CHUNKS - 1)
            sp.wait_ge(s.rows2_stored, 16 * CHUNKS)
            sp.wait_ge(s.mx_stored[0], 16 * (LASTP + 1))
            sp.wait_ge(s.mx_stored[1], 16 * (LASTP + 1))

        @block.gpsimd
        def _(pool):
            def gather(i, q, first):
                if not first:
                    pool.wait_ge(s.q_ready, i * 2 + q - 1)
                nc.gpsimd.tensor_copy(idx[q][:, :], m.src[:, bass.ds((i * 2 + q) * K, K)]).then_inc(s.idx2_ready, 1)
                pool.wait_ge(s.idx2_ready, i * 2 + q + 1)
                pool.sem_inc(s.idx2_seen, 1)
                for t in range(K):
                    nc.gpsimd.indirect_dma_start(g[q][:, t, :], None, d.tab2,
                                                 bass.IndirectOffsetOnAxis(idx[q][:, t:t + 1], 0)).then_inc(s.gather2_in[q], 16)

            gather(0, 0, True)
            gather(0, 1, True)
            with pool.Fori(1, CHUNKS // 2) as i:
                gather(i, 0, False)
                gather(i, 1, False)

        @block.scalar
        def _(act):
            def spread(k, q, first):
                if not first:
                    act.wait_ge(s.w_ready, k - 1)
                nc.scalar.copy(mask[q][:, :, 1:], over_channels(m.same[:, bass.ds(k * K, K)])).then_inc(s.mask2_ready, 1)
                act.wait_ge(s.v_in, 16 * (k + 1))
                if not first:
                    act.wait_ge(s.b_ready, k - 1)
                nc.scalar.copy(vct[q][:, :, 1:], vin[:, :, :].rearrange("p t c -> p c t")).then_inc(s.vct_ready, 1)

            def weights(k, q):
                act.wait_ge(s.arg_ready, k + 1)
                nc.scalar.activation(wt[q][:, :, 1:], wt[q][:, :, 1:], ACT.Relu).then_inc(s.step_ready, 1)
                nc.scalar.activation(pw[q][:, :, 1:], pw[q][:, :, 1:], ACT.Exp).then_inc(s.pw_ready, 1)
                act.wait_ge(s.step_ready, k + 1)
                nc.scalar.activation(wt[q][:, :, 1:], wt[q][:, :, 1:], ACT.Exp, scale=-1.0).then_inc(s.wt_ready, 1)

            def to_rows(k, first):
                act.wait_ge(s.sums_ready, 2 * (k + 1))
                if not first:
                    act.wait_ge(s.rows2_stored, 16 * k)
                nc.scalar.copy(rows[:, :, 0:C], den[:, :, 1:].rearrange("p c t -> p t c")).then_inc(s.den_copied, 1)
                nc.scalar.copy(rows[:, :, C:2 * C], num[:, :, 1:].rearrange("p c t -> p t c")).then_inc(s.num_copied, 1)
                act.wait_ge(s.den_copied, k + 1)
                act.wait_ge(s.num_copied, k + 1)
                act.sem_inc(s.rows2_ready, 1)

            act.wait_ge(s.mask2_zero, 2)
            spread(0, 0, True)
            spread(1, 1, True)
            weights(0, 0)
            spread(2, 0, False)
            weights(1, 1)
            to_rows(0, True)
            with act.Fori(0, LASTP - 1) as i:
                for q in range(2):
                    k = i * 2 + q
                    spread(k + 3, 1 - q, False)
                    weights(k + 2, q)
                    to_rows(k + 1, False)
            spread(CHUNKS - 1, 1, False)
            weights(CHUNKS - 2, 0)
            to_rows(CHUNKS - 3, False)
            weights(CHUNKS - 1, 1)
            to_rows(CHUNKS - 2, False)
            to_rows(CHUNKS - 1, False)

        @block.vector
        def _(dve):
            ch = Chain(dve, s.soft_dve)
            nc.vector.memset(mask[0][:, :, 0:1], 0.0).then_inc(s.mask2_zero, 1)
            nc.vector.memset(mask[1][:, :, 0:1], 0.0).then_inc(s.mask2_zero, 1)
            ch.step(nc.vector.memset(mx[1][:, :, K:K + 1], 0.0))
            ch.step(nc.vector.memset(den[:, :, K:K + 1], 0.0))
            ch.step(nc.vector.memset(num[:, :, K:K + 1], 0.0))
            ch.step(nc.vector.memset(wt[0][:, :, 0:1], 0.0))
            ch.step(nc.vector.memset(wt[1][:, :, 0:1], 0.0))
            ch.step(nc.vector.tensor_copy(bexp[:, :, K], m.b_open[:, :]))
            dve.wait_ge(s.soft_dve, ch.n)

            def scale_step(k, q):
                dve.wait_ge(s.wt_ready, k + 1)
                nc.vector.tensor_tensor(wt[q][:, :, 1:], wt[q][:, :, 1:], mask[q][:, :, 1:], ALU.mult).then_inc(s.w_ready, 1)

            def attention(i, q, first):
                k = i * 2 + q
                dve.wait_ge(s.vct_ready, k + 1)
                dve.wait_ge(s.mask2_ready, k + 1)
                nc.vector.tensor_copy(vct[q][:, :, 0:1], bexp[:, :, K:K + 1]).then_inc(s.b_carry, 1)
                dve.wait_ge(s.b_carry, k + 1)
                nc.vector.tensor_tensor_scan(flat(bexp[:, :, :]), flat(mask[q][:, :, :]), flat(vct[q][:, :, :]), 0.0,
                                             ALU.mult, ALU.add).then_inc(s.b_ready, 1)
                dve.wait_ge(s.gather2_in[q], 16 * K * (i + 1))
                dve.wait_ge(s.b_ready, k + 1)
                nc.vector.tensor_tensor(zb[:, :, 1:], g[q][:, :, 0:C].rearrange("p t c -> p c t"), bexp[:, :, 1:],
                                        ALU.add).then_inc(s.z2_ready, 1)
                nc.vector.tensor_copy(zb[:, :, 0:1], mx[1 - q][:, :, K:K + 1]).then_inc(s.m_carry, 1)
                dve.wait_ge(s.z2_ready, k + 1)
                dve.wait_ge(s.m_carry, k + 1)
                if not first:
                    dve.wait_ge(s.mx_stored[q], 16 * i)
                nc.vector.tensor_tensor_scan(flat(mx[q][:, :, :]), flat(mask[q][:, :, :]), flat(zb[:, :, :]), 0.0,
                                             ALU.mult, ALU.max).then_inc(s.mx_ready, 1)
                dve.wait_ge(s.mx_ready, k + 1)
                nc.vector.scalar_tensor_tensor(pw[q][:, :, 1:], zb[:, :, 1:], 0.0, mx[q][:, :, 1:], ALU.max, ALU.subtract).then_inc(s.att_done, 1)
                dve.wait_ge(s.att_done, k + 1)
                nc.vector.tensor_tensor(wt[q][:, :, 1:], mx[q][:, :, 1:], mx[q][:, :, 0:K], ALU.subtract).then_inc(s.arg_ready, 1)

            def sums(k, q, first):
                dve.wait_ge(s.pw_ready, k + 1)
                nc.vector.tensor_tensor(qs[:, :, 1:], pw[q][:, :, 1:], g[q][:, :, C:2 * C].rearrange("p t c -> p c t"),
                                        ALU.mult).then_inc(s.q_ready, 1)
                nc.vector.tensor_copy(pw[q][:, :, 0:1], den[:, :, K:K + 1]).then_inc(s.d_carry, 1)
                nc.vector.tensor_copy(qs[:, :, 0:1], num[:, :, K:K + 1]).then_inc(s.n_carry, 1)
                dve.wait_ge(s.d_carry, k + 1)
                dve.wait_ge(s.w_ready, k + 1)
                if not first:
                    dve.wait_ge(s.rows2_ready, k)
                nc.vector.tensor_tensor_scan(flat(den[:, :, :]), flat(wt[q][:, :, :]), flat(pw[q][:, :, :]), 0.0,
                                             ALU.mult, ALU.add).then_inc(s.sums_ready, 1)
                dve.wait_ge(s.q_ready, k + 1)
                dve.wait_ge(s.n_carry, k + 1)
                nc.vector.tensor_tensor_scan(flat(num[:, :, :]), flat(wt[q][:, :, :]), flat(qs[:, :, :]), 0.0,
                                             ALU.mult, ALU.add).then_inc(s.sums_ready, 1)
                dve.wait_ge(s.sums_ready, 2 * (k + 1))

            attention(0, 0, True)
            scale_step(0, 0)
            attention(0, 1, True)
            sums(0, 0, True)
            with dve.Fori(1, CHUNKS // 2) as i:
                scale_step(i * 2 - 1, 1)
                attention(i, 0, False)
                sums(i * 2 - 1, 1, False)
                scale_step(i * 2, 0)
                attention(i, 1, False)
                sums(i * 2, 0, False)
            scale_step(CHUNKS - 1, 1)
            sums(CHUNKS - 1, 1, False)
            for r, part in enumerate((mx[1], den, num)):
                ch.step(nc.vector.tensor_copy(m.tail2[:, r, :], part[:, :, K]))
            dve.wait_ge(s.soft_dve, ch.n)

        @block.tensor
        def _(pe):
            pe.wait_ge(s.mask2_zero, 2)


def end_phase(nc, d, s, m):
    with ExitStack() as ctx:
        sb = lambda name, shape, dt=fp32: ctx.enter_context(nc.sbuf_tensor(name, shape, dt))
        pb = lambda name, shape: ctx.enter_context(nc.psum_tensor(name, shape, fp32))
        tail_ps = pb("tail2_ps", [C, 4, P])
        carry_ps = pb("carry2_ps", [P, BANK])[:, 0:3 * C].rearrange("p (r c) -> p r c", c=C)
        tl = sb("tl", [C, 4, P])
        open_t = sb("open2_t", [C, 3, P + 1])
        w_old, w_new = sb("w_old", [C, P]), sb("w_new", [C, P])
        mrow = sb("mrow", [P, U])
        pick = sb("pick", [P, C, K + 1])
        slot = sb("slot_hit", [P, K + 1])
        seg = sb("seg2", [P, 2 * C])
        seg_m, mm = sb("seg_m", [P, C]), sb("mm", [P, C])
        e_row, e_car = sb("e_row", [P, C]), sb("e_car", [P, C])
        carry = sb("carry2", [P, 3, C])
        junk = sb("junk_k", [P, CHUNKS])
        mrow_f, mrow_i, tau = sb("mrow_f", [P, 1]), sb("mrow_i", [P, 1], i32), sb("tau", [P, 1])
        agg = sb("agg2", [P, NB, 2 * C])
        nf = sb("nf", [P, NB, 2 * C])
        res = sb("res", [P, NB, C])
        bo = sb("bo", [P, C])
        wo = sb("wo", [2 * C, C])
        nft = [sb(f"nft{q}", [P, P]) for q in range(2)]
        turn = [pb(f"turn3_{q}", [P, BANK])[:, 0:P] for q in range(2)]
        prod = [pb(f"prod{q}", [P, BANK])[:, 0:C] for q in range(2)]
        block = ctx.enter_context(nc.Block())

        @block.sync
        def _(sp):
            sp.dma_start(nf[:, :, C:2 * C], d.tab2.rearrange("(p b) c -> p b c", b=NB)[:, :, C:2 * C]).then_inc(s.h2_in, 16)
            sp.dma_start(wo[:, :], d.wout_t).then_inc(s.wo_in, 16)
            sp.dma_start(bo[:, :], d.b_out.unsqueeze(0).to_broadcast([P, C])).then_inc(s.bo_in, 16)
            sp.wait_ge(s.res_ready, NB)
            sp.dma_start(d.out.rearrange("(p b) c -> p b c", b=NB), res[:, :, :]).then_inc(s.out_stored, 16)
            sp.wait_ge(s.out_stored, 16)

        @block.gpsimd
        def _(pool):
            nc.gpsimd.indirect_dma_start(seg[:, :], None, d.s2,
                                         bass.IndirectOffsetOnAxis(m.seg_read_i[:, 0:1], 0)).then_inc(s.seg2_in, 16)
            pool.wait_ge(s.mrow_ready, 1)
            nc.gpsimd.indirect_dma_start(mrow[:, :], None, d.m2,
                                         bass.IndirectOffsetOnAxis(mrow_i[:, 0:1], 0)).then_inc(s.mrow_in, 16)
            pool.wait_ge(s.seg2_ready, 1)
            nc.gpsimd.indirect_dma_start(d.s2, bass.IndirectOffsetOnAxis(m.seg_write_i[:, 0:1], 0), seg[:, :], None,
                                         bounds_check=EDGES_PAD - 1, oob_is_err=False).then_inc(s.seg2_stored, 16)
            pool.wait_ge(s.seg2_stored, 16)
            for b in range(NB):
                nc.gpsimd.indirect_dma_start(agg[:, b, :], None, d.s2,
                                             bass.IndirectOffsetOnAxis(m.last_i[:, b:b + 1], 0)).then_inc(s.agg2_in, 16)

        @block.tensor
        def _(pe):
            for r in range(3):
                nc.tensor.transpose(tail_ps[:, r, :], m.tail2[:, r, :], m.ident[:, :])
            nc.tensor.transpose(tail_ps[:, 3, :], m.link[:, 0:1].to_broadcast([P, C]), m.ident[:, :]).then_inc(s.tail2_turned, 1)
            pe.wait_ge(s.open2_ready, 1)
            for r in range(3):
                last = nc.tensor.transpose(carry_ps[:, r, :], open_t[:, r, 0:P], m.ident[0:C, 0:C])
            last.then_inc(s.carry2_turned, 1)
            pe.wait_ge(s.nf_ready, 1)
            pe.wait_ge(s.wo_in, 16)

            def turn_block(b):
                if b >= 2:
                    pe.wait_ge(s.nft_ready, b - 1)
                nc.tensor.transpose(turn[b % 2][:, :], nf[:, b, :], m.ident[:, :]).then_inc(s.turned3, 1)

            turn_block(0)
            for b in range(NB):
                if b + 1 < NB:
                    turn_block(b + 1)
                pe.wait_ge(s.nft_ready, b + 1)
                if b >= 2:
                    pe.wait_ge(s.res_ready, b - 1)
                nc.tensor.matmul(prod[b % 2][:, :], nft[b % 2][:, :], wo[:, :], start=True, stop=True).then_inc(s.prod_ready, 1)

        @block.scalar
        def _(act):
            def exp_of(ap, n):
                act.wait_ge(s.exp_asked, n)
                nc.scalar.activation(ap, ap, ACT.Exp).then_inc(s.exp_answered, 1)

            exp_of(w_old[:, :], 1)
            exp_of(w_new[:, :], 2)
            exp_of(e_row[:, :], 3)
            exp_of(e_car[:, :], 4)
            for b in range(NB):
                act.wait_ge(s.turned3, b + 1)
                if b >= 2:
                    act.wait_ge(s.prod_ready, b - 1)
                nc.scalar.copy(nft[b % 2][:, :], turn[b % 2][:, :]).then_inc(s.nft_ready, 1)

        @block.vector
        def _(dve):
            ch = Chain(dve, s.end_dve)
            ch.then_wait(nc.vector.tensor_scalar(junk[:, :], m.kstart[:, :], m.seg_t[:, 0:1], 0.0, ALU.is_le, ALU.add,
                                                 accum_out=mrow_f[:, :]))
            ch.then_wait(nc.vector.tensor_scalar(mrow_f[:, :], mrow_f[:, :], -1.0, None, ALU.add))
            ch.then_wait(nc.vector.scalar_tensor_tensor(tau[:, :], mrow_f[:, :], float(-K), m.seg_t[:, :], ALU.mult, ALU.add))
            ch.then_wait(nc.vector.scalar_tensor_tensor(mrow_f[:, :], mrow_f[:, :], float(K), m.pstart[:, :], ALU.mult, ALU.add))
            ch.then_wait(nc.vector.tensor_scalar(mrow_f[:, :], mrow_f[:, :], 1.0 / K, 0.25, ALU.mult, ALU.add))
            ch.then_wait(nc.vector.tensor_copy(mrow_i[:, :], mrow_f[:, :]))
            ch.then_wait(nc.vector.tensor_scalar(slot[:, :], m.slot[:, :], tau[:, 0:1], None, ALU.is_equal))
            nc.vector.memset(junk[:, 0:1], 0.0).then_inc(s.mrow_ready, 1)
            dve.wait_ge(s.tail2_turned, 1)
            ch.then_wait(nc.vector.tensor_copy(tl[:, :, :], tail_ps[:, :, :]))
            ch.then_wait(nc.vector.memset(open_t[:, :, :], 0.0))
            ch.then_wait(nc.vector.tensor_tensor_scan(open_t[:, 0, 1:], tl[:, 3, :], tl[:, 0, :], 0.0, ALU.mult, ALU.max))
            ch.then_wait(nc.vector.tensor_tensor(w_old[:, :], open_t[:, 0, 0:P], open_t[:, 0, 1:], ALU.subtract))
            nc.vector.tensor_scalar(w_old[:, :], w_old[:, :], 0.0, None, ALU.min).then_inc(s.exp_asked, 1)
            nc.vector.tensor_tensor(w_new[:, :], tl[:, 0, :], open_t[:, 0, 1:], ALU.subtract).then_inc(s.exp_asked, 1)
            dve.wait_ge(s.exp_answered, 2)
            ch.then_wait(nc.vector.tensor_tensor(w_old[:, :], w_old[:, :], tl[:, 3, :], ALU.mult))
            for r in (1, 2):
                ch.then_wait(nc.vector.tensor_tensor(tl[:, r, :], tl[:, r, :], w_new[:, :], ALU.mult))
                ins = nc.vector.tensor_tensor_scan(open_t[:, r, 1:], w_old[:, :], tl[:, r, :], 0.0, ALU.mult, ALU.add)
                if r == 1:
                    ch.then_wait(ins)
                else:
                    ins.then_inc(s.open2_ready, 1)
            dve.wait_ge(s.mrow_in, 16)
            ch.then_wait(nc.vector.tensor_tensor(pick[:, :, :], mrow[:, :].rearrange("p (c t) -> p c t", c=C),
                                                 over_channels(slot[:, :]), ALU.mult))
            ch.then_wait(nc.vector.tensor_reduce(seg_m[:, :], pick[:, :, :], AX.X, ALU.add))
            dve.wait_ge(s.carry2_turned, 1)
            ch.then_wait(nc.vector.tensor_copy(carry[:, :, :], carry_ps[:, :, :]))
            ch.then_wait(nc.vector.tensor_tensor(mm[:, :], seg_m[:, :], carry[:, 0, :], ALU.max))
            nc.vector.tensor_tensor(e_row[:, :], seg_m[:, :], mm[:, :], ALU.subtract).then_inc(s.exp_asked, 1)
            nc.vector.tensor_tensor(e_car[:, :], carry[:, 0, :], mm[:, :], ALU.subtract).then_inc(s.exp_asked, 1)
            dve.wait_ge(s.seg2_in, 16)
            dve.wait_ge(s.exp_answered, 4)
            for r in range(2):
                part = seg[:, r * C:(r + 1) * C]
                ch.then_wait(nc.vector.tensor_tensor(part, part, e_row[:, :], ALU.mult))
                ch.then_wait(nc.vector.tensor_tensor(carry[:, 1 + r, :], carry[:, 1 + r, :], e_car[:, :], ALU.mult))
                ins = nc.vector.tensor_tensor(part, part, carry[:, 1 + r, :], ALU.add)
                if r == 0:
                    ch.then_wait(ins)
                else:
                    ins.then_inc(s.seg2_ready, 1)
            dve.wait_ge(s.bo_in, 16)
            ch.then_wait(nc.vector.tensor_tensor(m.x[:, :, :], m.x[:, :, :], bo[:, :].unsqueeze(1).to_broadcast([P, NB, C]), ALU.add))
            dve.wait_ge(s.h2_in, 16)
            ch.then_wait(nc.vector.tensor_tensor(nf[:, :, C:2 * C], nf[:, :, C:2 * C], over_last(m.has[:, :]), ALU.mult))
            dve.wait_ge(s.agg2_in, 16 * NB)
            ch.then_wait(nc.vector.reciprocal(agg[:, :, 0:C], agg[:, :, 0:C]))
            ch.then_wait(nc.vector.tensor_tensor(agg[:, :, C:2 * C], agg[:, :, C:2 * C], agg[:, :, 0:C], ALU.mult))
            nc.vector.tensor_tensor(nf[:, :, 0:C], agg[:, :, C:2 * C], over_last(m.has[:, :]), ALU.mult).then_inc(s.nf_ready, 1)
            for b in range(NB):
                dve.wait_ge(s.prod_ready, b + 1)
                nc.vector.tensor_tensor(res[:, b, :], prod[b % 2][:, :], m.x[:, b, :], ALU.add).then_inc(s.res_ready, 1)


class Semaphores:

    def __init__(self, sem):
        self.first_in = sem("first_in")
        self.x_in = sem("x_in")
        self.dst_in = sem("dst_in")
        self.src_in = sem("src_in")
        self.h1_ready = sem("h1_ready")
        self.h1_stored = sem("h1_stored")
        self.node_iota = sem("node_iota")
        self.row_ready = sem("row_ready")
        self.search_in = sem("search_in")
        self.w_in = sem("w_in")
        self.w3_in = sem("w3_in")
        self.var1_ready = sem("var1_ready")
        self.std1_ready = sem("std1_ready")
        self.setup_dve = sem("setup_dve")
        self.cnt_ready = sem("cnt_ready")
        self.cnt_stored = sem("cnt_stored")
        self.start_in = sem("start_in")
        self.z_ready = sem("z_ready")
        self.hw_ready = sem("hw_ready")
        self.v_zeroed = sem("v_zeroed")
        self.rows1_ready = sem("rows1_ready")
        self.msg_ready = sem("msg_ready")
        self.idx1_ready = sem("idx1_ready")
        self.d0_ready = sem("d0_ready")
        self.d0_cnt_in = sem("d0_cnt_in")
        self.seg_idx_ready = sem("seg_idx_ready")
        self.seg1_in = sem("seg1_in")
        self.seg1_ready = sem("seg1_ready")
        self.seg1_stored = sem("seg1_stored")
        self.sp_ready = sem("sp_ready")
        self.tail1_ready = sem("tail1_ready")
        self.tail1_turned = sem("tail1_turned")
        self.open1_ready = sem("open1_ready")
        self.carry1_ready = sem("carry1_ready")
        self.z_clamped = sem("z_clamped")
        self.exp_ready = sem("exp_ready")
        self.log_ready = sem("log_ready")
        self.scan1_ready = sem("scan1_ready")
        self.mask1_ready = sem("mask1_ready")
        self.mask1_zero = sem("mask1_zero")
        self.sum_dve = sem("sum_dve")
        self.msg_scaled = sem("msg_scaled")
        self.carry1_in = sem("carry1_in")
        self.agg_in = sem("agg_in")
        self.bd_ready = sem("bd_ready")
        self.v_stored = sem("v_stored")
        self.bd_stored = sem("bd_stored")
        self.b_open_in = sem("b_open_in")
        self.d0n_ready = sem("d0n_ready")
        self.wab_in = sem("wab_in")
        self.wab_zero = sem("wab_zero")
        self.tab_ready = sem("tab_ready")
        self.tab_stored = sem("tab_stored")
        self.var2_ready = sem("var2_ready")
        self.std2_ready = sem("std2_ready")
        self.h2_ready = sem("h2_ready")
        self.tab_h2 = sem("tab_h2")
        self.turned2 = sem("turned2")
        self.ab_ready = sem("ab_ready")
        self.h2t_ones = sem("h2t_ones")
        self.h2t_ready = sem("h2t_ready")
        self.ab_out = sem("ab_out")
        self.node_dve = sem("node_dve")
        self.vct_ready = sem("vct_ready")
        self.v_in = sem("v_in")
        self.mx_ready = sem("mx_ready")
        self.rows2_ready = sem("rows2_ready")
        self.rows2_stored = sem("rows2_stored")
        self.q_ready = sem("q_ready")
        self.idx2_ready = sem("idx2_ready")
        self.w_ready = sem("w_ready")
        self.mask2_ready = sem("mask2_ready")
        self.b_ready = sem("b_ready")
        self.arg_ready = sem("arg_ready")
        self.step_ready = sem("step_ready")
        self.pw_ready = sem("pw_ready")
        self.wt_ready = sem("wt_ready")
        self.sums_ready = sem("sums_ready")
        self.den_copied = sem("den_copied")
        self.num_copied = sem("num_copied")
        self.mask2_zero = sem("mask2_zero")
        self.soft_dve = sem("soft_dve")
        self.b_carry = sem("b_carry")
        self.z2_ready = sem("z2_ready")
        self.m_carry = sem("m_carry")
        self.att_done = sem("att_done")
        self.d_carry = sem("d_carry")
        self.n_carry = sem("n_carry")
        self.h2_in = sem("h2_in")
        self.wo_in = sem("wo_in")
        self.bo_in = sem("bo_in")
        self.res_ready = sem("res_ready")
        self.out_stored = sem("out_stored")
        self.seg2_in = sem("seg2_in")
        self.mrow_ready = sem("mrow_ready")
        self.mrow_in = sem("mrow_in")
        self.seg2_ready = sem("seg2_ready")
        self.seg2_stored = sem("seg2_stored")
        self.agg2_in = sem("agg2_in")
        self.tail2_turned = sem("tail2_turned")
        self.open2_ready = sem("open2_ready")
        self.carry2_turned = sem("carry2_turned")
        self.nf_ready = sem("nf_ready")
        self.nft_ready = sem("nft_ready")
        self.turned3 = sem("turned3")
        self.prod_ready = sem("prod_ready")
        self.exp_asked = sem("exp_asked")
        self.exp_answered = sem("exp_answered")
        self.end_dve = sem("end_dve")
        self.w23_zero = sem("w23_zero")
        self.idx1_seen = sem("idx1_seen")
        self.idx2_seen = sem("idx2_seen")
        self.edge_in = [sem(f"edge_in{q}") for q in range(2)]
        self.rows1_stored = [sem(f"rows1_stored{q}") for q in range(2)]
        self.gather1_in = [sem(f"gather1_in{q}") for q in range(2)]
        self.mx_stored = [sem(f"mx_stored{q}") for q in range(2)]
        self.gather2_in = [sem(f"gather2_in{q}") for q in range(2)]


class Dram:

    def __init__(self, nc, x, src, dst_ext, dst_rows, dst_first, rbf_t, ef_t, W1, b1, W2, b2, W3, b3, wlin_t, b_lin, wout_t, b_out, out):
        self.x = x
        self.src = src
        self.dst_ext = dst_ext
        self.dst_rows = dst_rows
        self.dst_first = dst_first
        self.rbf_t = rbf_t
        self.ef_t = ef_t
        self.W1 = W1
        self.b1 = b1
        self.W2 = W2
        self.b2 = b2
        self.W3 = W3
        self.b3 = b3
        self.wlin_t = wlin_t
        self.b_lin = b_lin
        self.wout_t = wout_t
        self.b_out = b_out
        self.out = out
        self.h1_tab = nc.dram_tensor("h1_tab", [NODES_PAD, C], fp32).ap()
        self.cnt_tab = nc.dram_tensor("cnt_tab", [NODES_PAD + 1, 1], fp32).ap()
        self.s1 = nc.dram_tensor("s1", [EDGES_PAD, C], fp32).ap()
        self.v = nc.dram_tensor("v", [EDGES_PAD, C], fp32).ap()
        self.tab2 = nc.dram_tensor("tab2", [NODES_PAD, 2 * C], fp32).ap()
        self.b_tab = nc.dram_tensor("b_tab", [NODES_PAD, C], fp32).ap()
        self.s2 = nc.dram_tensor("s2", [EDGES_PAD, 2 * C], fp32).ap()
        self.m2 = nc.dram_tensor("m2", [P * CHUNKS, U], fp32).ap()


class Resident:

    def __init__(self, sb):
        self.x = sb("x_sb", [P, NB, C])
        self.src = sb("src_sb", [P, T], i32)
        self.same = sb("same", [P, T])
        self.ident = sb("ident", [P, P])
        self.ident_i = sb("ident_i", [P, P], i32)
        self.node = sb("node", [P, NB])
        self.row = sb("row", [P, NB])
        self.row_i = sb("row_i", [P, NB], i32)
        self.cnt = sb("cnt", [P, NB])
        self.start = sb("start", [P, NB])
        self.has = sb("has", [P, NB])
        self.tmp = sb("tmp", [P, NB])
        self.last_i = sb("last_i", [P, NB], i32)
        self.start_i = sb("start_i", [P, NB], i32)
        self.d0 = sb("d0", [P, 1])
        self.d0_t = sb("d0_t", [P, 1])
        self.d0_i = sb("d0_i", [P, 1], i32)
        self.d0_cnt = sb("d0_cnt", [P, 1])
        self.link = sb("link", [P, 1])
        self.pstart = sb("pstart", [P, 1])
        self.pstart_i = sb("pstart_i", [P, 1], i32)
        self.kstart = sb("kstart", [P, CHUNKS])
        self.kstart_i = sb("kstart_i", [P, CHUNKS], i32)
        self.slot = sb("slot", [P, K + 1])
        self.slot_i = sb("slot_i", [P, K + 1], i32)
        self.seg_t = sb("seg_t", [P, 1])
        self.seg_ok = sb("seg_ok", [P, 1])
        self.seg_read_i = sb("seg_read_i", [P, 1], i32)
        self.seg_write_i = sb("seg_write_i", [P, 1], i32)
        self.b_open = sb("b_open", [P, C])
        self.tail2 = sb("tail2", [P, 3, C])
        self.w1h = sb("w1h", [RBF, C])
        self.b1h = sb("b1h", [C, 1])
        self.w23 = sb("w23", [P, 2 * C])
        self.bias_ones = sb("bias_ones", [3, P], bf16)
        self.bias_rows = sb("bias_rows", [3, GROUP * 2 * C], bf16)


def gnn_kernel(nc, x, src, dst_ext, dst_rows, dst_first, rbf_t, ef_t, W1, b1, W2, b2, W3, b3, wlin_t, b_lin, wout_t,
               b_out, out):
    d = Dram(nc, x, src, dst_ext, dst_rows, dst_first, rbf_t, ef_t, W1, b1, W2, b2, W3, b3, wlin_t, b_lin, wout_t, b_out, out)
    with ExitStack() as ctx:
        sb = lambda name, shape, dt=fp32: ctx.enter_context(nc.sbuf_tensor(name, shape, dt))
        s = Semaphores(lambda name: ctx.enter_context(nc.semaphore(name)))
        m = Resident(sb)
        with ExitStack() as early:
            m.search = early.enter_context(nc.sbuf_tensor("search", [P, NB, ROW], i32))
            with nc.Block() as block:
                @block.vector
                def _(dve):
                    nc.vector.memset(m.w23[:, :], 0.0).then_inc(s.w23_zero, 1)

                @block.sync
                def _(sp):
                    sp.wait_ge(s.w23_zero, 1)
                    sp.dma_start(m.w23[C:2 * C, C:2 * C], W3).then_inc(s.w3_in, 16)
            setup_phase(nc, d, s, m)
            sum_phase(nc, d, s, m)
        node_phase(nc, d, s, m)
        softmax_phase(nc, d, s, m)
        end_phase(nc, d, s, m)


def kernel(x, src, dst, edge_attr_128, edge_attr_64, L0_gnn_W1, L0_gnn_b1, L0_gnn_W2, L0_gnn_b2, L0_gnn_W3,
           L0_gnn_b3, L1_gnn_W_lin, L1_gnn_b_lin, L1_gnn_W_out, L1_gnn_b_out):
    import numpy as np
    import concourse.bacc as bacc
    from concourse.bass_utils import run_bass_kernel_spmd

    def padded(a, rows, fill=0):
        a = np.asarray(a)
        return np.concatenate([a, np.full((rows - a.shape[0],) + a.shape[1:], fill, a.dtype)])

    def by_column(a):
        return np.ascontiguousarray(padded(a, EDGES_PAD).reshape(P, T, -1).transpose(2, 1, 0)).reshape(-1, T * P)

    dst_pad = padded(dst, EDGES_PAD, NODES)
    before = np.concatenate([np.full((1,), -1, dst_pad.dtype), dst_pad[:-1]])
    arrays = {
        "in_x": padded(x, NODES_PAD),
        "in_src": padded(src, EDGES_PAD),
        "in_dst_ext": np.concatenate([before.reshape(P, T)[:, :1], dst_pad.reshape(P, T)], axis=1),
        "in_dst_rows": dst_pad.reshape(ROWS, ROW),
        "in_dst_first": np.ascontiguousarray(dst_pad.reshape(ROWS, ROW)[:, 0]),
        "in_rbf_t": by_column(edge_attr_128),
        "in_ef_t": by_column(edge_attr_64),
        "in_W1": np.asarray(L0_gnn_W1), "in_b1": np.asarray(L0_gnn_b1),
        "in_W2": np.asarray(L0_gnn_W2), "in_b2": np.asarray(L0_gnn_b2),
        "in_W3": np.asarray(L0_gnn_W3), "in_b3": np.asarray(L0_gnn_b3),
        "in_wlin_t": np.ascontiguousarray(np.asarray(L1_gnn_W_lin).T), "in_b_lin": np.asarray(L1_gnn_b_lin),
        "in_wout_t": np.ascontiguousarray(np.asarray(L1_gnn_W_out).T), "in_b_out": np.asarray(L1_gnn_b_out),
    }
    nc = bacc.Bacc("TRN2", target_bir_lowering=False, num_devices=1)
    args = [nc.dram_tensor(n, a.shape, mybir.dt.from_np(a.dtype), kind="ExternalInput").ap() for n, a in arrays.items()]
    args.append(nc.dram_tensor("out_x", (NODES_PAD, C), fp32, kind="ExternalOutput").ap())
    gnn_kernel(nc, *args)
    r = run_bass_kernel_spmd(nc, [arrays], core_ids=[0])
    return r.results[0]["out_x"][:NODES]
```

```python
import concourse.bass as bass
from concourse import mybir
from contextlib import ExitStack

P = 128
NODES, EDGES = 6250, 206250
C = 64
RBF = 128
K = 26
CHUNKS = 62
T = K * CHUNKS
EDGES_PAD = P * T
NB = 49
NODES_PAD = P * NB
GROUP = 4
GROUPS = -(-K // GROUP)
PAIR_G = 2 * GROUPS
ROW = 496
ROWS = EDGES_PAD // ROW
RC = 4
RP = ROWS // RC
WB = 7
TURNS = NB // WB
U = C * (K + 1)
SECTIONS = [(0, 12), (12, 24), (24, 36), (36, NB)]
QUADS = [(b, min(b + 4, NB)) for b in range(0, NB, 4)]
SKIP = EDGES_PAD + 1
EPS = 1e-5
BANK = 512
assert EDGES <= EDGES_PAD and NODES < NODES_PAD and RP * RC * ROW == EDGES_PAD
assert CHUNKS % 2 == 0 and ROW < BANK and TURNS * WB == NB and 2 * WB <= PAIR_G and TURNS < CHUNKS // 2

fp32 = mybir.dt.float32
bf16 = mybir.dt.bfloat16
i32 = mybir.dt.int32
ALU = mybir.AluOpType
ACT = mybir.ActivationFunctionType
AX = mybir.AxisListType


def section_of(b):
    return [b0 <= b < b1 for b0, b1 in SECTIONS].index(True)


class Chain:

    def __init__(self, eng, sem):
        self.eng, self.sem, self.n = eng, sem, 0

    def step(self, ins):
        self.n += 1
        ins.then_inc(self.sem, 1)
        return self.n

    def then_wait(self, ins):
        self.eng.wait_ge(self.sem, self.step(ins))


def size(j):
    return min(GROUP, K - j % GROUPS * GROUP)


def over_channels(ap, n=C):
    return ap.unsqueeze(1).to_broadcast([ap.shape[0], n, ap.shape[1]])


def over_last(ap, n=C):
    return ap.unsqueeze(2).to_broadcast([ap.shape[0], ap.shape[1], n])


def flat(ap):
    return ap.rearrange("p c t -> p (c t)")


def layer_norm_relu(nc, chain, act_asks, act_answers, asked, x, out, xc, mean, var):
    sq = out
    chain.then_wait(nc.vector.tensor_reduce(mean, x, AX.X, ALU.add))
    chain.then_wait(nc.vector.tensor_scalar(mean, mean, 1.0 / C, None, ALU.mult))
    chain.then_wait(nc.vector.tensor_tensor(xc, x, over_last(mean), ALU.subtract))
    chain.then_wait(nc.vector.tensor_tensor(sq, xc, xc, ALU.mult))
    chain.then_wait(nc.vector.tensor_reduce(var, sq, AX.X, ALU.add))
    nc.vector.tensor_scalar(var, var, 1.0 / C, EPS, ALU.mult, ALU.add).then_inc(act_asks, 1)
    chain.eng.wait_ge(act_answers, asked)
    chain.then_wait(nc.vector.reciprocal(var, var))
    return nc.vector.scalar_tensor_tensor(out, xc, 0.0, over_last(var), ALU.max, ALU.mult)


def setup_phase(nc, d, s, m):
    with ExitStack() as ctx:
        sb = lambda name, shape, dt=fp32: ctx.enter_context(nc.sbuf_tensor(name, shape, dt))
        h1 = sb("h1", [P, NB, C])
        xc = sb("xc1", [P, NB, C])
        stat = sb("stat1", [P, 2 * NB])
        block = ctx.enter_context(nc.Block())

        @block.sync
        def _(sp):
            sp.dma_start(m.x[:, :, :], d.x.rearrange("(p b) c -> p b c", b=NB)).then_inc(s.x_in, 16)
            sp.dma_start(m.early.dst_i[:, :], d.dst_ext).then_inc(s.dst_in, 16)
            table = d.dst_rows.rearrange("(p c) w -> p c w", c=RC)
            sp.dma_start(m.early.table_i[:, 1:, :], table).then_inc(s.table_in, 16)
            sp.dma_start(m.early.table_i[1:RP, 0, :], table[0:RP - 1, RC - 1, :]).then_inc(s.table_in, 16)
            sp.wait_ge(s.w23_zero, 1)
            sp.dma_start(m.w23[C:2 * C, C:2 * C], d.W3).then_inc(s.w3_in, 16)
            sp.wait_ge(s.h1_ready, 1)
            sp.dma_start(d.h1_tab.rearrange("(p b) c -> p b c", b=NB), h1[:, :, :]).then_inc(s.h1_stored, 16)
            sp.wait_ge(s.h1_stored, 16)

        @block.gpsimd
        def _(pool):
            nc.gpsimd.iota(m.node_i[:, :], [[1, NB]], base=0, channel_multiplier=NB).then_inc(s.iota_ready, 1)
            nc.gpsimd.iota(m.ident_i[:, :], [[1, P]], base=0, channel_multiplier=-1).then_inc(s.iota_ready, 1)
            nc.gpsimd.iota(m.pstart_i[:, :], [[0, 1]], base=0, channel_multiplier=T).then_inc(s.iota_ready, 1)
            nc.gpsimd.iota(m.kstart_i[:, :], [[K, CHUNKS]], base=0, channel_multiplier=0).then_inc(s.iota_ready, 1)
            nc.gpsimd.iota(m.slot_i[:, :], [[1, K + 1]], base=-1, channel_multiplier=0).then_inc(s.iota_ready, 1)
            nc.gpsimd.iota(m.early.turn_i[:, :, :], [[1, WB], [NB, P]], base=0, channel_multiplier=0).then_inc(s.iota_ready, 1)
            nc.gpsimd.iota(m.early.table_row_i[:, :], [[1, RC]], base=0, channel_multiplier=RC).then_inc(s.iota_ready, 1)

        @block.scalar
        def _(act):
            act.dma_start(m.w1_raw[:, :], d.W1).then_inc(s.w_in, 16)
            act.dma_start(m.w2_raw[:, :], d.W2).then_inc(s.w_in, 16)
            act.dma_start(m.b1_raw[:, :], d.b1.rearrange("(c o) -> c o", o=1)).then_inc(s.w_in, 16)
            act.dma_start(m.b23_f[:, 0:C], d.b2.unsqueeze(0).to_broadcast([3, C])).then_inc(s.w_in, 16)
            act.dma_start(m.b23_f[:, C:2 * C], d.b3.unsqueeze(0).to_broadcast([3, C])).then_inc(s.w_in, 16)
            act.wait_ge(s.var1_ready, 1)
            nc.scalar.activation(stat[:, NB:2 * NB], stat[:, NB:2 * NB], ACT.Sqrt).then_inc(s.std1_ready, 1)

        @block.vector
        def _(dve):
            ch = Chain(dve, s.setup_dve)
            nc.vector.memset(m.w23[:, :], 0.0).then_inc(s.w23_zero, 1)
            ch.step(nc.vector.memset(m.early.table_i[0:1, 0, :], 0))
            dve.wait_ge(s.x_in, 16)
            layer_norm_relu(nc, ch, s.var1_ready, s.std1_ready, 1, m.x[:, :, :], h1[:, :, :], xc[:, :, :],
                            stat[:, 0:NB], stat[:, NB:2 * NB]).then_inc(s.h1_ready, 1)


def prepare(nc, dve, s, m):
    ch = Chain(dve, s.prepare_dve)
    dve.wait_ge(s.iota_ready, 7)
    ch.step(nc.vector.tensor_copy(m.node[:, :], m.node_i[:, :]))
    ch.step(nc.vector.tensor_scalar(m.ident[:, :], m.ident_i[:, :], 0.0, None, ALU.is_equal))
    ch.step(nc.vector.tensor_copy(m.pstart[:, :], m.pstart_i[:, :]))
    ch.step(nc.vector.tensor_copy(m.kstart[:, :], m.kstart_i[:, :]))
    ch.step(nc.vector.tensor_copy(m.slot[:, :], m.slot_i[:, :]))
    ch.step(nc.vector.memset(m.bias_ones[:, :], 1.0))
    dve.wait_ge(s.dst_in, 16)
    ch.then_wait(nc.vector.tensor_copy(m.early.dst_f[:, :], m.early.dst_i[:, :]))
    ch.then_wait(nc.vector.tensor_tensor(m.same[:, :], m.early.dst_f[:, 1:T + 1], m.early.dst_f[:, 0:T], ALU.is_equal))
    ch.step(nc.vector.tensor_copy(m.d0[:, :], m.early.dst_f[:, 1:2]))
    ch.then_wait(nc.vector.tensor_tensor(m.link[:, :], m.early.dst_f[:, 1:2], m.early.dst_f[:, T:T + 1], ALU.is_equal))
    ch.then_wait(nc.vector.tensor_tensor(m.link[:, :], m.link[:, :], m.same[:, 0:1], ALU.mult))
    dve.wait_ge(s.w_in, 80)
    ch.step(nc.vector.tensor_scalar(m.w1h[:, :], m.w1_raw[:, :], 0.5, None, ALU.mult))
    ch.step(nc.vector.tensor_scalar(m.b1h[:, :], m.b1_raw[:, :], 0.5, None, ALU.mult))
    dve.wait_ge(s.w3_in, 16)
    ch.step(nc.vector.tensor_scalar(m.w23[0:C, 0:C], m.w2_raw[:, :], 2.0, None, ALU.mult))
    ch.then_wait(nc.vector.tensor_copy(m.b23_hi[:, :], m.b23_f[:, :]))
    ch.then_wait(nc.vector.tensor_tensor(m.b23_r[:, :], m.b23_f[:, :], m.b23_hi[:, :], ALU.subtract))
    ch.then_wait(nc.vector.tensor_copy(m.b23_mid[:, :], m.b23_r[:, :]))
    ch.then_wait(nc.vector.tensor_tensor(m.b23_r[:, :], m.b23_r[:, :], m.b23_mid[:, :], ALU.subtract))
    ch.then_wait(nc.vector.tensor_copy(m.b23_lo[:, :], m.b23_r[:, :]))
    ch.then_wait(nc.vector.tensor_scalar(m.b23_s[:, :], m.b23_hi[:, :], m.ident[0:3, 0:1], None, ALU.mult))
    for part, r in ((m.b23_mid, 1), (m.b23_lo, 2)):
        ch.then_wait(nc.vector.scalar_tensor_tensor(m.b23_s[:, :], part[:, :], m.ident[0:3, r:r + 1], m.b23_s[:, :],
                                                    ALU.mult, ALU.add))
    for j in range(GROUP):
        ch.step(nc.vector.tensor_copy(m.bias_rows[:, j * 2 * C:(j + 1) * 2 * C], m.b23_s[:, :]))
    dve.wait_ge(s.prepare_dve, ch.n)
    nc.vector.tensor_copy(m.d0_i[:, :], m.d0[:, :]).then_inc(s.prepared, 1)
    dve.wait_ge(s.table_in, 32)
    row_c = m.early.table[:, :, ROW:ROW + 1].rearrange("p c o -> p (c o)")
    ch.step(nc.vector.tensor_tensor(m.early.table[:, :, 0:ROW], m.early.table_i[:, 1:, :], m.early.table_i[:, 0:RC, :], ALU.subtract))
    ch.step(nc.vector.tensor_copy(m.early.table_first[:, :], m.early.table_i[:, 1:, 0]))
    ch.step(nc.vector.tensor_copy(m.early.turn_node[:, :, :], m.early.turn_i[:, :, :]))
    ch.step(nc.vector.tensor_copy(m.early.search_node[:, :], m.node[:, 0:WB]))
    ch.then_wait(nc.vector.tensor_scalar(row_c, m.early.table_row_i[:, :], 0.0, None, ALU.is_gt))
    ch.then_wait(nc.vector.tensor_tensor(m.early.table_first[:, :], m.early.table_first[:, :], row_c, ALU.mult))
    ch.then_wait(nc.vector.tensor_copy(m.early.table_hi[:, :, :], m.early.table[:, :, :]))
    ch.then_wait(nc.vector.tensor_tensor(m.early.table[:, :, :], m.early.table[:, :, :], m.early.table_hi[:, :, :], ALU.subtract))
    nc.vector.tensor_copy(m.early.table_lo[:, :, :], m.early.table[:, :, :]).then_inc(s.table_ready, 1)


def sum_phase(nc, d, s, m):
    with ExitStack() as ctx:
        sb = lambda name, shape, dt=fp32: ctx.enter_context(nc.sbuf_tensor(name, shape, dt))
        pb = lambda name, shape: ctx.enter_context(nc.psum_tensor(name, shape, fp32))
        GC = GROUP * P
        KP = K * P
        rbf = [sb(f"rbf{q}", [P, KP]) for q in range(2)]
        spef = [sb(f"spef{q}", [P, KP]) for q in range(2)]
        rows = sb("rows1", [P, K, C])
        g = [sb(f"h_src{q}", [P, K, C]) for q in range(2)]
        idx = [sb(f"idx1_{q}", [P, K], i32) for q in range(2)]
        mask = [sb(f"mask1_{q}", [P, C, K + 1]) for q in range(2)]
        msg = sb("msg", [P, C, K + 1])
        run = sb("run", [P, C, K + 1])
        zeros = sb("zeros", [P, K // 2 * C])
        zc = [sb(f"zc{q}", [C, GC]) for q in range(2)]
        lg = [sb(f"lg{q}", [C, GC]) for q in range(2)]
        below = sb("below", [RP, RC, WB * P], bf16)
        found_row, found_cnt = sb("found_row", [P, WB]), sb("found_cnt", [P, WB])
        hit = sb("hit", [P, ROW])
        found = [pb(f"found{q}", [P, BANK]) for q in range(2)]
        z = [pb(f"z{q}", [C, GC]) for q in range(2)]
        hw = [pb(f"hw{q}", [P, GROUP, 2 * C]) for q in range(2)]
        tail_ps = pb("tail_ps", [C, BANK])
        link_ps = tail_ps[:, P:2 * P]
        tail_ps = tail_ps[:, 0:P]
        carry_ps = pb("carry_ps", [P, BANK])[:, 0:C]
        tail_t = sb("tail_t", [C, P])
        link_t = sb("link_t", [C, P])
        open_t = sb("open_t", [C, P + 1])
        tail = sb("tail1", [P, C])
        seg_row = sb("seg_row", [P, C])
        block = ctx.enter_context(nc.Block())
        s1_rows = d.s1.rearrange("(p t) c -> p t c", t=T)
        v_halves = d.v.rearrange("(p j t) c -> p j (t c)", j=2 * CHUNKS, t=K // 2)

        @block.sync
        def _(sp):
            def load_edges(i, q, first):
                if not first:
                    sp.wait_ge(s.z_ready, i * PAIR_G + (q - 1) * GROUPS)
                    sp.wait_ge(s.hw_ready, i * PAIR_G + (q - 1) * GROUPS)
                k = i * 2 + q
                sp.dma_start(rbf[q][:, :], d.rbf_t[:, bass.ds(k * KP, KP)]).then_inc(s.edge_in[q], 16)
                sp.dma_start(spef[q][C:2 * C, :], d.ef_t[:, bass.ds(k * KP, KP)]).then_inc(s.edge_in[q], 16)
                sp.dma_start(v_halves[:, bass.ds(k * 2, 2), :],
                             zeros[:, :].unsqueeze(1).to_broadcast([P, 2, K // 2 * C])).then_inc(s.v_zeroed, 16)

            def load_sources(i, q, first):
                if not first:
                    sp.wait_ge(s.gather1_in[q], 16 * K * i)
                sp.dma_start(idx[q][:, :], d.src_rows[:, bass.ds((i * 2 + q) * K, K)]).then_inc(s.idx1_in[q], 16)

            def store(k):
                sp.wait_ge(s.rows1_ready, k + 1)
                sp.dma_start(s1_rows[:, bass.ds(k * K, K), :], rows[:, :, :]).then_inc(s.rows1_stored, 16)

            load_sources(0, 0, True)
            load_sources(0, 1, True)
            sp.wait_ge(s.zeros_ready, 1)
            load_edges(0, 0, True)
            load_edges(0, 1, True)
            load_sources(1, 0, False)
            with sp.Fori(1, CHUNKS // 2 - 1) as i:
                load_edges(i, 0, False)
                store(i * 2 - 2)
                load_sources(i, 1, False)
                load_edges(i, 1, False)
                store(i * 2 - 1)
                load_sources(i + 1, 0, False)
            i = CHUNKS // 2 - 1
            load_edges(i, 0, False)
            store(i * 2 - 2)
            load_sources(i, 1, False)
            load_edges(i, 1, False)
            store(i * 2 - 1)
            store(i * 2)
            store(i * 2 + 1)
            sp.wait_ge(s.rows1_stored, 16 * CHUNKS)
            sp.wait_ge(s.v_zeroed, 16 * CHUNKS)

        @block.gpsimd
        def _(pool):
            def gather(i, q, first):
                if not first:
                    pool.wait_ge(s.msg_ready, i * PAIR_G + (q - 1) * GROUPS)
                pool.wait_ge(s.idx1_in[q], 16 * (i + 1))
                pool.sem_inc(s.idx1_seen, 1)
                for t in range(K):
                    nc.gpsimd.indirect_dma_start(g[q][:, t, :], None, d.h1_tab,
                                                 bass.IndirectOffsetOnAxis(idx[q][:, t:t + 1], 0)).then_inc(s.gather1_in[q], 16)

            gather(0, 0, True)
            gather(0, 1, True)
            with pool.Fori(1, CHUNKS // 2) as i:
                gather(i, 0, False)
                gather(i, 1, False)
            pool.wait_ge(s.cnt_stored, 48)
            nc.gpsimd.indirect_dma_start(m.d0_cnt[:, :], None, d.cnt_tab1,
                                         bass.IndirectOffsetOnAxis(m.d0_i[:, 0:1], 0)).then_inc(s.d0_cnt_in, 16)
            pool.wait_ge(s.seg_idx_ready, 1)
            pool.wait_ge(s.rows1_stored, 16 * CHUNKS)
            nc.gpsimd.indirect_dma_start(seg_row[:, :], None, d.s1,
                                         bass.IndirectOffsetOnAxis(m.seg_read_i[:, 0:1], 0)).then_inc(s.seg1_in, 16)
            pool.wait_ge(s.seg1_ready, 1)
            nc.gpsimd.indirect_dma_start(d.s1, bass.IndirectOffsetOnAxis(m.seg_write_i[:, 0:1], 0), seg_row[:, :], None,
                                         bounds_check=EDGES_PAD - 1, oob_is_err=False).then_inc(s.seg1_stored, 16)
            pool.wait_ge(s.seg1_stored, 16)

        @block.tensor
        def _(pe):
            def hidden(i, j, first):
                q, gi = j // GROUPS % 2, i * PAIR_G + j
                if j % GROUPS == 0:
                    pe.wait_ge(s.edge_in[q], 32 * (i + 1))
                if not (first and j < 2):
                    pe.wait_ge(s.sp_ready, gi - 1)
                col, n = (j % GROUPS) * GC, size(j) * P
                nc.tensor.matmul(z[j % 2][:, 0:n], m.w1h[:, :], rbf[q][:, col:col + n], start=True, stop=True).then_inc(s.z_ready, 1)

            def messages(i, j, first):
                q, gi = j // GROUPS % 2, i * PAIR_G + j
                pe.wait_ge(s.sp_ready, gi + 1)
                if not (first and j < 2):
                    pe.wait_ge(s.msg_ready, gi - 1)
                out = hw[j % 2]
                n = size(j)
                for t in range(n):
                    col = (j % GROUPS) * GC + t * P
                    nc.tensor.matmul(out[:, t, :], spef[q][:, col:col + P], m.w23[:, :], start=(t == 0), stop=False,
                                     skip_group_check=True)
                nc.tensor.matmul(out[:, 0:n, :].rearrange("p t c -> p (t c)"), m.bias_ones[:, :], m.bias_rows[:, 0:n * 2 * C],
                                 start=False, stop=True, skip_group_check=True).then_inc(s.hw_ready, 1)

            def search(w, b, first):
                if b == 0:
                    pe.wait_ge(s.below_ready, RC * (w + 1))
                if not (first and b < 2):
                    pe.wait_ge(s.found_used, w * WB + b - 1)
                for c in range(RC):
                    for part in (m.early.table_hi, m.early.table_lo):
                        last = nc.tensor.matmul(found[b % 2][:, 0:ROW + 1], below[:, c, b * P:(b + 1) * P], part[:, c, :],
                                                start=(c == 0 and part is m.early.table_hi), stop=(c == RC - 1 and part is m.early.table_lo))
                last.then_inc(s.found_ready[b % 2], 1)

            def pair(i, first, searching):
                for j in range(PAIR_G):
                    if searching and j % 2 and j // 2 < WB:
                        search(i, j // 2, first)
                    hidden(i, j, first)
                    if j >= 2:
                        messages(i, j - 2, first)
                    elif not first:
                        messages(i - 1, j - 2 + PAIR_G, False)

            pe.wait_ge(s.prepared, 1)
            pe.wait_ge(s.table_ready, 1)
            pair(0, True, True)
            with pe.Fori(1, TURNS) as i:
                pair(i, False, True)
            with pe.Fori(TURNS, CHUNKS // 2) as i:
                pair(i, False, False)
            messages(CHUNKS // 2 - 1, PAIR_G - 2, False)
            messages(CHUNKS // 2 - 1, PAIR_G - 1, False)
            pe.wait_ge(s.tail1_ready, 1)
            nc.tensor.transpose(tail_ps, tail[:, :], m.ident[:, :])
            nc.tensor.transpose(link_ps, m.link[:, 0:1].to_broadcast([P, C]), m.ident[:, :]).then_inc(s.tail1_turned, 1)
            pe.wait_ge(s.open1_ready, 1)
            nc.tensor.transpose(carry_ps[:, :], open_t[:, 0:P], m.ident[0:C, 0:C]).then_inc(s.carry1_ready, 1)

        @block.scalar
        def _(act):
            def softplus(i, j):
                gi = i * PAIR_G + j
                act.wait_ge(s.z_clamped, gi + 1)
                n = size(j) * P
                nc.scalar.activation(lg[j % 2][:, 0:n], zc[j % 2][:, 0:n], ACT.Exp).then_inc(s.exp_ready, 1)
                act.wait_ge(s.exp_ready, gi + 1)
                nc.scalar.activation(lg[j % 2][:, 0:n], lg[j % 2][:, 0:n], ACT.Ln, bias=1.0).then_inc(s.log_ready, 1)

            def spread_mask(k, q, first):
                if not first:
                    act.wait_ge(s.scan1_ready, k - 1)
                nc.scalar.copy(mask[q][:, :, 1:], over_channels(m.same[:, bass.ds(k * K, K)])).then_inc(s.mask1_ready, 1)

            def to_rows(k, first):
                act.wait_ge(s.scan1_ready, k + 1)
                if not first:
                    act.wait_ge(s.rows1_stored, 16 * k)
                nc.scalar.copy(rows[:, :, :], run[:, :, 1:].rearrange("p c t -> p t c")).then_inc(s.rows1_ready, 1)

            def pair(i, first, last):
                for j in range(PAIR_G):
                    softplus(i, j)
                    q = j // GROUPS
                    if j % GROUPS == 3 and not (first and q == 0):
                        to_rows(i * 2 + q - 1, first)
                    if j == 5:
                        spread_mask(i * 2 + 1, 1, first)
                    if j == GROUPS + 5 and not last:
                        spread_mask(i * 2 + 2, 0, False)

            nc.scalar.preload_act_table_set("natural_log_exp_and_others")
            act.wait_ge(s.prepared, 1)
            act.wait_ge(s.mask1_zero, 2)
            spread_mask(0, 0, True)
            pair(0, True, False)
            with act.Fori(1, TURNS) as i:
                pair(i, False, False)
            act.wait_ge(s.cnt_ready, TURNS)
            act.dma_start(d.cnt_tab[1:1 + NODES_PAD, :].rearrange("(p b) o -> p (b o)", b=NB), m.cnt[:, :]).then_inc(s.cnt_stored, 16)
            act.dma_start(d.cnt_tab[0:1, :], zeros[0:1, 0:1]).then_inc(s.cnt_stored, 16)
            act.dma_start(d.cnt_tab1.rearrange("(p b) o -> p (b o)", b=NB), m.cnt[:, :]).then_inc(s.cnt_stored, 16)
            act.wait_ge(s.cnt_stored, 48)
            act.dma_start(m.start[:, :], d.cnt_tab[0:NODES_PAD, :].rearrange("(p b) o -> p (b o)", b=NB)).then_inc(s.start_in, 16)
            with act.Fori(TURNS, CHUNKS // 2 - 1) as i:
                pair(i, False, False)
            pair(CHUNKS // 2 - 1, False, True)
            to_rows(CHUNKS - 1, False)

        @block.vector
        def _(dve):
            ch = Chain(dve, s.sum_dve)
            nc.vector.memset(zeros[:, :], 0.0).then_inc(s.zeros_ready, 1)
            nc.vector.memset(mask[0][:, :, 0:1], 0.0).then_inc(s.mask1_zero, 1)
            nc.vector.memset(mask[1][:, :, 0:1], 0.0).then_inc(s.mask1_zero, 1)
            ch.step(nc.vector.memset(run[:, :, K:K + 1], 0.0))
            ch.step(nc.vector.memset(open_t[:, :], 0.0))
            prepare(nc, dve, s, m)

            def below_nodes(w, first):
                if not first:
                    for q in range(2):
                        dve.wait_ge(s.found_ready[q], w * ((WB + 1 - q) // 2))
                    nc.vector.tensor_scalar(m.early.table_first[:, :], m.early.table_first[:, :], float(-WB), None, ALU.add).then_inc(s.turn_moved, 1)
                    nc.vector.tensor_scalar(m.early.search_node[:, :], m.early.search_node[:, :], float(WB), None, ALU.add).then_inc(s.turn_moved, 1)
                    dve.wait_ge(s.turn_moved, w * 2)
                for c in range(RC):
                    nc.vector.tensor_scalar(below[:, c, :], m.early.turn_node[:, :, :].rearrange("p b n -> p (b n)"),
                                            m.early.table_first[:, c:c + 1], None, ALU.is_ge).then_inc(s.below_ready, 1)

            def count_edges(w, b):
                dve.wait_ge(s.found_ready[b % 2], w * ((WB + 1 - b % 2) // 2) + b // 2 + 1)
                nc.vector.tensor_copy(found_row[:, b:b + 1], found[b % 2][:, ROW:ROW + 1]).then_inc(s.row_copied, 1)
                dve.wait_ge(s.row_copied, w * WB + b + 1)
                nc.vector.tensor_scalar(hit[:, :], found[b % 2][:, 0:ROW], m.early.search_node[:, b:b + 1], 0.0, ALU.is_le, ALU.add,
                                        accum_out=found_cnt[:, b:b + 1]).then_inc(s.found_used, 1)
                dve.wait_ge(s.found_used, w * WB + b + 1)
                if b == WB - 1:
                    nc.vector.scalar_tensor_tensor(m.cnt[:, bass.ds(w * WB, WB)], found_row[:, :], float(ROW), found_cnt[:, :],
                                                   ALU.mult, ALU.add).then_inc(s.cnt_ready, 1)
                    dve.wait_ge(s.cnt_ready, w + 1)

            def node_indices():
                dve.wait_ge(s.cnt_ready, TURNS)
                dve.wait_ge(s.start_in, 16)
                ch.then_wait(nc.vector.tensor_tensor(m.has[:, :], m.cnt[:, :], m.start[:, :], ALU.is_gt))
                ch.then_wait(nc.vector.tensor_scalar(m.tmp[:, :], m.cnt[:, :], -1.0, 0.0, ALU.add, ALU.max))
                ch.then_wait(nc.vector.tensor_copy(m.last_i[:, :], m.tmp[:, :]))
                ch.then_wait(nc.vector.scalar_tensor_tensor(m.tmp[:, :], m.start[:, :], float(-SKIP), m.has[:, :], ALU.add, ALU.mult))
                ch.then_wait(nc.vector.tensor_scalar(m.tmp[:, :], m.tmp[:, :], float(SKIP), None, ALU.add))
                ch.then_wait(nc.vector.tensor_copy(m.start_i[:, :], m.tmp[:, :]))

            def segment_indices():
                dve.wait_ge(s.d0_cnt_in, 16)
                seg_t, ok = m.seg_t[:, :], m.seg_ok[:, :]
                ch.then_wait(nc.vector.scalar_tensor_tensor(seg_t, m.d0_cnt[:, :], -1.0, m.pstart[:, :], ALU.add, ALU.subtract))
                ch.then_wait(nc.vector.scalar_tensor_tensor(ok, seg_t, float(T), m.same[:, 0:1], ALU.is_lt, ALU.mult))
                ch.then_wait(nc.vector.tensor_scalar(seg_t, seg_t, float(T - 1), 0.0, ALU.min, ALU.max))
                ch.then_wait(nc.vector.tensor_tensor(m.d0_t[:, :], seg_t, m.pstart[:, :], ALU.add))
                ch.then_wait(nc.vector.tensor_copy(m.seg_read_i[:, :], m.d0_t[:, :]))
                ch.then_wait(nc.vector.scalar_tensor_tensor(m.d0_t[:, :], m.d0_t[:, :], float(-SKIP), ok, ALU.add, ALU.mult))
                ch.then_wait(nc.vector.tensor_scalar(m.d0_t[:, :], m.d0_t[:, :], float(SKIP), None, ALU.add))
                nc.vector.tensor_copy(m.seg_write_i[:, :], m.d0_t[:, :]).then_inc(s.seg_idx_ready, 1)

            def clamp(i, j):
                gi = i * PAIR_G + j
                dve.wait_ge(s.z_ready, gi + 1)
                n = size(j) * P
                nc.vector.tensor_scalar(zc[j % 2][:, 0:n], z[j % 2][:, 0:n], m.b1h[:, 0:1], 14.0, ALU.add, ALU.min).then_inc(s.z_clamped, 1)

            def softplus_max(i, j, first):
                q, gi = j // GROUPS % 2, i * PAIR_G + j
                dve.wait_ge(s.log_ready, gi + 1)
                col, n = (j % GROUPS) * GC, size(j) * P
                nc.vector.scalar_tensor_tensor(spef[q][0:C, col:col + n], z[j % 2][:, 0:n], m.b1h[:, 0:1], lg[j % 2][:, 0:n],
                                               ALU.add, ALU.max).then_inc(s.sp_ready, 1)

            def message(i, j, first):
                q, gi = j // GROUPS % 2, i * PAIR_G + j
                t0 = (j % GROUPS) * GROUP
                if j % GROUPS == 0:
                    dve.wait_ge(s.gather1_in[q], 16 * K * (i + 1))
                dve.wait_ge(s.hw_ready, gi + 1)
                t1 = t0 + size(j)
                out = msg[:, :, 1 + t0:1 + t1]
                nc.vector.tensor_tensor(out, g[q][:, t0:t1, :].rearrange("p t c -> p c t"),
                                        hw[j % 2][:, 0:t1 - t0, 0:C].rearrange("p t c -> p c t"), ALU.mult).then_inc(s.msg_scaled, 1)
                dve.wait_ge(s.msg_scaled, gi + 1)
                nc.vector.tensor_tensor(out, out, hw[j % 2][:, 0:t1 - t0, C:2 * C].rearrange("p t c -> p c t"), ALU.add).then_inc(s.msg_ready, 1)
                if j % GROUPS == GROUPS - 1:
                    k = i * 2 + q
                    nc.vector.tensor_copy(msg[:, :, 0:1], run[:, :, K:K + 1]).then_inc(s.carry1_in, 1)
                    dve.wait_ge(s.carry1_in, k + 1)
                    dve.wait_ge(s.msg_ready, gi + 1)
                    dve.wait_ge(s.mask1_ready, k + 1)
                    if not first or q:
                        dve.wait_ge(s.rows1_ready, k)
                    nc.vector.tensor_tensor_scan(flat(run[:, :, :]), flat(mask[q][:, :, :]), flat(msg[:, :, :]), 0.0,
                                                 ALU.mult, ALU.add).then_inc(s.scan1_ready, 1)
                    dve.wait_ge(s.scan1_ready, k + 1)

            def pair(i, first, searching):
                for j in range(PAIR_G):
                    if searching and j == 0:
                        below_nodes(i, first)
                    clamp(i, j)
                    if searching and j % 2 == 0 and 0 < j // 2 <= WB:
                        count_edges(i, j // 2 - 1)
                    for lag, work in ((1, softplus_max), (3, message)):
                        if j >= lag:
                            work(i, j - lag, first)
                        elif not first:
                            work(i - 1, j - lag + PAIR_G, False)
                if searching:
                    for b in range((PAIR_G + 1) // 2 - 1, WB):
                        count_edges(i, b)

            pair(0, True, True)
            with dve.Fori(1, TURNS) as i:
                pair(i, False, True)
            with dve.Fori(TURNS, CHUNKS // 2) as i:
                pair(i, False, False)
            node_indices()
            i = CHUNKS // 2 - 1
            softplus_max(i, PAIR_G - 1, False)
            for j in (3, 2, 1):
                message(i, PAIR_G - j, False)

            nc.vector.tensor_copy(tail[:, :], run[:, :, K]).then_inc(s.tail1_ready, 1)
            segment_indices()
            dve.wait_ge(s.tail1_turned, 1)
            ch.then_wait(nc.vector.tensor_copy(tail_t[:, :], tail_ps))
            ch.then_wait(nc.vector.tensor_copy(link_t[:, :], link_ps))
            nc.vector.tensor_tensor_scan(open_t[:, 1:P + 1], link_t[:, :], tail_t[:, :], 0.0, ALU.mult, ALU.add).then_inc(s.open1_ready, 1)
            dve.wait_ge(s.seg1_in, 16)
            dve.wait_ge(s.carry1_ready, 1)
            nc.vector.tensor_tensor(seg_row[:, :], seg_row[:, :], carry_ps[:, :], ALU.add).then_inc(s.seg1_ready, 1)


def node_phase(nc, d, s, m):
    with ExitStack() as ctx:
        sb = lambda name, shape, dt=fp32: ctx.enter_context(nc.sbuf_tensor(name, shape, dt))
        pb = lambda name, shape: ctx.enter_context(nc.psum_tensor(name, shape, fp32))
        agg = sb("agg", [P, NB, C])
        tab = sb("tab", [P, NB, 2 * C])
        h2 = sb("h2", [P, NB, C])
        bd = sb("bd", [P, NB, C])
        xc = sb("xc2", [P, NB, C])
        stat = sb("stat2", [P, 2 * NB])
        wab = sb("wab", [C + 1, 2 * C])
        h2t = [sb(f"h2t{q}", [C + 1, 4 * P]) for q in range(2)]
        turn = [pb(f"turn{q}", [C, BANK]) for q in range(2)]
        ab = [pb(f"ab{q}", [P, BANK]) for q in range(2)]
        block = ctx.enter_context(nc.Block())

        @block.gpsimd
        def _(pool):
            for n, (b0, b1) in enumerate(SECTIONS):
                for b in range(b0, b1):
                    nc.gpsimd.indirect_dma_start(agg[:, b, :], None, d.s1,
                                                 bass.IndirectOffsetOnAxis(m.last_i[:, b:b + 1], 0)).then_inc(s.agg_in[n], 16)
            for u, (b0, b1) in enumerate(QUADS):
                pool.wait_ge(s.ab_out, u + 1)
                for b in range(b0, b1):
                    nc.gpsimd.indirect_dma_start(d.v, bass.IndirectOffsetOnAxis(m.start_i[:, b:b + 1], 0), bd[:, b, :], None,
                                                 bounds_check=EDGES_PAD - 1, oob_is_err=False).then_inc(s.v_stored, 16)
            pool.wait_ge(s.bd_stored, 16)
            nc.gpsimd.indirect_dma_start(m.b_open[:, :], None, d.b_tab,
                                         bass.IndirectOffsetOnAxis(m.d0_i[:, 0:1], 0)).then_inc(s.b_open_in, 16)
            pool.wait_ge(s.v_stored, 16 * NB)
            pool.wait_ge(s.b_open_in, 16)

        @block.sync
        def _(sp):
            sp.dma_start(wab[0:C, 0:C], d.wlin_t[0:C, 0:C]).then_inc(s.wab_in, 16)
            sp.dma_start(wab[0:C, C:2 * C], d.wlin_t[C:2 * C, 0:C]).then_inc(s.wab_in, 16)
            sp.wait_ge(s.wab_zero, 1)
            sp.dma_start(wab[C:C + 1, C:2 * C], d.b_lin[0:C].unsqueeze(0)).then_inc(s.wab_in, 16)
            sp.wait_ge(s.ab_out, len(QUADS))
            sp.wait_ge(s.tab_h2, len(SECTIONS))
            sp.dma_start(d.tab2.rearrange("(p b) c -> p b c", b=NB), tab[:, :, :]).then_inc(s.tab_stored, 16)
            sp.dma_start(d.b_tab.rearrange("(p b) c -> p b c", b=NB), bd[:, :, :]).then_inc(s.bd_stored, 16)
            sp.wait_ge(s.tab_stored, 16)
            sp.wait_ge(s.bd_stored, 16)

        @block.scalar
        def _(act):
            act.wait_ge(s.h2t_ones, 2)
            u = 0
            for n, (b0, b1) in enumerate(SECTIONS):
                act.wait_ge(s.var2_ready, n + 1)
                nc.scalar.activation(stat[:, NB + b0:NB + b1], stat[:, NB + b0:NB + b1], ACT.Sqrt).then_inc(s.std2_ready, 1)
                act.wait_ge(s.h2_ready, n + 1)
                nc.scalar.copy(tab[:, b0:b1, C:2 * C], h2[:, b0:b1, :]).then_inc(s.tab_h2, 1)
                while u < len(QUADS) and QUADS[u][1] <= b1:
                    w = (QUADS[u][1] - QUADS[u][0]) * P
                    act.wait_ge(s.turned2, u + 1)
                    if u >= 2:
                        act.wait_ge(s.ab_ready, u - 1)
                    nc.scalar.copy(h2t[u % 2][0:C, 0:w], turn[u % 2][:, 0:w]).then_inc(s.h2t_ready, 1)
                    u += 1

        @block.tensor
        def _(pe):
            pe.wait_ge(s.wab_in, 48)

            def turn_quad(u):
                b0, b1 = QUADS[u]
                pe.wait_ge(s.h2_ready, section_of(b0) + 1)
                if u >= 2:
                    pe.wait_ge(s.h2t_ready, u - 1)
                for b in range(b0, b1):
                    last = nc.tensor.transpose(turn[u % 2][:, (b - b0) * P:(b - b0 + 1) * P], h2[:, b, :], m.ident[:, :])
                last.then_inc(s.turned2, 1)

            def product(u):
                b0, b1 = QUADS[u]
                pe.wait_ge(s.h2t_ready, u + 1)
                if u >= 2:
                    pe.wait_ge(s.ab_out, u - 1)
                for b in range(b0, b1):
                    at = (b - b0) * P
                    last = nc.tensor.matmul(ab[u % 2][:, at:at + P], h2t[u % 2][:, at:at + P], wab[:, :], start=True, stop=True)
                last.then_inc(s.ab_ready, 1)

            for u in range(len(QUADS)):
                turn_quad(u)
                product(u)

        @block.vector
        def _(dve):
            ch = Chain(dve, s.node_dve)
            nc.vector.memset(wab[C:C + 1, :], 0.0).then_inc(s.wab_zero, 1)
            for q in range(2):
                nc.vector.memset(h2t[q][C:C + 1, :], 1.0).then_inc(s.h2t_ones, 1)

            def normalise(n):
                b0, b1 = SECTIONS[n]
                part = slice(b0, b1)
                dve.wait_ge(s.agg_in[n], 16 * (b1 - b0))
                ch.then_wait(nc.vector.tensor_tensor(agg[:, part, :], agg[:, part, :], over_last(m.has[:, part]), ALU.mult))
                ch.then_wait(nc.vector.tensor_tensor(m.x[:, part, :], m.x[:, part, :], agg[:, part, :], ALU.add))
                layer_norm_relu(nc, ch, s.var2_ready, s.std2_ready, n + 1, m.x[:, part, :], h2[:, part, :], xc[:, part, :],
                                stat[:, b0:b1], stat[:, NB + b0:NB + b1]).then_inc(s.h2_ready, 1)

            def copy_out(n):
                for u, (b0, b1) in enumerate(QUADS):
                    if section_of(b0) == n:
                        dve.wait_ge(s.ab_ready, u + 1)
                        quad = ab[u % 2][:, 0:(b1 - b0) * P].rearrange("p (b c) -> p b c", c=2 * C)
                        ch.step(nc.vector.tensor_copy(tab[:, b0:b1, 0:C], quad[:, :, 0:C]))
                        dve.wait_ge(s.node_dve, ch.n)
                        nc.vector.tensor_copy(bd[:, b0:b1, :], quad[:, :, C:2 * C]).then_inc(s.ab_out, 1)

            for n in range(len(SECTIONS)):
                normalise(n)
                copy_out(n)


def softmax_phase(nc, d, s, m):
    with ExitStack() as ctx:
        sb = lambda name, shape, dt=fp32: ctx.enter_context(nc.sbuf_tensor(name, shape, dt))
        pb = lambda name, shape: ctx.enter_context(nc.psum_tensor(name, shape, fp32))
        g = [sb(f"ah_src{q}", [P, K, 2 * C]) for q in range(2)]
        idx = [sb(f"idx2_{q}", [P, K], i32) for q in range(2)]
        vin = sb("vin", [P, K, C])
        rows = sb("rows2", [P, K, 2 * C])
        unit = lambda name: sb(name, [P, C, K + 1])
        mask = [unit(f"mask2_{q}") for q in range(2)]
        vct = [unit(f"vct{q}") for q in range(2)]
        bexp, zb = unit("bexp"), unit("zb")
        mx = [unit(f"mx{q}") for q in range(2)]
        pw = [unit(f"pw{q}") for q in range(2)]
        wt = [unit(f"wt{q}") for q in range(2)]
        qs, den, num = unit("qs"), unit("den"), unit("num")
        block = ctx.enter_context(nc.Block())
        s2_rows = d.s2.rearrange("(p t) c -> p t c", t=T)
        m2_rows = d.m2.rearrange("(p k) u -> p k u", k=CHUNKS)
        v_rows = d.v.rearrange("(p t) c -> p t c", t=T)
        LASTP = CHUNKS // 2 - 1

        @block.sync
        def _(sp):
            def load_sources(i, q, first):
                if not first:
                    sp.wait_ge(s.gather2_in[q], 16 * K * i)
                sp.dma_start(idx[q][:, :], d.src_rows[:, bass.ds((i * 2 + q) * K, K)]).then_inc(s.idx2_in[q], 16)

            def load_b(k, first):
                if not first:
                    sp.wait_ge(s.vct_ready, k)
                sp.dma_start(vin[:, :, :], v_rows[:, bass.ds(k * K, K), :]).then_inc(s.v_in, 16)

            def store(k, q):
                sp.wait_ge(s.mx_ready, k + 1)
                sp.dma_start(m2_rows[:, bass.ds(k, 1), :], flat(mx[q][:, :, :]).unsqueeze(1)).then_inc(s.mx_stored[q], 16)
                sp.wait_ge(s.rows2_ready, k + 1)
                sp.dma_start(s2_rows[:, bass.ds(k * K, K), :], rows[:, :, :]).then_inc(s.rows2_stored, 16)

            load_sources(0, 0, True)
            load_sources(0, 1, True)
            load_b(0, True)
            load_b(1, False)
            with sp.Fori(0, LASTP) as i:
                for q in range(2):
                    load_sources(i + 1, q, False)
                    load_b(i * 2 + q + 2, False)
                    store(i * 2 + q, q)
            store(CHUNKS - 2, 0)
            store(CHUNKS - 1, 1)
            sp.wait_ge(s.rows2_stored, 16 * CHUNKS)
            sp.wait_ge(s.mx_stored[0], 16 * (LASTP + 1))
            sp.wait_ge(s.mx_stored[1], 16 * (LASTP + 1))

        @block.gpsimd
        def _(pool):
            def gather(i, q, first):
                if not first:
                    pool.wait_ge(s.q_ready, i * 2 + q - 1)
                pool.wait_ge(s.idx2_in[q], 16 * (i + 1))
                pool.sem_inc(s.idx2_seen, 1)
                for t in range(K):
                    nc.gpsimd.indirect_dma_start(g[q][:, t, :], None, d.tab2,
                                                 bass.IndirectOffsetOnAxis(idx[q][:, t:t + 1], 0)).then_inc(s.gather2_in[q], 16)

            gather(0, 0, True)
            gather(0, 1, True)
            with pool.Fori(1, CHUNKS // 2) as i:
                gather(i, 0, False)
                gather(i, 1, False)

        @block.scalar
        def _(act):
            def spread(k, q, first):
                if not first:
                    act.wait_ge(s.w_ready, k - 1)
                nc.scalar.copy(mask[q][:, :, 1:], over_channels(m.same[:, bass.ds(k * K, K)])).then_inc(s.mask2_ready, 1)
                act.wait_ge(s.v_in, 16 * (k + 1))
                if not first:
                    act.wait_ge(s.b_ready, k - 1)
                nc.scalar.copy(vct[q][:, :, 1:], vin[:, :, :].rearrange("p t c -> p c t")).then_inc(s.vct_ready, 1)

            def weights(k, q):
                act.wait_ge(s.step_raw, k + 1)
                nc.scalar.activation(wt[q][:, :, 1:], wt[q][:, :, 1:], ACT.Relu).then_inc(s.step_ready, 1)
                act.wait_ge(s.arg_ready, k + 1)
                nc.scalar.activation(pw[q][:, :, 1:], pw[q][:, :, 1:], ACT.Exp).then_inc(s.pw_ready, 1)
                act.wait_ge(s.step_ready, k + 1)
                nc.scalar.activation(wt[q][:, :, 1:], wt[q][:, :, 1:], ACT.Exp, scale=-1.0).then_inc(s.wt_ready, 1)

            def to_rows(k, first):
                act.wait_ge(s.sums_ready, 2 * (k + 1))
                if not first:
                    act.wait_ge(s.rows2_stored, 16 * k)
                nc.scalar.copy(rows[:, :, 0:C], den[:, :, 1:].rearrange("p c t -> p t c")).then_inc(s.den_copied, 1)
                nc.scalar.copy(rows[:, :, C:2 * C], num[:, :, 1:].rearrange("p c t -> p t c")).then_inc(s.num_copied, 1)
                act.wait_ge(s.den_copied, k + 1)
                act.wait_ge(s.num_copied, k + 1)
                act.sem_inc(s.rows2_ready, 1)

            def pair(i, first, last):
                for q in range(2):
                    k = i * 2 + q
                    weights(k, q)
                    if not last:
                        spread(k + 2, q, False)
                    to_rows(k, first and q == 0)

            act.wait_ge(s.mask2_zero, 2)
            spread(0, 0, True)
            spread(1, 1, True)
            pair(0, True, False)
            with act.Fori(1, LASTP) as i:
                pair(i, False, False)
            pair(LASTP, False, True)

        @block.vector
        def _(dve):
            ch = Chain(dve, s.soft_dve)
            nc.vector.memset(mask[0][:, :, 0:1], 0.0).then_inc(s.mask2_zero, 1)
            nc.vector.memset(mask[1][:, :, 0:1], 0.0).then_inc(s.mask2_zero, 1)
            ch.step(nc.vector.memset(mx[1][:, :, K:K + 1], 0.0))
            ch.step(nc.vector.memset(den[:, :, K:K + 1], 0.0))
            ch.step(nc.vector.memset(num[:, :, K:K + 1], 0.0))
            ch.step(nc.vector.memset(wt[0][:, :, 0:1], 0.0))
            ch.step(nc.vector.memset(wt[1][:, :, 0:1], 0.0))
            ch.step(nc.vector.tensor_copy(bexp[:, :, K], m.b_open[:, :]))
            dve.wait_ge(s.soft_dve, ch.n)

            def scale_step(k, q):
                dve.wait_ge(s.wt_ready, k + 1)
                nc.vector.tensor_tensor(wt[q][:, :, 1:], wt[q][:, :, 1:], mask[q][:, :, 1:], ALU.mult).then_inc(s.w_ready, 1)

            def spread_b(k, q):
                dve.wait_ge(s.vct_ready, k + 1)
                dve.wait_ge(s.mask2_ready, k + 1)
                nc.vector.tensor_copy(vct[q][:, :, 0:1], bexp[:, :, K:K + 1]).then_inc(s.b_carry, 1)
                dve.wait_ge(s.b_carry, k + 1)
                nc.vector.tensor_tensor_scan(flat(bexp[:, :, :]), flat(mask[q][:, :, :]), flat(vct[q][:, :, :]), 0.0,
                                             ALU.mult, ALU.add).then_inc(s.b_ready, 1)

            def attention(i, q, first):
                k = i * 2 + q
                dve.wait_ge(s.gather2_in[q], 16 * K * (i + 1))
                dve.wait_ge(s.b_ready, k + 1)
                nc.vector.tensor_tensor(zb[:, :, 1:], g[q][:, :, 0:C].rearrange("p t c -> p c t"), bexp[:, :, 1:],
                                        ALU.add).then_inc(s.z2_ready, 1)
                nc.vector.tensor_copy(zb[:, :, 0:1], mx[1 - q][:, :, K:K + 1]).then_inc(s.m_carry, 1)
                dve.wait_ge(s.z2_ready, k + 1)
                dve.wait_ge(s.m_carry, k + 1)
                if not first:
                    dve.wait_ge(s.mx_stored[q], 16 * i)
                nc.vector.tensor_tensor_scan(flat(mx[q][:, :, :]), flat(mask[q][:, :, :]), flat(zb[:, :, :]), 0.0,
                                             ALU.mult, ALU.max).then_inc(s.mx_ready, 1)
                dve.wait_ge(s.mx_ready, k + 1)
                nc.vector.tensor_tensor(wt[q][:, :, 1:], mx[q][:, :, 1:], mx[q][:, :, 0:K], ALU.subtract).then_inc(s.step_raw, 1)
                nc.vector.scalar_tensor_tensor(pw[q][:, :, 1:], zb[:, :, 1:], 0.0, mx[q][:, :, 1:], ALU.max, ALU.subtract).then_inc(s.arg_ready, 1)

            def sums(k, q, first):
                dve.wait_ge(s.pw_ready, k + 1)
                nc.vector.tensor_tensor(qs[:, :, 1:], pw[q][:, :, 1:], g[q][:, :, C:2 * C].rearrange("p t c -> p c t"),
                                        ALU.mult).then_inc(s.q_ready, 1)
                nc.vector.tensor_copy(pw[q][:, :, 0:1], den[:, :, K:K + 1]).then_inc(s.d_carry, 1)
                nc.vector.tensor_copy(qs[:, :, 0:1], num[:, :, K:K + 1]).then_inc(s.n_carry, 1)
                dve.wait_ge(s.d_carry, k + 1)
                dve.wait_ge(s.w_ready, k + 1)
                if not first:
                    dve.wait_ge(s.rows2_ready, k)
                nc.vector.tensor_tensor_scan(flat(den[:, :, :]), flat(wt[q][:, :, :]), flat(pw[q][:, :, :]), 0.0,
                                             ALU.mult, ALU.add).then_inc(s.sums_ready, 1)
                dve.wait_ge(s.q_ready, k + 1)
                dve.wait_ge(s.n_carry, k + 1)
                nc.vector.tensor_tensor_scan(flat(num[:, :, :]), flat(wt[q][:, :, :]), flat(qs[:, :, :]), 0.0,
                                             ALU.mult, ALU.add).then_inc(s.sums_ready, 1)
                dve.wait_ge(s.sums_ready, 2 * (k + 1))

            def pair(i, first, last):
                for q in range(2):
                    k = i * 2 + q
                    attention(i, q, first)
                    if not (last and q == 1):
                        spread_b(k + 1, 1 - q)
                    scale_step(k, q)
                    sums(k, q, first and q == 0)

            spread_b(0, 0)
            pair(0, True, False)
            with dve.Fori(1, LASTP) as i:
                pair(i, False, False)
            pair(LASTP, False, True)
            for r, part in enumerate((mx[1], den, num)):
                ch.step(nc.vector.tensor_copy(m.tail2[:, r, :], part[:, :, K]))
            dve.wait_ge(s.soft_dve, ch.n)

        @block.tensor
        def _(pe):
            pe.wait_ge(s.mask2_zero, 2)


def end_phase(nc, d, s, m):
    with ExitStack() as ctx:
        sb = lambda name, shape, dt=fp32: ctx.enter_context(nc.sbuf_tensor(name, shape, dt))
        pb = lambda name, shape: ctx.enter_context(nc.psum_tensor(name, shape, fp32))
        tail_ps = pb("tail2_ps", [C, 4, P])
        carry_ps = pb("carry2_ps", [P, BANK])[:, 0:3 * C].rearrange("p (r c) -> p r c", c=C)
        tl = sb("tl", [C, 4, P])
        open_t = sb("open2_t", [C, 3, P + 1])
        w_old, w_new = sb("w_old", [C, P]), sb("w_new", [C, P])
        mrow = sb("mrow", [P, U])
        pick = sb("pick", [P, C, K + 1])
        slot = sb("slot_hit", [P, K + 1])
        seg = sb("seg2", [P, 2 * C])
        seg_m, mm = sb("seg_m", [P, C]), sb("mm", [P, C])
        e_row, e_car = sb("e_row", [P, C]), sb("e_car", [P, C])
        carry = sb("carry2", [P, 3, C])
        junk = sb("junk_k", [P, CHUNKS])
        mrow_f, mrow_i, tau = sb("mrow_f", [P, 1]), sb("mrow_i", [P, 1], i32), sb("tau", [P, 1])
        agg = sb("agg2", [P, NB, 2 * C])
        nf = sb("nf", [P, NB, 2 * C])
        res = sb("res", [P, NB, C])
        bo = sb("bo", [P, C])
        wo = sb("wo", [2 * C, C])
        nft = [sb(f"nft{q}", [P, BANK]) for q in range(2)]
        turn = [pb(f"turn3_{q}", [P, BANK]) for q in range(2)]
        prod = [pb(f"prod{q}", [P, BANK]) for q in range(2)]
        block = ctx.enter_context(nc.Block())

        @block.sync
        def _(sp):
            sp.dma_start(nf[:, :, C:2 * C], d.tab2.rearrange("(p b) c -> p b c", b=NB)[:, :, C:2 * C]).then_inc(s.h2_in, 16)
            sp.dma_start(wo[:, :], d.wout_t).then_inc(s.wo_in, 16)
            sp.dma_start(bo[:, :], d.b_out.unsqueeze(0).to_broadcast([P, C])).then_inc(s.bo_in, 16)
            out = d.out.rearrange("(p b) c -> p b c", b=NB)
            for n, (b0, b1) in enumerate(SECTIONS):
                sp.wait_ge(s.res_ready, [e for _, e in QUADS].index(b1) + 1)
                sp.dma_start(out[:, b0:b1, :], res[:, b0:b1, :]).then_inc(s.out_stored, 16)
            sp.wait_ge(s.out_stored, 16 * len(SECTIONS))

        @block.gpsimd
        def _(pool):
            nc.gpsimd.indirect_dma_start(seg[:, :], None, d.s2,
                                         bass.IndirectOffsetOnAxis(m.seg_read_i[:, 0:1], 0)).then_inc(s.seg2_in, 16)
            pool.wait_ge(s.mrow_ready, 1)
            nc.gpsimd.indirect_dma_start(mrow[:, :], None, d.m2,
                                         bass.IndirectOffsetOnAxis(mrow_i[:, 0:1], 0)).then_inc(s.mrow_in, 16)
            pool.wait_ge(s.seg2_ready, 1)
            nc.gpsimd.indirect_dma_start(d.s2, bass.IndirectOffsetOnAxis(m.seg_write_i[:, 0:1], 0), seg[:, :], None,
                                         bounds_check=EDGES_PAD - 1, oob_is_err=False).then_inc(s.seg2_stored, 16)
            pool.wait_ge(s.seg2_stored, 16)
            for n, (b0, b1) in enumerate(SECTIONS):
                for b in range(b0, b1):
                    nc.gpsimd.indirect_dma_start(agg[:, b, :], None, d.s2,
                                                 bass.IndirectOffsetOnAxis(m.last_i[:, b:b + 1], 0)).then_inc(s.agg2_in[n], 16)

        @block.tensor
        def _(pe):
            for r in range(3):
                nc.tensor.transpose(tail_ps[:, r, :], m.tail2[:, r, :], m.ident[:, :])
            nc.tensor.transpose(tail_ps[:, 3, :], m.link[:, 0:1].to_broadcast([P, C]), m.ident[:, :]).then_inc(s.tail2_turned, 1)
            pe.wait_ge(s.open2_ready, 1)
            for r in range(3):
                last = nc.tensor.transpose(carry_ps[:, r, :], open_t[:, r, 0:P], m.ident[0:C, 0:C])
            last.then_inc(s.carry2_turned, 1)
            pe.wait_ge(s.wo_in, 16)
            for u, (b0, b1) in enumerate(QUADS):
                pe.wait_ge(s.nf_ready, section_of(b0) + 1)
                if u >= 2:
                    pe.wait_ge(s.nft_ready, u - 1)
                for b in range(b0, b1):
                    last = nc.tensor.transpose(turn[u % 2][:, (b - b0) * P:(b - b0 + 1) * P], nf[:, b, :], m.ident[:, :])
                last.then_inc(s.turned3, 1)
                pe.wait_ge(s.nft_ready, u + 1)
                if u >= 2:
                    pe.wait_ge(s.res_ready, u - 1)
                for b in range(b0, b1):
                    last = nc.tensor.matmul(prod[u % 2][:, (b - b0) * C:(b - b0 + 1) * C],
                                            nft[u % 2][:, (b - b0) * P:(b - b0 + 1) * P], wo[:, :], start=True, stop=True)
                last.then_inc(s.prod_ready, 1)

        @block.scalar
        def _(act):
            def exp_of(ap, n):
                act.wait_ge(s.exp_asked, n)
                nc.scalar.activation(ap, ap, ACT.Exp).then_inc(s.exp_answered, 1)

            exp_of(w_old[:, :], 1)
            exp_of(w_new[:, :], 2)
            exp_of(e_row[:, :], 3)
            exp_of(e_car[:, :], 4)
            for u, (b0, b1) in enumerate(QUADS):
                act.wait_ge(s.turned3, u + 1)
                if u >= 2:
                    act.wait_ge(s.prod_ready, u - 1)
                nc.scalar.copy(nft[u % 2][:, 0:(b1 - b0) * P], turn[u % 2][:, 0:(b1 - b0) * P]).then_inc(s.nft_ready, 1)

        @block.vector
        def _(dve):
            ch = Chain(dve, s.end_dve)
            ch.then_wait(nc.vector.tensor_scalar(junk[:, :], m.kstart[:, :], m.seg_t[:, 0:1], 0.0, ALU.is_le, ALU.add,
                                                 accum_out=mrow_f[:, :]))
            ch.then_wait(nc.vector.tensor_scalar(mrow_f[:, :], mrow_f[:, :], -1.0, None, ALU.add))
            ch.then_wait(nc.vector.scalar_tensor_tensor(tau[:, :], mrow_f[:, :], float(-K), m.seg_t[:, :], ALU.mult, ALU.add))
            ch.then_wait(nc.vector.scalar_tensor_tensor(mrow_f[:, :], mrow_f[:, :], float(K), m.pstart[:, :], ALU.mult, ALU.add))
            ch.then_wait(nc.vector.tensor_scalar(mrow_f[:, :], mrow_f[:, :], 1.0 / K, 0.25, ALU.mult, ALU.add))
            ch.then_wait(nc.vector.tensor_copy(mrow_i[:, :], mrow_f[:, :]))
            ch.then_wait(nc.vector.tensor_scalar(slot[:, :], m.slot[:, :], tau[:, 0:1], None, ALU.is_equal))
            nc.vector.memset(junk[:, 0:1], 0.0).then_inc(s.mrow_ready, 1)
            dve.wait_ge(s.tail2_turned, 1)
            ch.then_wait(nc.vector.tensor_copy(tl[:, :, :], tail_ps[:, :, :]))
            ch.then_wait(nc.vector.memset(open_t[:, :, :], 0.0))
            ch.then_wait(nc.vector.tensor_tensor_scan(open_t[:, 0, 1:], tl[:, 3, :], tl[:, 0, :], 0.0, ALU.mult, ALU.max))
            ch.then_wait(nc.vector.tensor_tensor(w_old[:, :], open_t[:, 0, 0:P], open_t[:, 0, 1:], ALU.subtract))
            nc.vector.tensor_scalar(w_old[:, :], w_old[:, :], 0.0, None, ALU.min).then_inc(s.exp_asked, 1)
            nc.vector.tensor_tensor(w_new[:, :], tl[:, 0, :], open_t[:, 0, 1:], ALU.subtract).then_inc(s.exp_asked, 1)
            dve.wait_ge(s.exp_answered, 2)
            ch.then_wait(nc.vector.tensor_tensor(w_old[:, :], w_old[:, :], tl[:, 3, :], ALU.mult))
            for r in (1, 2):
                ch.then_wait(nc.vector.tensor_tensor(tl[:, r, :], tl[:, r, :], w_new[:, :], ALU.mult))
                ins = nc.vector.tensor_tensor_scan(open_t[:, r, 1:], w_old[:, :], tl[:, r, :], 0.0, ALU.mult, ALU.add)
                if r == 1:
                    ch.then_wait(ins)
                else:
                    ins.then_inc(s.open2_ready, 1)
            dve.wait_ge(s.mrow_in, 16)
            ch.then_wait(nc.vector.tensor_tensor(pick[:, :, :], mrow[:, :].rearrange("p (c t) -> p c t", c=C),
                                                 over_channels(slot[:, :]), ALU.mult))
            ch.then_wait(nc.vector.tensor_reduce(seg_m[:, :], pick[:, :, :], AX.X, ALU.add))
            dve.wait_ge(s.carry2_turned, 1)
            ch.then_wait(nc.vector.tensor_copy(carry[:, :, :], carry_ps[:, :, :]))
            ch.then_wait(nc.vector.tensor_tensor(mm[:, :], seg_m[:, :], carry[:, 0, :], ALU.max))
            nc.vector.tensor_tensor(e_row[:, :], seg_m[:, :], mm[:, :], ALU.subtract).then_inc(s.exp_asked, 1)
            nc.vector.tensor_tensor(e_car[:, :], carry[:, 0, :], mm[:, :], ALU.subtract).then_inc(s.exp_asked, 1)
            dve.wait_ge(s.seg2_in, 16)
            dve.wait_ge(s.exp_answered, 4)
            for r in range(2):
                part = seg[:, r * C:(r + 1) * C]
                ch.then_wait(nc.vector.tensor_tensor(part, part, e_row[:, :], ALU.mult))
                ch.then_wait(nc.vector.tensor_tensor(carry[:, 1 + r, :], carry[:, 1 + r, :], e_car[:, :], ALU.mult))
                ins = nc.vector.tensor_tensor(part, part, carry[:, 1 + r, :], ALU.add)
                if r == 0:
                    ch.then_wait(ins)
                else:
                    ins.then_inc(s.seg2_ready, 1)
            dve.wait_ge(s.bo_in, 16)
            ch.then_wait(nc.vector.tensor_tensor(m.x[:, :, :], m.x[:, :, :], bo[:, :].unsqueeze(1).to_broadcast([P, NB, C]), ALU.add))
            dve.wait_ge(s.h2_in, 16)
            ch.then_wait(nc.vector.tensor_tensor(nf[:, :, C:2 * C], nf[:, :, C:2 * C], over_last(m.has[:, :]), ALU.mult))
            for n, (b0, b1) in enumerate(SECTIONS):
                part = slice(b0, b1)
                dve.wait_ge(s.agg2_in[n], 16 * (b1 - b0))
                ch.then_wait(nc.vector.reciprocal(agg[:, part, 0:C], agg[:, part, 0:C]))
                ch.then_wait(nc.vector.tensor_tensor(agg[:, part, C:2 * C], agg[:, part, C:2 * C], agg[:, part, 0:C], ALU.mult))
                nc.vector.tensor_tensor(nf[:, part, 0:C], agg[:, part, C:2 * C], over_last(m.has[:, part]), ALU.mult).then_inc(s.nf_ready, 1)
                for u, (c0, c1) in enumerate(QUADS):
                    if section_of(c0) == n:
                        dve.wait_ge(s.prod_ready, u + 1)
                        nc.vector.tensor_tensor(res[:, c0:c1, :], prod[u % 2][:, 0:(c1 - c0) * C].rearrange("p (b c) -> p b c", c=C),
                                                m.x[:, c0:c1, :], ALU.add).then_inc(s.res_ready, 1)


class Semaphores:

    def __init__(self, sem):
        self.table_in = sem("table_in")
        self.table_ready = sem("table_ready")
        self.below_ready = sem("below_ready")
        self.turn_moved = sem("turn_moved")
        self.row_copied = sem("row_copied")
        self.found_used = sem("found_used")
        self.x_in = sem("x_in")
        self.dst_in = sem("dst_in")
        self.h1_ready = sem("h1_ready")
        self.h1_stored = sem("h1_stored")
        self.w_in = sem("w_in")
        self.w3_in = sem("w3_in")
        self.var1_ready = sem("var1_ready")
        self.std1_ready = sem("std1_ready")
        self.setup_dve = sem("setup_dve")
        self.cnt_ready = sem("cnt_ready")
        self.cnt_stored = sem("cnt_stored")
        self.start_in = sem("start_in")
        self.z_ready = sem("z_ready")
        self.hw_ready = sem("hw_ready")
        self.v_zeroed = sem("v_zeroed")
        self.rows1_ready = sem("rows1_ready")
        self.msg_ready = sem("msg_ready")
        self.d0_cnt_in = sem("d0_cnt_in")
        self.seg_idx_ready = sem("seg_idx_ready")
        self.seg1_in = sem("seg1_in")
        self.seg1_ready = sem("seg1_ready")
        self.seg1_stored = sem("seg1_stored")
        self.sp_ready = sem("sp_ready")
        self.tail1_ready = sem("tail1_ready")
        self.tail1_turned = sem("tail1_turned")
        self.open1_ready = sem("open1_ready")
        self.carry1_ready = sem("carry1_ready")
        self.z_clamped = sem("z_clamped")
        self.exp_ready = sem("exp_ready")
        self.log_ready = sem("log_ready")
        self.scan1_ready = sem("scan1_ready")
        self.mask1_ready = sem("mask1_ready")
        self.mask1_zero = sem("mask1_zero")
        self.sum_dve = sem("sum_dve")
        self.msg_scaled = sem("msg_scaled")
        self.carry1_in = sem("carry1_in")
        self.v_stored = sem("v_stored")
        self.bd_stored = sem("bd_stored")
        self.b_open_in = sem("b_open_in")
        self.wab_in = sem("wab_in")
        self.wab_zero = sem("wab_zero")
        self.tab_stored = sem("tab_stored")
        self.var2_ready = sem("var2_ready")
        self.std2_ready = sem("std2_ready")
        self.h2_ready = sem("h2_ready")
        self.tab_h2 = sem("tab_h2")
        self.turned2 = sem("turned2")
        self.ab_ready = sem("ab_ready")
        self.h2t_ones = sem("h2t_ones")
        self.h2t_ready = sem("h2t_ready")
        self.ab_out = sem("ab_out")
        self.node_dve = sem("node_dve")
        self.vct_ready = sem("vct_ready")
        self.v_in = sem("v_in")
        self.mx_ready = sem("mx_ready")
        self.rows2_ready = sem("rows2_ready")
        self.rows2_stored = sem("rows2_stored")
        self.q_ready = sem("q_ready")
        self.w_ready = sem("w_ready")
        self.mask2_ready = sem("mask2_ready")
        self.b_ready = sem("b_ready")
        self.arg_ready = sem("arg_ready")
        self.step_ready = sem("step_ready")
        self.pw_ready = sem("pw_ready")
        self.wt_ready = sem("wt_ready")
        self.sums_ready = sem("sums_ready")
        self.den_copied = sem("den_copied")
        self.num_copied = sem("num_copied")
        self.mask2_zero = sem("mask2_zero")
        self.soft_dve = sem("soft_dve")
        self.b_carry = sem("b_carry")
        self.z2_ready = sem("z2_ready")
        self.m_carry = sem("m_carry")
        self.d_carry = sem("d_carry")
        self.n_carry = sem("n_carry")
        self.h2_in = sem("h2_in")
        self.wo_in = sem("wo_in")
        self.bo_in = sem("bo_in")
        self.res_ready = sem("res_ready")
        self.out_stored = sem("out_stored")
        self.seg2_in = sem("seg2_in")
        self.mrow_ready = sem("mrow_ready")
        self.mrow_in = sem("mrow_in")
        self.seg2_ready = sem("seg2_ready")
        self.seg2_stored = sem("seg2_stored")
        self.tail2_turned = sem("tail2_turned")
        self.open2_ready = sem("open2_ready")
        self.carry2_turned = sem("carry2_turned")
        self.nf_ready = sem("nf_ready")
        self.nft_ready = sem("nft_ready")
        self.turned3 = sem("turned3")
        self.prod_ready = sem("prod_ready")
        self.exp_asked = sem("exp_asked")
        self.exp_answered = sem("exp_answered")
        self.end_dve = sem("end_dve")
        self.w23_zero = sem("w23_zero")
        self.idx1_seen = sem("idx1_seen")
        self.idx2_seen = sem("idx2_seen")
        self.iota_ready = sem("iota_ready")
        self.prepare_dve = sem("prepare_dve")
        self.prepared = sem("prepared")
        self.rows1_stored = sem("rows1_stored")
        self.step_raw = sem("step_raw")
        self.zeros_ready = sem("zeros_ready")
        self.edge_in = [sem(f"edge_in{q}") for q in range(2)]
        self.gather1_in = [sem(f"gather1_in{q}") for q in range(2)]
        self.gather2_in = [sem(f"gather2_in{q}") for q in range(2)]
        self.idx1_in = [sem(f"idx1_in{q}") for q in range(2)]
        self.idx2_in = [sem(f"idx2_in{q}") for q in range(2)]
        self.mx_stored = [sem(f"mx_stored{q}") for q in range(2)]
        self.found_ready = [sem(f"found_ready{q}") for q in range(2)]
        self.agg2_in = [sem(f"agg2_in{n}") for n in range(len(SECTIONS))]
        self.agg_in = [sem(f"agg_in{n}") for n in range(len(SECTIONS))]


class Dram:

    def __init__(self, nc, x, src, dst_ext, dst_rows, rbf_t, ef_t, W1, b1, W2, b2, W3, b3, wlin_t, b_lin, wout_t, b_out, out):
        self.x = x
        self.src_rows = src.rearrange("(p t) -> p t", t=T)
        self.dst_ext = dst_ext
        self.dst_rows = dst_rows
        self.rbf_t = rbf_t
        self.ef_t = ef_t
        self.W1 = W1
        self.b1 = b1
        self.W2 = W2
        self.b2 = b2
        self.W3 = W3
        self.b3 = b3
        self.wlin_t = wlin_t
        self.b_lin = b_lin
        self.wout_t = wout_t
        self.b_out = b_out
        self.out = out
        self.h1_tab = nc.dram_tensor("h1_tab", [NODES_PAD, C], fp32).ap()
        self.cnt_tab = nc.dram_tensor("cnt_tab", [NODES_PAD + 1, 1], fp32).ap()
        self.cnt_tab1 = nc.dram_tensor("cnt_tab1", [NODES_PAD, 1], fp32).ap()
        self.s1 = nc.dram_tensor("s1", [EDGES_PAD, C], fp32).ap()
        self.v = nc.dram_tensor("v", [EDGES_PAD, C], fp32).ap()
        self.tab2 = nc.dram_tensor("tab2", [NODES_PAD, 2 * C], fp32).ap()
        self.b_tab = nc.dram_tensor("b_tab", [NODES_PAD, C], fp32).ap()
        self.s2 = nc.dram_tensor("s2", [EDGES_PAD, 2 * C], fp32).ap()
        self.m2 = nc.dram_tensor("m2", [P * CHUNKS, U], fp32).ap()


class Resident:

    def __init__(self, sb):
        self.x = sb("x_sb", [P, NB, C])
        self.node_i = sb("node_i", [P, NB], i32)
        self.same = sb("same", [P, T])
        self.ident = sb("ident", [P, P])
        self.ident_i = sb("ident_i", [P, P], i32)
        self.node = sb("node", [P, NB])
        self.cnt = sb("cnt", [P, NB])
        self.start = sb("start", [P, NB])
        self.has = sb("has", [P, NB])
        self.tmp = sb("tmp", [P, NB])
        self.last_i = sb("last_i", [P, NB], i32)
        self.start_i = sb("start_i", [P, NB], i32)
        self.d0 = sb("d0", [P, 1])
        self.d0_t = sb("d0_t", [P, 1])
        self.d0_i = sb("d0_i", [P, 1], i32)
        self.d0_cnt = sb("d0_cnt", [P, 1])
        self.link = sb("link", [P, 1])
        self.pstart = sb("pstart", [P, 1])
        self.pstart_i = sb("pstart_i", [P, 1], i32)
        self.kstart = sb("kstart", [P, CHUNKS])
        self.kstart_i = sb("kstart_i", [P, CHUNKS], i32)
        self.slot = sb("slot", [P, K + 1])
        self.slot_i = sb("slot_i", [P, K + 1], i32)
        self.seg_t = sb("seg_t", [P, 1])
        self.seg_ok = sb("seg_ok", [P, 1])
        self.seg_read_i = sb("seg_read_i", [P, 1], i32)
        self.seg_write_i = sb("seg_write_i", [P, 1], i32)
        self.b_open = sb("b_open", [P, C])
        self.tail2 = sb("tail2", [P, 3, C])
        self.w1h = sb("w1h", [RBF, C])
        self.b1h = sb("b1h", [C, 1])
        self.w23 = sb("w23", [P, 2 * C])
        self.w1_raw = sb("w1_raw", [RBF, C])
        self.w2_raw = sb("w2_raw", [C, C])
        self.b1_raw = sb("b1_raw", [C, 1])
        self.b23_f = sb("b23_f", [3, 2 * C])
        self.b23_hi = sb("b23_hi", [3, 2 * C], bf16)
        self.b23_mid = sb("b23_mid", [3, 2 * C], bf16)
        self.b23_lo = sb("b23_lo", [3, 2 * C], bf16)
        self.b23_r = sb("b23_r", [3, 2 * C])
        self.b23_s = sb("b23_s", [3, 2 * C])
        self.bias_ones = sb("bias_ones", [3, P], bf16)
        self.bias_rows = sb("bias_rows", [3, GROUP * 2 * C], bf16)


class Early:

    def __init__(self, sb):
        self.dst_i = sb("dst_i", [P, T + 1], i32)
        self.dst_f = sb("dst_f", [P, T + 1])
        self.table_i = sb("table_i", [RP, RC + 1, ROW], i32)
        self.table = sb("table", [RP, RC, ROW + 1])
        self.table_hi = sb("table_hi", [RP, RC, ROW + 1], bf16)
        self.table_lo = sb("table_lo", [RP, RC, ROW + 1], bf16)
        self.table_first = sb("table_first", [RP, RC])
        self.table_row_i = sb("table_row_i", [RP, RC], i32)
        self.turn_i = sb("turn_i", [RP, WB, P], i32)
        self.turn_node = sb("turn_node", [RP, WB, P])
        self.search_node = sb("search_node", [P, WB])


def gnn_kernel(nc, x, src, dst_ext, dst_rows, rbf_t, ef_t, W1, b1, W2, b2, W3, b3, wlin_t, b_lin, wout_t,
               b_out, out):
    d = Dram(nc, x, src, dst_ext, dst_rows, rbf_t, ef_t, W1, b1, W2, b2, W3, b3, wlin_t, b_lin, wout_t, b_out, out)
    with ExitStack() as ctx:
        sb = lambda name, shape, dt=fp32: ctx.enter_context(nc.sbuf_tensor(name, shape, dt))
        s = Semaphores(lambda name: ctx.enter_context(nc.semaphore(name)))
        m = Resident(sb)
        with ExitStack() as early:
            m.early = Early(lambda name, shape, dt=fp32: early.enter_context(nc.sbuf_tensor(name, shape, dt)))
            setup_phase(nc, d, s, m)
            sum_phase(nc, d, s, m)
        node_phase(nc, d, s, m)
        softmax_phase(nc, d, s, m)
        end_phase(nc, d, s, m)


def kernel(x, src, dst, edge_attr_128, edge_attr_64, L0_gnn_W1, L0_gnn_b1, L0_gnn_W2, L0_gnn_b2, L0_gnn_W3,
           L0_gnn_b3, L1_gnn_W_lin, L1_gnn_b_lin, L1_gnn_W_out, L1_gnn_b_out):
    import numpy as np
    import concourse.bacc as bacc
    from concourse.bass_utils import run_bass_kernel_spmd

    def padded(a, rows, fill=0):
        a = np.asarray(a)
        return np.concatenate([a, np.full((rows - a.shape[0],) + a.shape[1:], fill, a.dtype)])

    def by_column(a):
        return np.ascontiguousarray(padded(a, EDGES_PAD).reshape(P, T, -1).transpose(2, 1, 0)).reshape(-1, T * P)

    dst_pad = padded(dst, EDGES_PAD, NODES)
    before = np.concatenate([np.full((1,), -1, dst_pad.dtype), dst_pad[:-1]])
    arrays = {
        "in_x": padded(x, NODES_PAD),
        "in_src": padded(src, EDGES_PAD),
        "in_dst_ext": np.concatenate([before.reshape(P, T)[:, :1], dst_pad.reshape(P, T)], axis=1),
        "in_dst_rows": dst_pad.reshape(ROWS, ROW),
        "in_rbf_t": by_column(edge_attr_128),
        "in_ef_t": by_column(edge_attr_64),
        "in_W1": np.asarray(L0_gnn_W1), "in_b1": np.asarray(L0_gnn_b1),
        "in_W2": np.asarray(L0_gnn_W2), "in_b2": np.asarray(L0_gnn_b2),
        "in_W3": np.asarray(L0_gnn_W3), "in_b3": np.asarray(L0_gnn_b3),
        "in_wlin_t": np.ascontiguousarray(np.asarray(L1_gnn_W_lin).T), "in_b_lin": np.asarray(L1_gnn_b_lin),
        "in_wout_t": np.ascontiguousarray(np.asarray(L1_gnn_W_out).T), "in_b_out": np.asarray(L1_gnn_b_out),
    }
    nc = bacc.Bacc("TRN2", target_bir_lowering=False, num_devices=1)
    args = [nc.dram_tensor(n, a.shape, mybir.dt.from_np(a.dtype), kind="ExternalInput").ap() for n, a in arrays.items()]
    args.append(nc.dram_tensor("out_x", (NODES_PAD, C), fp32, kind="ExternalOutput").ap())
    gnn_kernel(nc, *args)
    r = run_bass_kernel_spmd(nc, [arrays], core_ids=[0])
    return r.results[0]["out_x"][:NODES]
```

```python
import concourse.bass as bass
from concourse import mybir
from contextlib import ExitStack

P = 128
NODES, EDGES = 6250, 206250
C = 64
RBF = 128
K = 26
CHUNKS = 62
T = K * CHUNKS
EDGES_PAD = P * T
NB = 49
NODES_PAD = P * NB
GROUP = 4
GROUPS = -(-K // GROUP)
PAIR_G = 2 * GROUPS
ROW = 496
ROWS = EDGES_PAD // ROW
RC = 4
RP = ROWS // RC
WB = 7
TURNS = NB // WB
LAG = 6
SECTIONS = [(0, 12), (12, 24), (24, 36), (36, 44), (44, NB)]
SETUP_SECTIONS = [(0, 20), (20, 40), (40, NB)]
END_SECTIONS = [(0, 8), (8, 16), (16, 24), (24, 32), (32, 40), (40, 44), (44, 48), (48, NB)]
QUADS = [(b, min(b + 4, NB)) for b in range(0, NB, 4)]
SKIP = EDGES_PAD + 1
EPS = 1e-5
BANK = 512
assert EDGES <= EDGES_PAD and NODES < NODES_PAD and RP * RC * ROW == EDGES_PAD
assert 2 <= LAG < GROUPS
assert CHUNKS % 2 == 0 and ROW < BANK and TURNS * WB == NB and 2 * WB <= PAIR_G and TURNS + 1 < CHUNKS // 2 - 1

fp32 = mybir.dt.float32
bf16 = mybir.dt.bfloat16
i32 = mybir.dt.int32
ALU = mybir.AluOpType
ACT = mybir.ActivationFunctionType
AX = mybir.AxisListType


def section_of(b, sections=SECTIONS):
    return [b0 <= b < b1 for b0, b1 in sections].index(True)


class Chain:

    def __init__(self, eng, sem):
        self.eng, self.sem, self.n = eng, sem, 0

    def step(self, ins):
        self.n += 1
        ins.then_inc(self.sem, 1)
        return self.n

    def then_wait(self, ins):
        self.eng.wait_ge(self.sem, self.step(ins))


def ends_in(nc, ch, s, m, sel):
    for w in range(TURNS):
        ch.step(nc.vector.tensor_scalar(sel[:, w * WB:(w + 1) * WB, :], m.turn_node[:, :, :], float(w * WB), m.carried[:, 0:1],
                                        ALU.add, ALU.is_equal))


def quads_of(n, sections=SECTIONS):
    return [u for u, (b0, _) in enumerate(QUADS) if section_of(b0, sections) == n]


def size(j):
    return min(GROUP, K - j % GROUPS * GROUP)


def over_channels(ap, n=C):
    return ap.unsqueeze(1).to_broadcast([ap.shape[0], n, ap.shape[1]])


def over_last(ap, n=C):
    return ap.unsqueeze(2).to_broadcast([ap.shape[0], ap.shape[1], n])


def flat(ap):
    return ap.rearrange("p c t -> p (c t)")


def variance(nc, chain, act_asks, x, xc, sq, mean, var):
    chain.then_wait(nc.vector.tensor_reduce(mean, x, AX.X, ALU.add))
    chain.then_wait(nc.vector.tensor_scalar(mean, mean, 1.0 / C, None, ALU.mult))
    chain.then_wait(nc.vector.tensor_tensor(xc, x, over_last(mean), ALU.subtract))
    chain.then_wait(nc.vector.tensor_tensor(sq, xc, xc, ALU.mult))
    chain.then_wait(nc.vector.tensor_reduce(var, sq, AX.X, ALU.add))
    nc.vector.tensor_scalar(var, var, 1.0 / C, EPS, ALU.mult, ALU.add).then_inc(act_asks, 1)


def relu_of_norm(nc, chain, act_answers, asked, out, xc, var):
    chain.eng.wait_ge(act_answers, asked)
    chain.then_wait(nc.vector.reciprocal(var, var))
    return nc.vector.scalar_tensor_tensor(out, xc, 0.0, over_last(var), ALU.max, ALU.mult)


def setup_phase(nc, d, s, m):
    with ExitStack() as ctx:
        sb = lambda name, shape, dt=fp32: ctx.enter_context(nc.sbuf_tensor(name, shape, dt))
        h1 = sb("h1", [P, NB, C])
        xc, sq = sb("xc1", [P, NB, C]), sb("sq1", [P, NB, C])
        stat = sb("stat1", [P, 2 * NB])
        block = ctx.enter_context(nc.Block())

        @block.sync
        def _(sp):
            x_rows = d.x.rearrange("(p b) c -> p b c", b=NB)
            for n, (b0, b1) in enumerate(SETUP_SECTIONS):
                sp.dma_start(m.x[:, b0:b1, :], x_rows[:, b0:b1, :]).then_inc(s.x_in[n], 16)
            sp.dma_start(m.early.dst_i[:, :], d.dst_ext).then_inc(s.dst_in, 16)
            table = d.dst_rows.rearrange("(p c) w -> p c w", c=RC)
            sp.dma_start(m.early.table_i[:, 1:, :], table).then_inc(s.table_in, 16)
            sp.dma_start(m.early.table_i[1:RP, 0, :], table[0:RP - 1, RC - 1, :]).then_inc(s.table_in, 16)
            sp.wait_ge(s.w23_zero, 1)
            sp.dma_start(m.w23[C:2 * C, C:2 * C], d.W3).then_inc(s.w3_in, 16)
            h1_rows = d.h1_tab.rearrange("(p b) c -> p b c", b=NB)
            for n, (b0, b1) in enumerate(SETUP_SECTIONS):
                sp.wait_ge(s.h1_ready, n + 1)
                sp.dma_start(h1_rows[:, b0:b1, :], h1[:, b0:b1, :]).then_inc(s.h1_stored, 16)
            sp.wait_ge(s.h1_stored, 16 * len(SETUP_SECTIONS))

        @block.gpsimd
        def _(pool):
            nc.gpsimd.iota(m.node_i[:, :], [[1, NB]], base=0, channel_multiplier=NB).then_inc(s.iota_ready, 1)
            nc.gpsimd.iota(m.ident_i[:, :], [[1, P]], base=0, channel_multiplier=-1).then_inc(s.iota_ready, 1)
            nc.gpsimd.iota(m.early.turn_i[:, :, :], [[1, WB], [NB, P]], base=0, channel_multiplier=0).then_inc(s.iota_ready, 1)
            nc.gpsimd.iota(m.early.table_row_i[:, :], [[1, RC]], base=0, channel_multiplier=RC).then_inc(s.iota_ready, 1)

        @block.scalar
        def _(act):
            act.dma_start(m.w1_raw[:, :], d.W1).then_inc(s.w_in, 16)
            act.dma_start(m.w2_raw[:, :], d.W2).then_inc(s.w_in, 16)
            act.dma_start(m.b1_raw[:, :], d.b1.rearrange("(c o) -> c o", o=1)).then_inc(s.w_in, 16)
            act.dma_start(m.b23_f[:, 0:C], d.b2.unsqueeze(0).to_broadcast([3, C])).then_inc(s.w_in, 16)
            act.dma_start(m.b23_f[:, C:2 * C], d.b3.unsqueeze(0).to_broadcast([3, C])).then_inc(s.w_in, 16)
            def square(n):
                b0, b1 = SETUP_SECTIONS[n]
                act.wait_ge(s.xc1_ready, n + 1)
                nc.scalar.activation(sq[:, b0:b1, :], xc[:, b0:b1, :], ACT.Square).then_inc(s.sq1_ready, 1)

            square(0)
            for n, (b0, b1) in enumerate(SETUP_SECTIONS):
                if n + 1 < len(SETUP_SECTIONS):
                    square(n + 1)
                act.wait_ge(s.var1_ready, n + 1)
                nc.scalar.activation(stat[:, NB + b0:NB + b1], stat[:, NB + b0:NB + b1], ACT.Sqrt).then_inc(s.std1_ready, 1)

        @block.vector
        def _(dve):
            ch = Chain(dve, s.setup_dve)
            nc.vector.memset(m.w23[:, :], 0.0).then_inc(s.w23_zero, 1)
            ch.step(nc.vector.memset(m.early.table_i[0:1, 0, :], 0))

            def centre(n):
                b0, b1 = SETUP_SECTIONS[n]
                mean = stat[:, b0:b1]
                dve.wait_ge(s.x_in[n], 16)
                ch.then_wait(nc.vector.tensor_reduce(mean, m.x[:, b0:b1, :], AX.X, ALU.add))
                ch.then_wait(nc.vector.tensor_scalar(mean, mean, 1.0 / C, None, ALU.mult))
                nc.vector.tensor_tensor(xc[:, b0:b1, :], m.x[:, b0:b1, :], over_last(mean), ALU.subtract).then_inc(s.xc1_ready, 1)

            def spread(n):
                b0, b1 = SETUP_SECTIONS[n]
                var = stat[:, NB + b0:NB + b1]
                dve.wait_ge(s.sq1_ready, n + 1)
                ch.then_wait(nc.vector.tensor_reduce(var, sq[:, b0:b1, :], AX.X, ALU.add))
                nc.vector.tensor_scalar(var, var, 1.0 / C, EPS, ALU.mult, ALU.add).then_inc(s.var1_ready, 1)

            def finish(n):
                b0, b1 = SETUP_SECTIONS[n]
                relu_of_norm(nc, ch, s.std1_ready, n + 1, h1[:, b0:b1, :], xc[:, b0:b1, :], stat[:, NB + b0:NB + b1]).then_inc(s.h1_ready, 1)

            centre(0)
            centre(1)
            spread(0)
            centre(2)
            finish(0)
            spread(1)
            finish(1)
            spread(2)
            finish(2)


def prepare(nc, dve, s, m):
    ch = Chain(dve, s.prepare_dve)
    dve.wait_ge(s.iota_ready, 4)
    ch.step(nc.vector.tensor_copy(m.node[:, :], m.node_i[:, :]))
    ch.step(nc.vector.tensor_scalar(m.ident[:, :], m.ident_i[:, :], 0.0, None, ALU.is_equal))
    ch.step(nc.vector.memset(m.bias_ones[:, :], 1.0))
    dve.wait_ge(s.dst_in, 16)
    ch.then_wait(nc.vector.tensor_copy(m.early.dst_f[:, :], m.early.dst_i[:, :]))
    ch.then_wait(nc.vector.tensor_tensor(m.same[:, :], m.early.dst_f[:, 1:T + 1], m.early.dst_f[:, 0:T], ALU.is_equal))
    ch.step(nc.vector.tensor_copy(m.d0[:, :], m.early.dst_f[:, 1:2]))
    ch.step(nc.vector.tensor_copy(m.d0_i[:, :], m.early.dst_i[:, 1:2]))
    ch.then_wait(nc.vector.tensor_tensor(m.link[:, :], m.early.dst_f[:, 1:2], m.early.dst_f[:, T:T + 1], ALU.is_equal))
    ch.then_wait(nc.vector.tensor_tensor(m.link[:, :], m.link[:, :], m.same[:, 0:1], ALU.mult))
    dve.wait_ge(s.w_in, 80)
    ch.step(nc.vector.tensor_scalar(m.w1h[:, :], m.w1_raw[:, :], 0.5, None, ALU.mult))
    ch.step(nc.vector.tensor_scalar(m.b1h[:, :], m.b1_raw[:, :], 0.5, None, ALU.mult))
    dve.wait_ge(s.w3_in, 16)
    ch.step(nc.vector.tensor_scalar(m.w23[0:C, 0:C], m.w2_raw[:, :], 2.0, None, ALU.mult))
    ch.then_wait(nc.vector.tensor_copy(m.b23_hi[:, :], m.b23_f[:, :]))
    ch.then_wait(nc.vector.tensor_tensor(m.b23_r[:, :], m.b23_f[:, :], m.b23_hi[:, :], ALU.subtract))
    ch.then_wait(nc.vector.tensor_copy(m.b23_mid[:, :], m.b23_r[:, :]))
    ch.then_wait(nc.vector.tensor_tensor(m.b23_r[:, :], m.b23_r[:, :], m.b23_mid[:, :], ALU.subtract))
    ch.then_wait(nc.vector.tensor_copy(m.b23_lo[:, :], m.b23_r[:, :]))
    ch.then_wait(nc.vector.tensor_scalar(m.b23_s[:, :], m.b23_hi[:, :], m.ident[0:3, 0:1], None, ALU.mult))
    for part, r in ((m.b23_mid, 1), (m.b23_lo, 2)):
        ch.then_wait(nc.vector.scalar_tensor_tensor(m.b23_s[:, :], part[:, :], m.ident[0:3, r:r + 1], m.b23_s[:, :],
                                                    ALU.mult, ALU.add))
    for j in range(GROUP):
        ch.step(nc.vector.tensor_copy(m.bias_rows[:, j * 2 * C:(j + 1) * 2 * C], m.b23_s[:, :]))
    dve.wait_ge(s.prepare_dve, ch.n)
    nc.vector.tensor_scalar(m.first[:, :], m.early.dst_f[:, 1:T + 1], m.d0[:, 0:1], None, ALU.is_equal).then_inc(s.prepared, 1)
    ends = m.early.ends[:, :]
    ch.then_wait(nc.vector.tensor_tensor(ends, m.early.dst_f[:, T + 1:T + 2], m.d0[:, :], ALU.not_equal))
    ch.then_wait(nc.vector.tensor_tensor(ends, ends, m.same[:, 0:1], ALU.mult))
    ch.then_wait(nc.vector.scalar_tensor_tensor(m.carried[:, :], m.d0[:, :], 1.0, ends, ALU.add, ALU.mult))
    ch.then_wait(nc.vector.tensor_scalar(m.carried[:, :], m.carried[:, :], -1.0, None, ALU.add))

def search_table(nc, dve, s, m):
    ch = Chain(dve, s.table_dve)
    dve.wait_ge(s.table_in, 32)
    row_c = m.early.table[:, :, ROW:ROW + 1].rearrange("p c o -> p (c o)")
    ch.step(nc.vector.tensor_tensor(m.early.table[:, :, 0:ROW], m.early.table_i[:, 1:, :], m.early.table_i[:, 0:RC, :], ALU.subtract))
    ch.step(nc.vector.tensor_copy(m.early.table_first[:, :], m.early.table_i[:, 1:, 0]))
    ch.step(nc.vector.tensor_copy(m.turn_node[:, :, :], m.early.turn_i[:, :, :]))
    ch.step(nc.vector.tensor_copy(m.early.search_node[:, :], m.node[:, 0:WB]))
    ch.then_wait(nc.vector.tensor_scalar(row_c, m.early.table_row_i[:, :], 0.0, None, ALU.is_gt))
    ch.then_wait(nc.vector.tensor_tensor(m.early.table_first[:, :], m.early.table_first[:, :], row_c, ALU.mult))
    ch.then_wait(nc.vector.tensor_copy(m.early.table_hi[:, :, :], m.early.table[:, :, :]))
    ch.then_wait(nc.vector.tensor_tensor(m.early.table[:, :, :], m.early.table[:, :, :], m.early.table_hi[:, :, :], ALU.subtract))
    nc.vector.tensor_copy(m.early.table_lo[:, :, :], m.early.table[:, :, :]).then_inc(s.table_ready, 1)


def sum_phase(nc, d, s, m):
    with ExitStack() as ctx:
        sb = lambda name, shape, dt=fp32: ctx.enter_context(nc.sbuf_tensor(name, shape, dt))
        pb = lambda name, shape: ctx.enter_context(nc.psum_tensor(name, shape, fp32))
        GC = GROUP * P
        KP = K * P
        rbf = [sb(f"rbf{q}", [P, KP]) for q in range(2)]
        spef = [sb(f"spef{q}", [P, KP]) for q in range(2)]
        rows = sb("rows1", [P, K, C])
        g = [sb(f"h_src{q}", [P, K, C]) for q in range(2)]
        idx = [sb(f"idx1_{q}", [P, K], i32) for q in range(2)]
        mask = [sb(f"mask1_{q}", [P, C, K + 1]) for q in range(2)]
        msg = sb("msg", [P, C, K + 1])
        run = sb("run", [P, C, K + 1])
        zeros = sb("zeros", [P, K // 2 * C])
        zc = [sb(f"zc{q}", [C, GC]) for q in range(2)]
        lg = [sb(f"lg{q}", [C, GC]) for q in range(2)]
        below = sb("below", [RP, RC, WB * P], bf16)
        found_row, found_cnt = sb("found_row", [P, WB]), sb("found_cnt", [P, WB])
        hit = sb("hit", [P, ROW])
        found = [pb(f"found{q}", [P, BANK]) for q in range(2)]
        z = [pb(f"z{q}", [C, GC]) for q in range(2)]
        hw = [pb(f"hw{q}", [P, GROUP, 2 * C]) for q in range(2)]
        turned = pb("turned1", [C, BANK])
        tail_ps, link_ps = turned[:, 0:P], turned[:, P:2 * P]
        carry_ps = pb("carry_ps", [P, BANK])[:, 0:C]
        tail_t = sb("tail_t", [C, P])
        link_t = sb("link_t", [C, P])
        open_t = sb("open_t", [C, P + 1])
        tail = sb("tail1", [P, C])
        block = ctx.enter_context(nc.Block())
        s1_rows = d.s1.rearrange("(p t) c -> p t c", t=T)
        v_halves = d.v.rearrange("(p j t) c -> p j (t c)", j=2 * CHUNKS, t=K // 2)

        @block.sync
        def _(sp):
            def load_edges(i, q, first):
                k = i * 2 + q
                if not first:
                    sp.wait_ge(s.z_ready, i * PAIR_G + (q - 1) * GROUPS)
                sp.dma_start(rbf[q][:, :], d.rbf_t[:, bass.ds(k * KP, KP)]).then_inc(s.rbf_in[q], 16)
                if not first:
                    sp.wait_ge(s.hw_ready, i * PAIR_G + (q - 1) * GROUPS)
                sp.dma_start(spef[q][C:2 * C, :], d.ef_t[:, bass.ds(k * KP, KP)]).then_inc(s.ef_in[q], 16)
                sp.dma_start(v_halves[:, bass.ds(k * 2, 2), :],
                             zeros[:, :].unsqueeze(1).to_broadcast([P, 2, K // 2 * C])).then_inc(s.v_zeroed, 16)

            def load_sources(i, q, first):
                if not first:
                    sp.wait_ge(s.gather1_in[q], 16 * K * i)
                sp.dma_start(idx[q][:, :], d.src_rows[:, bass.ds((i * 2 + q) * K, K)]).then_inc(s.idx1_in[q], 16)

            def store(k):
                sp.wait_ge(s.rows1_ready, k + 1)
                sp.dma_start(s1_rows[:, bass.ds(k * K, K), :], rows[:, :, :]).then_inc(s.rows1_stored, 16)

            load_sources(0, 0, True)
            load_sources(0, 1, True)
            sp.wait_ge(s.zeros_ready, 1)
            load_edges(0, 0, True)
            load_edges(0, 1, True)
            load_sources(1, 0, False)
            with sp.Fori(1, CHUNKS // 2 - 1) as i:
                load_edges(i, 0, False)
                store(i * 2 - 2)
                load_sources(i, 1, False)
                load_edges(i, 1, False)
                store(i * 2 - 1)
                load_sources(i + 1, 0, False)
            i = CHUNKS // 2 - 1
            load_edges(i, 0, False)
            store(i * 2 - 2)
            load_sources(i, 1, False)
            load_edges(i, 1, False)
            store(i * 2 - 1)
            store(i * 2)
            store(i * 2 + 1)
            sp.wait_ge(s.rows1_stored, 16 * CHUNKS)
            sp.wait_ge(s.v_zeroed, 16 * CHUNKS)

        @block.gpsimd
        def _(pool):
            def gather(i, q, first, last=False):
                if not first:
                    pool.wait_ge(s.msg_ready, i * PAIR_G + (q - 1) * GROUPS)
                pool.wait_ge(s.idx1_in[q], 16 * (i + 1))
                pool.sem_inc(s.idx1_seen, 1)
                for t in range(K):
                    arrived = s.last_in[t // GROUP] if last else s.gather1_in[q]
                    nc.gpsimd.indirect_dma_start(g[q][:, t, :], None, d.h1_tab,
                                                 bass.IndirectOffsetOnAxis(idx[q][:, t:t + 1], 0)).then_inc(arrived, 16)

            gather(0, 0, True)
            gather(0, 1, True)
            with pool.Fori(1, CHUNKS // 2 - 1) as i:
                gather(i, 0, False)
                gather(i, 1, False)
            gather(CHUNKS // 2 - 1, 0, False)
            gather(CHUNKS // 2 - 1, 1, False, last=True)

        @block.tensor
        def _(pe):
            def hidden(i, j, first):
                q, gi = j // GROUPS % 2, i * PAIR_G + j
                if j % GROUPS == 0:
                    pe.wait_ge(s.rbf_in[q], 16 * (i + 1))
                if not (first and j < 2):
                    pe.wait_ge(s.sp_ready, gi - 1)
                col, n = (j % GROUPS) * GC, size(j) * P
                nc.tensor.matmul(z[j % 2][:, 0:n], m.w1h[:, :], rbf[q][:, col:col + n], start=True, stop=True).then_inc(s.z_ready, 1)

            def messages(i, j, first):
                q, gi = j // GROUPS % 2, i * PAIR_G + j
                if j % GROUPS == 0:
                    pe.wait_ge(s.ef_in[q], 16 * (i + 1))
                pe.wait_ge(s.sp_ready, gi + 1)
                if not (first and j < 2):
                    pe.wait_ge(s.msg_ready, gi - 1)
                out = hw[j % 2]
                n = size(j)
                for t in range(n):
                    col = (j % GROUPS) * GC + t * P
                    nc.tensor.matmul(out[:, t, :], spef[q][:, col:col + P], m.w23[:, :], start=(t == 0), stop=False,
                                     skip_group_check=True)
                nc.tensor.matmul(out[:, 0:n, :].rearrange("p t c -> p (t c)"), m.bias_ones[:, :], m.bias_rows[:, 0:n * 2 * C],
                                 start=False, stop=True, skip_group_check=True).then_inc(s.hw_ready, 1)

            def search(w, b, first):
                if b == 0:
                    pe.wait_ge(s.below_ready, RC * (w + 1))
                if not (first and b < 2):
                    pe.wait_ge(s.found_used, w * 2 * WB + 2 * (b - 1))
                for c in range(RC):
                    for part in (m.early.table_hi, m.early.table_lo):
                        last = nc.tensor.matmul(found[b % 2][:, 0:ROW + 1], below[:, c, b * P:(b + 1) * P], part[:, c, :],
                                                start=(c == 0 and part is m.early.table_hi), stop=(c == RC - 1 and part is m.early.table_lo))
                last.then_inc(s.found_ready[b % 2], 1)

            def pair(i, first, searching=False, first_turn=False):
                for j in range(PAIR_G):
                    hidden(i, j, first)
                    if j >= LAG - 1:
                        messages(i, j - LAG + 1, first)
                    elif not first:
                        messages(i - 1, j - LAG + 1 + PAIR_G, False)
                    if searching and j % 2 == 0:
                        search(i - 1, j // 2, first_turn)

            pe.wait_ge(s.prepared, 1)
            pair(0, True)
            pe.wait_ge(s.table_ready, 1)
            pair(1, False, searching=True, first_turn=True)
            with pe.Fori(2, TURNS + 1) as i:
                pair(i, False, searching=True)
            with pe.Fori(TURNS + 1, CHUNKS // 2) as i:
                pair(i, False)
            for j in range(PAIR_G - LAG + 1, PAIR_G):
                messages(CHUNKS // 2 - 1, j, False)
            pe.wait_ge(s.tail1_ready, 1)
            nc.tensor.transpose(tail_ps, tail[:, :], m.ident[:, :])
            nc.tensor.transpose(link_ps, m.link[:, 0:1].to_broadcast([P, C]), m.ident[:, :]).then_inc(s.tail1_turned, 1)
            pe.wait_ge(s.open1_ready, 1)
            nc.tensor.transpose(carry_ps[:, :], open_t[:, 0:P], m.ident[0:C, 0:C]).then_inc(s.carry1_ready, 1)

        @block.scalar
        def _(act):
            def softplus(i, j):
                gi = i * PAIR_G + j
                act.wait_ge(s.z_clamped, gi + 1)
                n = size(j) * P
                nc.scalar.activation(lg[j % 2][:, 0:n], zc[j % 2][:, 0:n], ACT.Exp).then_inc(s.exp_ready, 1)
                act.wait_ge(s.exp_ready, gi + 1)
                nc.scalar.activation(lg[j % 2][:, 0:n], lg[j % 2][:, 0:n], ACT.Ln, bias=1.0).then_inc(s.log_ready, 1)

            def spread_mask(k, q, first):
                if not first:
                    act.wait_ge(s.scan1_ready, k - 1)
                nc.scalar.copy(mask[q][:, :, 1:], over_channels(m.same[:, bass.ds(k * K, K)])).then_inc(s.mask1_ready, 1)

            def to_rows(k, first):
                act.wait_ge(s.scan1_ready, k + 1)
                if not first:
                    act.wait_ge(s.rows1_stored, 16 * k)
                nc.scalar.copy(rows[:, :, :], run[:, :, 1:].rearrange("p c t -> p t c")).then_inc(s.rows1_ready, 1)

            def pair(i, first, last):
                for j in range(PAIR_G):
                    softplus(i, j)
                    q = j // GROUPS
                    if j % GROUPS == LAG - 1 and not (first and q == 0):
                        to_rows(i * 2 + q - 1, first)
                    if j == LAG:
                        spread_mask(i * 2 + 1, 1, first)
                    if j == GROUPS + LAG and not last:
                        spread_mask(i * 2 + 2, 0, False)

            nc.scalar.preload_act_table_set("natural_log_exp_and_others")
            act.wait_ge(s.prepared, 1)
            act.wait_ge(s.mask1_zero, 2)
            spread_mask(0, 0, True)
            pair(0, True, False)
            with act.Fori(1, TURNS + 1) as i:
                pair(i, False, False)
            act.wait_ge(s.cnt_ready, TURNS)
            act.dma_start(d.cnt_tab[1:1 + NODES_PAD, :].rearrange("(p b) o -> p (b o)", b=NB), m.cnt[:, :]).then_inc(s.cnt_stored, 16)
            act.dma_start(d.cnt_tab[0:1, :], zeros[0:1, 0:1]).then_inc(s.cnt_stored, 16)
            act.wait_ge(s.cnt_stored, 32)
            act.dma_start(m.start[:, :], d.cnt_tab[0:NODES_PAD, :].rearrange("(p b) o -> p (b o)", b=NB)).then_inc(s.start_in, 16)
            with act.Fori(TURNS + 1, CHUNKS // 2 - 1) as i:
                pair(i, False, False)
            pair(CHUNKS // 2 - 1, False, True)
            to_rows(CHUNKS - 1, False)

        @block.vector
        def _(dve):
            ch = Chain(dve, s.sum_dve)
            nc.vector.memset(zeros[:, :], 0.0).then_inc(s.zeros_ready, 1)
            nc.vector.memset(mask[0][:, :, 0:1], 0.0).then_inc(s.mask1_zero, 1)
            nc.vector.memset(mask[1][:, :, 0:1], 0.0).then_inc(s.mask1_zero, 1)
            ch.step(nc.vector.memset(run[:, :, K:K + 1], 0.0))
            ch.step(nc.vector.memset(open_t[:, :], 0.0))
            prepare(nc, dve, s, m)

            def below_nodes(w, first):
                if not first:
                    for q in range(2):
                        dve.wait_ge(s.found_ready[q], w * ((WB + 1 - q) // 2))
                    nc.vector.tensor_scalar(m.early.table_first[:, :], m.early.table_first[:, :], float(-WB), None, ALU.add).then_inc(s.turn_moved, 1)
                    nc.vector.tensor_scalar(m.early.search_node[:, :], m.early.search_node[:, :], float(WB), None, ALU.add).then_inc(s.turn_moved, 1)
                    dve.wait_ge(s.turn_moved, w * 2)
                for c in range(RC):
                    nc.vector.tensor_scalar(below[:, c, :], m.turn_node[0:RP, :, :].rearrange("p b n -> p (b n)"),
                                            m.early.table_first[:, c:c + 1], None, ALU.is_ge).then_inc(s.below_ready, 1)

            def count_edges(w, b):
                dve.wait_ge(s.found_ready[b % 2], w * ((WB + 1 - b % 2) // 2) + b // 2 + 1)
                nc.vector.tensor_copy(found_row[:, b:b + 1], found[b % 2][:, ROW:ROW + 1]).then_inc(s.found_used, 1)
                nc.vector.tensor_scalar(hit[:, :], found[b % 2][:, 0:ROW], m.early.search_node[:, b:b + 1], 0.0, ALU.is_le, ALU.add,
                                        accum_out=found_cnt[:, b:b + 1]).then_inc(s.found_used, 1)
                if b == WB - 1:
                    dve.wait_ge(s.found_used, (w + 1) * 2 * WB)
                    nc.vector.scalar_tensor_tensor(m.cnt[:, bass.ds(w * WB, WB)], found_row[:, :], float(ROW), found_cnt[:, :],
                                                   ALU.mult, ALU.add).then_inc(s.cnt_ready, 1)
                    dve.wait_ge(s.cnt_ready, w + 1)

            def node_indices():
                dve.wait_ge(s.cnt_ready, TURNS)
                dve.wait_ge(s.start_in, 16)
                ch.then_wait(nc.vector.tensor_tensor(m.has[:, :], m.cnt[:, :], m.start[:, :], ALU.is_gt))
                ch.then_wait(nc.vector.tensor_scalar(m.tmp[:, :], m.cnt[:, :], -1.0, 0.0, ALU.add, ALU.max))
                ch.then_wait(nc.vector.tensor_copy(m.last_i[:, :], m.tmp[:, :]))
                ch.then_wait(nc.vector.scalar_tensor_tensor(m.tmp[:, :], m.start[:, :], float(-SKIP), m.has[:, :], ALU.add, ALU.mult))
                ch.then_wait(nc.vector.tensor_scalar(m.tmp[:, :], m.tmp[:, :], float(SKIP), None, ALU.add))
                ch.then_wait(nc.vector.tensor_copy(m.start_i[:, :], m.tmp[:, :]))

            def clamp(i, j):
                gi = i * PAIR_G + j
                dve.wait_ge(s.z_ready, gi + 1)
                n = size(j) * P
                nc.vector.tensor_scalar(zc[j % 2][:, 0:n], z[j % 2][:, 0:n], m.b1h[:, 0:1], 14.0, ALU.add, ALU.min).then_inc(s.z_clamped, 1)

            def softplus_max(i, j, first):
                q, gi = j // GROUPS % 2, i * PAIR_G + j
                if j % GROUPS == 0 and not first:
                    dve.wait_ge(s.hw_ready, i * PAIR_G + (q - 1) * GROUPS)
                dve.wait_ge(s.log_ready, gi + 1)
                col, n = (j % GROUPS) * GC, size(j) * P
                nc.vector.scalar_tensor_tensor(spef[q][0:C, col:col + n], z[j % 2][:, 0:n], m.b1h[:, 0:1], lg[j % 2][:, 0:n],
                                               ALU.add, ALU.max).then_inc(s.sp_ready, 1)

            def message(i, j, first, last=False):
                q, gi = j // GROUPS % 2, i * PAIR_G + j
                t0 = (j % GROUPS) * GROUP
                if last:
                    dve.wait_ge(s.last_in[j % GROUPS], 16 * size(j))
                elif j % GROUPS == 0:
                    dve.wait_ge(s.gather1_in[q], 16 * K * (i + 1))
                dve.wait_ge(s.hw_ready, gi + 1)
                t1 = t0 + size(j)
                out = msg[:, :, 1 + t0:1 + t1]
                nc.vector.tensor_tensor(out, g[q][:, t0:t1, :].rearrange("p t c -> p c t"),
                                        hw[j % 2][:, 0:t1 - t0, 0:C].rearrange("p t c -> p c t"), ALU.mult).then_inc(s.msg_scaled, 1)
                dve.wait_ge(s.msg_scaled, gi + 1)
                nc.vector.tensor_tensor(out, out, hw[j % 2][:, 0:t1 - t0, C:2 * C].rearrange("p t c -> p c t"), ALU.add).then_inc(s.msg_ready, 1)
                if j % GROUPS == GROUPS - 1:
                    k = i * 2 + q
                    nc.vector.tensor_copy(msg[:, :, 0:1], run[:, :, K:K + 1]).then_inc(s.carry1_in, 1)
                    dve.wait_ge(s.carry1_in, k + 1)
                    dve.wait_ge(s.msg_ready, gi + 1)
                    dve.wait_ge(s.mask1_ready, k + 1)
                    if not first or q:
                        dve.wait_ge(s.rows1_ready, k)
                    nc.vector.tensor_tensor_scan(flat(run[:, :, :]), flat(mask[q][:, :, :]), flat(msg[:, :, :]), 0.0,
                                                 ALU.mult, ALU.add).then_inc(s.scan1_ready, 1)
                    dve.wait_ge(s.scan1_ready, k + 1)

            def pair(i, first, searching=False, first_turn=False, last=False):
                for j in range(PAIR_G):
                    if searching and j == 0:
                        below_nodes(i - 1, first_turn)
                    clamp(i, j)
                    if searching and j % 2 == 0 and 0 < j // 2 <= WB:
                        count_edges(i - 1, j // 2 - 1)
                    if j >= 1:
                        softplus_max(i, j - 1, first)
                    elif not first:
                        softplus_max(i - 1, PAIR_G - 1, False)
                    if j >= LAG:
                        message(i, j - LAG, first, last and j - LAG >= GROUPS)
                    elif not first:
                        message(i - 1, j - LAG + PAIR_G, False)
                if searching:
                    for b in range((PAIR_G + 1) // 2 - 1, WB):
                        count_edges(i - 1, b)

            pair(0, True)
            search_table(nc, dve, s, m)
            pair(1, False, searching=True, first_turn=True)
            with dve.Fori(2, TURNS + 1) as i:
                pair(i, False, searching=True)
            with dve.Fori(TURNS + 1, CHUNKS // 2 - 1) as i:
                pair(i, False)
            node_indices()
            i = CHUNKS // 2 - 1
            pair(i, False, last=True)
            softplus_max(i, PAIR_G - 1, False)
            for j in range(PAIR_G - LAG, PAIR_G):
                message(i, j, False, last=True)

            nc.vector.tensor_copy(tail[:, :], run[:, :, K]).then_inc(s.tail1_ready, 1)
            dve.wait_ge(s.tail1_turned, 1)
            ch.then_wait(nc.vector.tensor_copy(tail_t[:, :], tail_ps))
            ch.then_wait(nc.vector.tensor_copy(link_t[:, :], link_ps))
            ch.step(nc.vector.memset(m.carry1[:, C:C + 1], 1.0))
            nc.vector.tensor_tensor_scan(open_t[:, 1:P + 1], link_t[:, :], tail_t[:, :], 0.0, ALU.mult, ALU.add).then_inc(s.open1_ready, 1)
            dve.wait_ge(s.carry1_ready, 1)
            ch.step(nc.vector.tensor_copy(m.carry1[:, 0:C], carry_ps[:, :]))
            dve.wait_ge(s.sum_dve, ch.n)


def node_phase(nc, d, s, m):
    with ExitStack() as ctx:
        sb = lambda name, shape, dt=fp32: ctx.enter_context(nc.sbuf_tensor(name, shape, dt))
        pb = lambda name, shape: ctx.enter_context(nc.psum_tensor(name, shape, fp32))
        agg = sb("agg", [P, NB, C])
        tab = sb("tab", [P, NB, 2 * C])
        h2 = sb("h2", [P, NB, C])
        bd = sb("bd", [P, NB, C])
        xc = sb("xc2", [P, NB, C])
        stat = sb("stat2", [P, 2 * NB])
        wab = sb("wab", [C + 1, 2 * C])
        h2t = [sb(f"h2t{q}", [C + 1, 4 * P]) for q in range(2)]
        turn = [pb(f"turn{q}", [C, BANK]) for q in range(2)]
        ab = [pb(f"ab{q}", [P, BANK]) for q in range(2)]
        car = [pb(f"car{q}", [P, BANK]) for q in range(2)]
        ends = sb("ends_in", [P, NB, P])
        ho = sb("ho", [P, NB, C])
        wo2 = sb("wo2", [C, C])
        block = ctx.enter_context(nc.Block())
        ring = [car[0], car[1], ab[0], ab[1]]

        @block.gpsimd
        def _(pool):
            for n, (b0, b1) in enumerate(SECTIONS):
                for b in range(b0, b1):
                    nc.gpsimd.indirect_dma_start(agg[:, b, :], None, d.s1,
                                                 bass.IndirectOffsetOnAxis(m.last_i[:, b:b + 1], 0)).then_inc(s.agg_in[n], 16)
            for u, (b0, b1) in enumerate(QUADS):
                pool.wait_ge(s.ab_out, u + 1)
                for b in range(b0, b1):
                    nc.gpsimd.indirect_dma_start(d.v, bass.IndirectOffsetOnAxis(m.start_i[:, b:b + 1], 0), bd[:, b, :], None,
                                                 bounds_check=EDGES_PAD - 1, oob_is_err=False).then_inc(s.v_stored, 16)
            pool.wait_ge(s.v_stored, 16 * NB)

        @block.sync
        def _(sp):
            sp.dma_start(wab[0:C, 0:C], d.wlin_t[0:C, 0:C]).then_inc(s.wab_in, 16)
            sp.dma_start(wab[0:C, C:2 * C], d.wlin_t[C:2 * C, 0:C]).then_inc(s.wab_in, 16)
            sp.wait_ge(s.wab_zero, 1)
            sp.dma_start(wab[C:C + 1, C:2 * C], d.b_lin[0:C].unsqueeze(0)).then_inc(s.wab_in, 16)
            sp.dma_start(wo2[:, :], d.wout_t[C:2 * C, :]).then_inc(s.wab_in, 16)
            sp.dma_start(m.bo[:, :], d.b_out.unsqueeze(0).to_broadcast([P, C])).then_inc(s.bo_in, 16)
            for n, (b0, b1) in enumerate(SECTIONS):
                sp.wait_ge(s.ab_out, [c0 < b1 <= c1 for c0, c1 in QUADS].index(True) + 1)
                sp.wait_ge(s.tab_h2, n + 1)
                sp.dma_start(d.tab2.rearrange("(p b) c -> p b c", b=NB)[:, b0:b1, :], tab[:, b0:b1, :]).then_inc(s.tab_stored, 16)
            for q in range(2):
                sp.dma_start(m.idx2[q][:, :], d.src_rows[:, q * K:(q + 1) * K]).then_inc(s.idx2_in[q], 16)
            sp.wait_ge(s.tab_stored, 16 * len(SECTIONS))

        @block.scalar
        def _(act):
            def output_half(u):
                c0, c1 = QUADS[u]
                act.wait_ge(s.ho_ready, u + 1)
                for b in range(c0, c1):
                    last = nc.scalar.activation(ho[:, b, :], car[u % 2][:, (b - c0) * C:(b - c0 + 1) * C], ACT.Copy, scale=m.has[:, b:b + 1])
                last.then_inc(s.ho_out, 1)

            act.wait_ge(s.h2t_ones, 2)
            u = 0
            for n, (b0, b1) in enumerate(SECTIONS):
                act.wait_ge(s.var2_ready, n + 1)
                nc.scalar.activation(stat[:, NB + b0:NB + b1], stat[:, NB + b0:NB + b1], ACT.Sqrt).then_inc(s.std2_ready, 1)
                act.wait_ge(s.h2_ready, n + 1)
                nc.scalar.copy(tab[:, b0:b1, C:2 * C], h2[:, b0:b1, :]).then_inc(s.tab_h2, 1)
                while u < len(QUADS) and QUADS[u][1] <= b1:
                    w = (QUADS[u][1] - QUADS[u][0]) * P
                    act.wait_ge(s.turned2, u + 1)
                    if u >= 2:
                        act.wait_ge(s.ho_ready, u - 1)
                    nc.scalar.copy(h2t[u % 2][0:C, 0:w], turn[u % 2][:, 0:w]).then_inc(s.h2t_ready, 1)
                    if QUADS[u][0] > b0:
                        output_half(u - 1)
                    if QUADS[u][1] == b1:
                        output_half(u)
                    u += 1

        @block.tensor
        def _(pe):
            pe.wait_ge(s.wab_in, 64)

            def turn_quad(u):
                b0, b1 = QUADS[u]
                pe.wait_ge(s.h2_ready, section_of(b0) + 1)
                if u >= 2:
                    pe.wait_ge(s.h2t_ready, u - 1)
                for b in range(b0, b1):
                    last = nc.tensor.transpose(turn[u % 2][:, (b - b0) * P:(b - b0 + 1) * P], h2[:, b, :], m.ident[:, :])
                last.then_inc(s.turned2, 1)

            def product(u):
                b0, b1 = QUADS[u]
                pe.wait_ge(s.h2t_ready, u + 1)
                if u >= 2:
                    pe.wait_ge(s.ab_out, u - 1)
                    pe.wait_ge(s.ho_out, u - 1)
                else:
                    pe.wait_ge(s.car1_used, len(QUADS))
                for b in range(b0, b1):
                    at = (b - b0) * P
                    last = nc.tensor.matmul(ab[u % 2][:, at:at + P], h2t[u % 2][:, at:at + P], wab[:, :], start=True, stop=True)
                last.then_inc(s.ab_ready, 1)
                for b in range(b0, b1):
                    at = b - b0
                    last = nc.tensor.matmul(car[u % 2][:, at * C:(at + 1) * C], h2t[u % 2][0:C, at * P:(at + 1) * P], wo2[:, :],
                                            start=True, stop=True)
                last.then_inc(s.ho_ready, 1)

            def carried(u):
                b0, b1 = QUADS[u]
                pe.wait_ge(s.ends_ready, 1)
                if u >= 4:
                    pe.wait_ge(s.car1_used, u - 3)
                for b in range(b0, b1):
                    last = nc.tensor.matmul(ring[u % 4][:, (b - b0) * (C + 1):(b - b0 + 1) * (C + 1)], ends[:, b, :], m.carry1[:, :],
                                            start=True, stop=True)
                last.then_inc(s.car1_ready, 1)

            for u in range(len(QUADS)):
                carried(u)
            for u in range(len(QUADS)):
                turn_quad(u)
                if u and section_of(QUADS[u][0]) == section_of(QUADS[u - 1][0]):
                    product(u - 1)
                if [QUADS[u][1] == e for _, e in SECTIONS].count(True):
                    product(u)

        @block.vector
        def _(dve):
            ch = Chain(dve, s.node_dve)
            nc.vector.memset(wab[C:C + 1, :], 0.0).then_inc(s.wab_zero, 1)
            for q in range(2):
                nc.vector.memset(h2t[q][C:C + 1, :], 1.0).then_inc(s.h2t_ones, 1)

            def normalise(n):
                b0, b1 = SECTIONS[n]
                part = slice(b0, b1)
                dve.wait_ge(s.agg_in[n], 16 * (b1 - b0))
                ch.then_wait(nc.vector.tensor_tensor(agg[:, part, :], agg[:, part, :], over_last(m.has[:, part]), ALU.mult))
                ch.then_wait(nc.vector.tensor_tensor(m.x[:, part, :], m.x[:, part, :], agg[:, part, :], ALU.add))
                variance(nc, ch, s.var2_ready, m.x[:, part, :], xc[:, part, :], h2[:, part, :], stat[:, b0:b1], stat[:, NB + b0:NB + b1])

            def add_half(n):
                b0, b1 = SECTIONS[n]
                dve.wait_ge(s.ho_out, quads_of(n)[-1] + 1)
                ch.then_wait(nc.vector.tensor_tensor(m.x[:, b0:b1, :], m.x[:, b0:b1, :], ho[:, b0:b1, :], ALU.add))

            def copy_out(n):
                for u, (b0, b1) in enumerate(QUADS):
                    if section_of(b0) == n:
                        dve.wait_ge(s.ab_ready, u + 1)
                        quad = ab[u % 2][:, 0:(b1 - b0) * P].rearrange("p (b c) -> p b c", c=2 * C)
                        ch.step(nc.vector.tensor_copy(tab[:, b0:b1, 0:C], quad[:, :, 0:C]))
                        dve.wait_ge(s.node_dve, ch.n)
                        nc.vector.tensor_copy(bd[:, b0:b1, :], quad[:, :, C:2 * C]).then_inc(s.ab_out, 1)

            ends_in(nc, ch, s, m, ends)
            dve.wait_ge(s.node_dve, ch.n)
            dve.sem_inc(s.ends_ready, 1)
            for u, (b0, b1) in enumerate(QUADS):
                dve.wait_ge(s.car1_ready, u + 1)
                quad = ring[u % 4][:, 0:(b1 - b0) * (C + 1)].rearrange("p (b c) -> p b c", c=C + 1)
                ch.step(nc.vector.tensor_tensor(m.x[:, b0:b1, :], m.x[:, b0:b1, :], quad[:, :, 0:C], ALU.add))
                ch.step(nc.vector.tensor_scalar(m.keep[:, b0:b1], quad[:, :, C], -1.0, 1.0, ALU.mult, ALU.add))
                dve.wait_ge(s.node_dve, ch.n)
                dve.sem_inc(s.car1_used, 1)
            normalise(0)
            for n, (b0, b1) in enumerate(SECTIONS):
                relu_of_norm(nc, ch, s.std2_ready, n + 1, h2[:, b0:b1, :], xc[:, b0:b1, :], stat[:, NB + b0:NB + b1]).then_inc(s.h2_ready, 1)
                if n + 1 < len(SECTIONS):
                    normalise(n + 1)
                copy_out(n)
                if n:
                    add_half(n - 1)
            add_half(len(SECTIONS) - 1)
            ch.step(nc.vector.tensor_tensor(m.keep2[:, :], m.keep[:, :], m.has[:, :], ALU.mult))
            dve.wait_ge(s.node_dve, ch.n)


def softmax_phase(nc, d, s, m):
    with ExitStack() as ctx:
        sb = lambda name, shape, dt=fp32: ctx.enter_context(nc.sbuf_tensor(name, shape, dt))
        pb = lambda name, shape: ctx.enter_context(nc.psum_tensor(name, shape, fp32))
        g = [sb(f"ah_src{q}", [P, K, 2 * C]) for q in range(2)]
        idx = m.idx2
        vin = sb("vin", [P, K, C])
        rows = sb("rows2", [P, K, 2 * C])
        unit = lambda name: sb(name, [P, C, K + 1])
        mask = [unit(f"mask2_{q}") for q in range(2)]
        vct = [unit(f"vct{q}") for q in range(2)]
        bexp, zb = unit("bexp"), unit("zb")
        mx = [unit(f"mx{q}") for q in range(2)]
        pw = [unit(f"pw{q}") for q in range(2)]
        wt = [unit(f"wt{q}") for q in range(2)]
        qs, den, num = unit("qs"), unit("den"), unit("num")
        fm, fm_max = sb("fm", [P, C, K]), sb("fm_max", [P, C])
        open_row = sb("open_row", [P, 2 * C])
        open_h2t = sb("open_h2t", [C + 1, P])
        wb = sb("wb", [C + 1, C])
        open_ps = pb("open_ps", [P, BANK])
        tail_ps = pb("tail2_ps", [C, 4, P])
        carry_ps = pb("carry2_ps", [P, BANK])[:, 0:3 * C].rearrange("p (r c) -> p r c", c=C)
        tl = sb("tl", [C, 4, P])
        open_t = sb("open2_t", [C, 3, P + 1])
        w_old, w_new = sb("w_old", [C, P]), sb("w_new", [C, P])
        mm, e_car = sb("mm", [P, C]), sb("e_car", [P, C])
        carry = sb("carry2", [P, 3, C])
        block = ctx.enter_context(nc.Block())
        s2_rows = d.s2.rearrange("(p t) c -> p t c", t=T)
        v_rows = d.v.rearrange("(p t) c -> p t c", t=T)
        LASTP = CHUNKS // 2 - 1

        @block.sync
        def _(sp):
            def load_sources(i, q):
                sp.wait_ge(s.gather2_in[q], 16 * K * i)
                sp.dma_start(idx[q][:, :], d.src_rows[:, bass.ds((i * 2 + q) * K, K)]).then_inc(s.idx2_in[q], 16)

            def load_b(k, first):
                if not first:
                    sp.wait_ge(s.vct_ready, k)
                sp.dma_start(vin[:, :, :], v_rows[:, bass.ds(k * K, K), :]).then_inc(s.v_in, 16)

            def store(k):
                sp.wait_ge(s.rows2_ready, k + 1)
                sp.dma_start(s2_rows[:, bass.ds(k * K, K), :], rows[:, :, :]).then_inc(s.rows2_stored, 16)

            sp.dma_start(wb[0:C, :], d.wlin_t[C:2 * C, 0:C]).then_inc(s.wb_in, 16)
            sp.dma_start(wb[C:C + 1, :], d.b_lin[0:C].unsqueeze(0)).then_inc(s.wb_in, 16)
            load_b(0, True)
            load_b(1, False)
            with sp.Fori(0, LASTP) as i:
                for q in range(2):
                    load_sources(i + 1, q)
                    load_b(i * 2 + q + 2, False)
                    store(i * 2 + q)
            store(CHUNKS - 2)
            store(CHUNKS - 1)
            sp.wait_ge(s.rows2_stored, 16 * CHUNKS)

        @block.gpsimd
        def _(pool):
            def gather(i, q, first):
                if not first:
                    pool.wait_ge(s.q_ready, i * 2 + q - 1)
                pool.wait_ge(s.idx2_in[q], 16 * (i + 1))
                pool.sem_inc(s.idx2_seen, 1)
                for t in range(K):
                    nc.gpsimd.indirect_dma_start(g[q][:, t, :], None, d.tab2,
                                                 bass.IndirectOffsetOnAxis(idx[q][:, t:t + 1], 0)).then_inc(s.gather2_in[q], 16)

            nc.gpsimd.indirect_dma_start(open_row[:, :], None, d.tab2,
                                         bass.IndirectOffsetOnAxis(m.d0_i[:, 0:1], 0)).then_inc(s.open_row_in, 16)
            gather(0, 0, True)
            gather(0, 1, True)
            with pool.Fori(1, CHUNKS // 2) as i:
                gather(i, 0, False)
                gather(i, 1, False)

        @block.scalar
        def _(act):
            def spread(k, q, first):
                if not first:
                    act.wait_ge(s.w_ready, k - 1)
                nc.scalar.copy(mask[q][:, :, 1:], over_channels(m.same[:, bass.ds(k * K, K)])).then_inc(s.mask2_ready, 1)
                act.wait_ge(s.v_in, 16 * (k + 1))
                if not first:
                    act.wait_ge(s.b_ready, k - 1)
                nc.scalar.copy(vct[q][:, :, 1:], vin[:, :, :].rearrange("p t c -> p c t")).then_inc(s.vct_ready, 1)

            def weights(k, q):
                act.wait_ge(s.step_raw, k + 1)
                nc.scalar.activation(wt[q][:, :, 1:], wt[q][:, :, 1:], ACT.Relu).then_inc(s.step_ready, 1)
                act.wait_ge(s.arg_ready, k + 1)
                nc.scalar.activation(pw[q][:, :, 1:], pw[q][:, :, 1:], ACT.Exp).then_inc(s.pw_ready, 1)
                act.wait_ge(s.step_ready, k + 1)
                nc.scalar.activation(wt[q][:, :, 1:], wt[q][:, :, 1:], ACT.Exp, scale=-1.0).then_inc(s.wt_ready, 1)

            def to_rows(k, first):
                act.wait_ge(s.sums_ready, 2 * (k + 1))
                if not first:
                    act.wait_ge(s.rows2_stored, 16 * k)
                nc.scalar.copy(rows[:, :, 0:C], den[:, :, 1:].rearrange("p c t -> p t c")).then_inc(s.den_copied, 1)
                nc.scalar.copy(rows[:, :, C:2 * C], num[:, :, 1:].rearrange("p c t -> p t c")).then_inc(s.num_copied, 1)
                act.wait_ge(s.den_copied, k + 1)
                act.wait_ge(s.num_copied, k + 1)
                act.sem_inc(s.rows2_ready, 1)

            def pair(i, first, last):
                for q in range(2):
                    k = i * 2 + q
                    weights(k, q)
                    if not last:
                        spread(k + 2, q, False)
                    to_rows(k, first and q == 0)

            act.wait_ge(s.mask2_zero, 2)
            spread(0, 0, True)
            spread(1, 1, True)
            pair(0, True, False)
            with act.Fori(1, LASTP) as i:
                pair(i, False, False)
            pair(LASTP, False, True)
            def exp_of(ap, n):
                act.wait_ge(s.exp_asked, n)
                nc.scalar.activation(ap, ap, ACT.Exp).then_inc(s.exp_answered, 1)

            exp_of(w_old[:, :], 1)
            exp_of(w_new[:, :], 2)
            exp_of(m.fix[:, 0, :], 3)
            exp_of(e_car[:, :], 4)

        @block.vector
        def _(dve):
            ch = Chain(dve, s.soft_dve)
            nc.vector.memset(mask[0][:, :, 0:1], 0.0).then_inc(s.mask2_zero, 1)
            nc.vector.memset(mask[1][:, :, 0:1], 0.0).then_inc(s.mask2_zero, 1)
            ch.step(nc.vector.memset(mx[1][:, :, K:K + 1], 0.0))
            ch.step(nc.vector.memset(m.seg_m[:, :], 0.0))
            ch.step(nc.vector.memset(den[:, :, K:K + 1], 0.0))
            ch.step(nc.vector.memset(num[:, :, K:K + 1], 0.0))
            ch.step(nc.vector.memset(wt[0][:, :, 0:1], 0.0))
            ch.step(nc.vector.memset(wt[1][:, :, 0:1], 0.0))
            ch.step(nc.vector.memset(open_h2t[C:C + 1, :], 1.0))
            dve.wait_ge(s.bo_in, 16)
            ch.step(nc.vector.tensor_tensor(m.x[:, :, :], m.x[:, :, :], m.bo[:, :].unsqueeze(1).to_broadcast([P, NB, C]), ALU.add))
            dve.wait_ge(s.open_turned, 1)
            ch.step(nc.vector.tensor_copy(open_h2t[0:C, :], open_ps[0:C, 0:P]))
            dve.wait_ge(s.soft_dve, ch.n)
            dve.sem_inc(s.open_h2t_ready, 1)
            dve.wait_ge(s.b_open_ready, 1)
            ch.then_wait(nc.vector.tensor_copy(bexp[:, :, K], open_ps[:, P:P + C]))

            def scale_step(k, q):
                dve.wait_ge(s.wt_ready, k + 1)
                nc.vector.tensor_tensor(wt[q][:, :, 1:], wt[q][:, :, 1:], mask[q][:, :, 1:], ALU.mult).then_inc(s.w_ready, 1)

            def spread_b(k, q):
                dve.wait_ge(s.vct_ready, k + 1)
                dve.wait_ge(s.mask2_ready, k + 1)
                nc.vector.tensor_copy(vct[q][:, :, 0:1], bexp[:, :, K:K + 1]).then_inc(s.b_carry, 1)
                dve.wait_ge(s.b_carry, k + 1)
                nc.vector.tensor_tensor_scan(flat(bexp[:, :, :]), flat(mask[q][:, :, :]), flat(vct[q][:, :, :]), 0.0,
                                             ALU.mult, ALU.add).then_inc(s.b_ready, 1)

            def attention(i, q, first):
                k = i * 2 + q
                dve.wait_ge(s.gather2_in[q], 16 * K * (i + 1))
                dve.wait_ge(s.b_ready, k + 1)
                nc.vector.tensor_tensor(zb[:, :, 1:], g[q][:, :, 0:C].rearrange("p t c -> p c t"), bexp[:, :, 1:],
                                        ALU.add).then_inc(s.z2_ready, 1)
                nc.vector.tensor_copy(zb[:, :, 0:1], mx[1 - q][:, :, K:K + 1]).then_inc(s.m_carry, 1)
                dve.wait_ge(s.z2_ready, k + 1)
                dve.wait_ge(s.m_carry, k + 1)
                nc.vector.tensor_tensor_scan(flat(mx[q][:, :, :]), flat(mask[q][:, :, :]), flat(zb[:, :, :]), 0.0,
                                             ALU.mult, ALU.max).then_inc(s.mx_ready, 1)
                dve.wait_ge(s.mx_ready, k + 1)
                nc.vector.tensor_tensor(wt[q][:, :, 1:], mx[q][:, :, 1:], mx[q][:, :, 0:K], ALU.subtract).then_inc(s.step_raw, 1)
                nc.vector.scalar_tensor_tensor(pw[q][:, :, 1:], zb[:, :, 1:], 0.0, mx[q][:, :, 1:], ALU.max, ALU.subtract).then_inc(s.arg_ready, 1)

            def first_max(k, q):
                nc.vector.tensor_tensor(fm[:, :, :], mx[q][:, :, 1:], over_channels(m.first[:, bass.ds(k * K, K)]), ALU.mult).then_inc(s.first_masked, 1)
                dve.wait_ge(s.first_masked, k + 1)
                nc.vector.tensor_reduce(fm_max[:, :], fm[:, :, :], AX.X, ALU.max).then_inc(s.first_reduced, 1)
                dve.wait_ge(s.first_reduced, k + 1)
                nc.vector.tensor_tensor(m.seg_m[:, :], m.seg_m[:, :], fm_max[:, :], ALU.max).then_inc(s.first_kept, 1)
                dve.wait_ge(s.first_kept, k + 1)

            def weighted(k, q):
                dve.wait_ge(s.pw_ready, k + 1)
                nc.vector.tensor_tensor(qs[:, :, 1:], pw[q][:, :, 1:], g[q][:, :, C:2 * C].rearrange("p t c -> p c t"),
                                        ALU.mult).then_inc(s.q_ready, 1)
                nc.vector.tensor_copy(pw[q][:, :, 0:1], den[:, :, K:K + 1]).then_inc(s.d_carry, 1)
                nc.vector.tensor_copy(qs[:, :, 0:1], num[:, :, K:K + 1]).then_inc(s.n_carry, 1)

            def sums(k, q, first):
                dve.wait_ge(s.d_carry, k + 1)
                dve.wait_ge(s.w_ready, k + 1)
                if not first:
                    dve.wait_ge(s.rows2_ready, k)
                nc.vector.tensor_tensor_scan(flat(den[:, :, :]), flat(wt[q][:, :, :]), flat(pw[q][:, :, :]), 0.0,
                                             ALU.mult, ALU.add).then_inc(s.sums_ready, 1)
                dve.wait_ge(s.q_ready, k + 1)
                dve.wait_ge(s.n_carry, k + 1)
                nc.vector.tensor_tensor_scan(flat(num[:, :, :]), flat(wt[q][:, :, :]), flat(qs[:, :, :]), 0.0,
                                             ALU.mult, ALU.add).then_inc(s.sums_ready, 1)
                dve.wait_ge(s.sums_ready, 2 * (k + 1))

            def pair(i, first, last):
                for q in range(2):
                    k = i * 2 + q
                    attention(i, q, first)
                    if not (last and q == 1):
                        spread_b(k + 1, 1 - q)
                    weighted(k, q)
                    scale_step(k, q)
                    sums(k, q, first and q == 0)
                    if not (last and q == 1):
                        first_max(k, q)

            spread_b(0, 0)
            pair(0, True, False)
            with dve.Fori(1, LASTP) as i:
                pair(i, False, False)
            pair(LASTP, False, True)
            for r, part in enumerate((mx[1], den, num)):
                ch.step(nc.vector.tensor_copy(m.tail2[:, r, :], part[:, :, K]))
            dve.wait_ge(s.soft_dve, ch.n)
            dve.sem_inc(s.tail2_ready, 1)
            first_max(CHUNKS - 1, 1)
            dve.wait_ge(s.tail2_turned, 1)
            ch.then_wait(nc.vector.tensor_copy(tl[:, :, :], tail_ps[:, :, :]))
            ch.then_wait(nc.vector.memset(open_t[:, :, :], 0.0))
            ch.then_wait(nc.vector.tensor_tensor_scan(open_t[:, 0, 1:], tl[:, 3, :], tl[:, 0, :], 0.0, ALU.mult, ALU.max))
            ch.then_wait(nc.vector.tensor_tensor(w_old[:, :], open_t[:, 0, 0:P], open_t[:, 0, 1:], ALU.subtract))
            nc.vector.tensor_scalar(w_old[:, :], w_old[:, :], 0.0, None, ALU.min).then_inc(s.exp_asked, 1)
            nc.vector.tensor_tensor(w_new[:, :], tl[:, 0, :], open_t[:, 0, 1:], ALU.subtract).then_inc(s.exp_asked, 1)
            dve.wait_ge(s.exp_answered, 2)
            ch.then_wait(nc.vector.tensor_tensor(w_old[:, :], w_old[:, :], tl[:, 3, :], ALU.mult))
            for r in (1, 2):
                ch.then_wait(nc.vector.tensor_tensor(tl[:, r, :], tl[:, r, :], w_new[:, :], ALU.mult))
                ins = nc.vector.tensor_tensor_scan(open_t[:, r, 1:], w_old[:, :], tl[:, r, :], 0.0, ALU.mult, ALU.add)
                if r == 1:
                    ch.then_wait(ins)
                else:
                    ins.then_inc(s.open2_ready, 1)
            dve.wait_ge(s.carry2_turned, 1)
            ch.then_wait(nc.vector.tensor_copy(carry[:, :, :], carry_ps[:, :, :]))
            ch.then_wait(nc.vector.tensor_tensor(mm[:, :], m.seg_m[:, :], carry[:, 0, :], ALU.max))
            nc.vector.tensor_tensor(m.fix[:, 0, :], m.seg_m[:, :], mm[:, :], ALU.subtract).then_inc(s.exp_asked, 1)
            nc.vector.tensor_tensor(e_car[:, :], carry[:, 0, :], mm[:, :], ALU.subtract).then_inc(s.exp_asked, 1)
            dve.wait_ge(s.exp_answered, 4)
            nc.vector.tensor_tensor(m.fix[:, 1:3, :], carry[:, 1:3, :], e_car[:, :].unsqueeze(1).to_broadcast([P, 2, C]),
                                    ALU.mult).then_inc(s.fix_ready, 1)

        @block.tensor
        def _(pe):
            pe.wait_ge(s.open_row_in, 16)
            nc.tensor.transpose(open_ps[0:C, 0:P], open_row[:, C:2 * C], m.ident[:, :]).then_inc(s.open_turned, 1)
            pe.wait_ge(s.wb_in, 32)
            pe.wait_ge(s.open_h2t_ready, 1)
            nc.tensor.matmul(open_ps[:, P:P + C], open_h2t[:, :], wb[:, :], start=True, stop=True).then_inc(s.b_open_ready, 1)
            pe.wait_ge(s.tail2_ready, 1)
            for r in range(3):
                nc.tensor.transpose(tail_ps[:, r, :], m.tail2[:, r, :], m.ident[:, :])
            nc.tensor.transpose(tail_ps[:, 3, :], m.link[:, 0:1].to_broadcast([P, C]), m.ident[:, :]).then_inc(s.tail2_turned, 1)
            pe.wait_ge(s.open2_ready, 1)
            for r in range(3):
                last = nc.tensor.transpose(carry_ps[:, r, :], open_t[:, r, 0:P], m.ident[0:C, 0:C])
            last.then_inc(s.carry2_turned, 1)


def end_phase(nc, d, s, m):
    with ExitStack() as ctx:
        sb = lambda name, shape, dt=fp32: ctx.enter_context(nc.sbuf_tensor(name, shape, dt))
        pb = lambda name, shape: ctx.enter_context(nc.psum_tensor(name, shape, fp32))
        ends = sb("ends2_in", [P, NB, P])
        factor, addend = sb("factor", [P, NB, 2, C]), sb("addend", [P, NB, 2 * C])
        agg = sb("agg2", [P, NB, 2 * C])
        nf = sb("nf", [P, NB, C])
        res = sb("res", [P, NB, C])
        wo = sb("wo", [C, C])
        nft = [sb(f"nft{q}", [C, BANK]) for q in range(2)]
        turn = [pb(f"turn3_{q}", [P, BANK]) for q in range(2)]
        prod = [pb(f"prod{q}", [P, BANK]) for q in range(2)]
        car = [pb(f"car2_{q}", [P, BANK]) for q in range(4)]
        block = ctx.enter_context(nc.Block())

        @block.sync
        def _(sp):
            sp.dma_start(wo[:, :], d.wout_t[0:C, :]).then_inc(s.wo_in, 16)
            out = d.out.rearrange("(p b) c -> p b c", b=NB)
            for n, (b0, b1) in enumerate(END_SECTIONS):
                sp.wait_ge(s.res_ready, [e for _, e in QUADS].index(b1) + 1)
                sp.dma_start(out[:, b0:b1, :], res[:, b0:b1, :]).then_inc(s.out_stored, 16)
            sp.wait_ge(s.out_stored, 16 * len(END_SECTIONS))

        @block.gpsimd
        def _(pool):
            for n, (b0, b1) in enumerate(END_SECTIONS):
                for b in range(b0, b1):
                    nc.gpsimd.indirect_dma_start(agg[:, b, :], None, d.s2,
                                                 bass.IndirectOffsetOnAxis(m.last_i[:, b:b + 1], 0)).then_inc(s.agg2_in[n], 16)

        @block.tensor
        def _(pe):
            pe.wait_ge(s.wo_in, 16)
            pe.wait_ge(s.fix_ready, 1)
            pe.wait_ge(s.ends2_ready, 1)

            def carried(u):
                b0, b1 = QUADS[u]
                if u >= 4:
                    pe.wait_ge(s.factor_out, u - 3)
                for b in range(b0, b1):
                    last = nc.tensor.matmul(car[u % 4][:, (b - b0) * C:(b - b0 + 1) * C], ends[:, b, :], m.fix[:, 0, :], start=True, stop=True)
                last.then_inc(s.factor_ready, 1)
                if u >= 2:
                    pe.wait_ge(s.addend_out, u - 1)
                for b in range(b0, b1):
                    last = nc.tensor.matmul(turn[u % 2][:, (b - b0) * 2 * C:(b - b0 + 1) * 2 * C], ends[:, b, :],
                                            m.fix[:, 1:3, :].rearrange("p r c -> p (r c)"), start=True, stop=True)
                last.then_inc(s.addend_ready, 1)

            def turn_quad(u):
                b0, b1 = QUADS[u]
                n = section_of(b0, END_SECTIONS)
                pe.wait_ge(s.nf_ready, n + 1)
                pe.wait_ge(s.addend_out, 1 + quads_of(min(n + 2, len(END_SECTIONS) - 1), END_SECTIONS)[-1])
                if u >= 2:
                    pe.wait_ge(s.nft_ready, u - 1)
                for b in range(b0, b1):
                    last = nc.tensor.transpose(turn[u % 2][0:C, (b - b0) * P:(b - b0 + 1) * P], nf[:, b, :], m.ident[:, :])
                last.then_inc(s.turned3, 1)

            def product(u):
                b0, b1 = QUADS[u]
                pe.wait_ge(s.nft_ready, u + 1)
                if u >= 2:
                    pe.wait_ge(s.res_ready, u - 1)
                for b in range(b0, b1):
                    last = nc.tensor.matmul(prod[u % 2][:, (b - b0) * C:(b - b0 + 1) * C],
                                            nft[u % 2][:, (b - b0) * P:(b - b0 + 1) * P], wo[:, :], start=True, stop=True)
                last.then_inc(s.prod_ready, 1)

            for n in range(-2, len(END_SECTIONS)):
                if n + 2 < len(END_SECTIONS):
                    for u in quads_of(n + 2, END_SECTIONS):
                        carried(u)
                if n >= 0:
                    for work in (turn_quad, product):
                        for u in quads_of(n, END_SECTIONS):
                            work(u)

        @block.scalar
        def _(act):
            def copy_addend(u):
                b0, b1 = QUADS[u]
                act.wait_ge(s.addend_ready, u + 1)
                nc.scalar.copy(addend[:, b0:b1, :], turn[u % 2][:, 0:(b1 - b0) * 2 * C].rearrange("p (b c) -> p b c", c=2 * C)).then_inc(s.addend_out, 1)

            def copy_turned(u):
                b0, b1 = QUADS[u]
                act.wait_ge(s.turned3, u + 1)
                if u >= 2:
                    act.wait_ge(s.prod_ready, u - 1)
                nc.scalar.copy(nft[u % 2][:, 0:(b1 - b0) * P], turn[u % 2][0:C, 0:(b1 - b0) * P]).then_inc(s.nft_ready, 1)

            for n in range(-2, len(END_SECTIONS)):
                if n + 2 < len(END_SECTIONS):
                    for u in quads_of(n + 2, END_SECTIONS):
                        copy_addend(u)
                if n >= 0:
                    for u in quads_of(n, END_SECTIONS):
                        copy_turned(u)

        @block.vector
        def _(dve):
            ch = Chain(dve, s.end_dve)
            ends_in(nc, ch, s, m, ends)
            dve.wait_ge(s.end_dve, ch.n)
            dve.sem_inc(s.ends2_ready, 1)
            def factors(n):
                for u in quads_of(n, END_SECTIONS):
                    b0, b1 = QUADS[u]
                    dve.wait_ge(s.factor_ready, u + 1)
                    quad = car[u % 4][:, 0:(b1 - b0) * C].rearrange("p (b c) -> p b c", c=C)
                    ch.step(nc.vector.tensor_tensor(factor[:, b0:b1, 0, :], quad, over_last(m.keep[:, b0:b1]), ALU.add))
                    ch.step(nc.vector.tensor_tensor(factor[:, b0:b1, 1, :], quad, over_last(m.keep2[:, b0:b1]), ALU.add))
                    dve.wait_ge(s.end_dve, ch.n)
                    dve.sem_inc(s.factor_out, 1)

            def divide(n):
                b0, b1 = END_SECTIONS[n]
                own = agg[:, b0:b1, :]
                dve.wait_ge(s.agg2_in[n], 16 * (b1 - b0))
                ch.then_wait(nc.vector.tensor_tensor(own, own, factor[:, b0:b1, :, :].rearrange("p b r c -> p b (r c)"), ALU.mult))
                dve.wait_ge(s.addend_out, quads_of(n, END_SECTIONS)[-1] + 1)
                ch.then_wait(nc.vector.tensor_tensor(own, own, addend[:, b0:b1, :], ALU.add))
                ch.then_wait(nc.vector.reciprocal(own[:, :, 0:C], own[:, :, 0:C]))
                nc.vector.tensor_tensor(nf[:, b0:b1, :], own[:, :, C:2 * C], own[:, :, 0:C], ALU.mult).then_inc(s.nf_ready, 1)

            def results(n):
                for u in quads_of(n, END_SECTIONS):
                    b0, b1 = QUADS[u]
                    dve.wait_ge(s.prod_ready, u + 1)
                    nc.vector.tensor_tensor(res[:, b0:b1, :], prod[u % 2][:, 0:(b1 - b0) * C].rearrange("p (b c) -> p b c", c=C),
                                            m.x[:, b0:b1, :], ALU.add).then_inc(s.res_ready, 1)

            factors(0)
            factors(1)
            divide(0)
            for n in range(len(END_SECTIONS)):
                if n + 2 < len(END_SECTIONS):
                    factors(n + 2)
                if n + 1 < len(END_SECTIONS):
                    divide(n + 1)
                results(n)


class Semaphores:

    def __init__(self, sem):
        self.table_in = sem("table_in")
        self.table_ready = sem("table_ready")
        self.table_dve = sem("table_dve")
        self.below_ready = sem("below_ready")
        self.turn_moved = sem("turn_moved")
        self.found_used = sem("found_used")
        self.ends_ready = sem("ends_ready")
        self.car1_ready = sem("car1_ready")
        self.car1_used = sem("car1_used")
        self.b_open_ready = sem("b_open_ready")
        self.open_row_in = sem("open_row_in")
        self.open_turned = sem("open_turned")
        self.open_h2t_ready = sem("open_h2t_ready")
        self.wb_in = sem("wb_in")
        self.first_masked = sem("first_masked")
        self.first_reduced = sem("first_reduced")
        self.first_kept = sem("first_kept")
        self.ends2_ready = sem("ends2_ready")
        self.fix_ready = sem("fix_ready")
        self.tail2_ready = sem("tail2_ready")
        self.factor_ready = sem("factor_ready")
        self.factor_out = sem("factor_out")
        self.addend_ready = sem("addend_ready")
        self.addend_out = sem("addend_out")
        self.ho_ready = sem("ho_ready")
        self.ho_out = sem("ho_out")
        self.dst_in = sem("dst_in")
        self.h1_ready = sem("h1_ready")
        self.h1_stored = sem("h1_stored")
        self.w_in = sem("w_in")
        self.w3_in = sem("w3_in")
        self.var1_ready = sem("var1_ready")
        self.xc1_ready = sem("xc1_ready")
        self.sq1_ready = sem("sq1_ready")
        self.std1_ready = sem("std1_ready")
        self.setup_dve = sem("setup_dve")
        self.cnt_ready = sem("cnt_ready")
        self.cnt_stored = sem("cnt_stored")
        self.start_in = sem("start_in")
        self.z_ready = sem("z_ready")
        self.hw_ready = sem("hw_ready")
        self.v_zeroed = sem("v_zeroed")
        self.rows1_ready = sem("rows1_ready")
        self.msg_ready = sem("msg_ready")
        self.sp_ready = sem("sp_ready")
        self.tail1_ready = sem("tail1_ready")
        self.tail1_turned = sem("tail1_turned")
        self.open1_ready = sem("open1_ready")
        self.carry1_ready = sem("carry1_ready")
        self.z_clamped = sem("z_clamped")
        self.exp_ready = sem("exp_ready")
        self.log_ready = sem("log_ready")
        self.scan1_ready = sem("scan1_ready")
        self.mask1_ready = sem("mask1_ready")
        self.mask1_zero = sem("mask1_zero")
        self.sum_dve = sem("sum_dve")
        self.msg_scaled = sem("msg_scaled")
        self.carry1_in = sem("carry1_in")
        self.v_stored = sem("v_stored")
        self.wab_in = sem("wab_in")
        self.wab_zero = sem("wab_zero")
        self.tab_stored = sem("tab_stored")
        self.var2_ready = sem("var2_ready")
        self.std2_ready = sem("std2_ready")
        self.h2_ready = sem("h2_ready")
        self.tab_h2 = sem("tab_h2")
        self.turned2 = sem("turned2")
        self.ab_ready = sem("ab_ready")
        self.h2t_ones = sem("h2t_ones")
        self.h2t_ready = sem("h2t_ready")
        self.ab_out = sem("ab_out")
        self.node_dve = sem("node_dve")
        self.vct_ready = sem("vct_ready")
        self.v_in = sem("v_in")
        self.mx_ready = sem("mx_ready")
        self.rows2_ready = sem("rows2_ready")
        self.rows2_stored = sem("rows2_stored")
        self.q_ready = sem("q_ready")
        self.w_ready = sem("w_ready")
        self.mask2_ready = sem("mask2_ready")
        self.b_ready = sem("b_ready")
        self.arg_ready = sem("arg_ready")
        self.step_ready = sem("step_ready")
        self.pw_ready = sem("pw_ready")
        self.wt_ready = sem("wt_ready")
        self.sums_ready = sem("sums_ready")
        self.den_copied = sem("den_copied")
        self.num_copied = sem("num_copied")
        self.mask2_zero = sem("mask2_zero")
        self.soft_dve = sem("soft_dve")
        self.b_carry = sem("b_carry")
        self.z2_ready = sem("z2_ready")
        self.m_carry = sem("m_carry")
        self.d_carry = sem("d_carry")
        self.n_carry = sem("n_carry")
        self.wo_in = sem("wo_in")
        self.bo_in = sem("bo_in")
        self.res_ready = sem("res_ready")
        self.out_stored = sem("out_stored")
        self.tail2_turned = sem("tail2_turned")
        self.open2_ready = sem("open2_ready")
        self.carry2_turned = sem("carry2_turned")
        self.nf_ready = sem("nf_ready")
        self.nft_ready = sem("nft_ready")
        self.turned3 = sem("turned3")
        self.prod_ready = sem("prod_ready")
        self.exp_asked = sem("exp_asked")
        self.exp_answered = sem("exp_answered")
        self.end_dve = sem("end_dve")
        self.w23_zero = sem("w23_zero")
        self.idx1_seen = sem("idx1_seen")
        self.idx2_seen = sem("idx2_seen")
        self.iota_ready = sem("iota_ready")
        self.prepare_dve = sem("prepare_dve")
        self.prepared = sem("prepared")
        self.rows1_stored = sem("rows1_stored")
        self.step_raw = sem("step_raw")
        self.zeros_ready = sem("zeros_ready")
        self.rbf_in = [sem(f"rbf_in{q}") for q in range(2)]
        self.ef_in = [sem(f"ef_in{q}") for q in range(2)]
        self.gather1_in = [sem(f"gather1_in{q}") for q in range(2)]
        self.gather2_in = [sem(f"gather2_in{q}") for q in range(2)]
        self.idx1_in = [sem(f"idx1_in{q}") for q in range(2)]
        self.idx2_in = [sem(f"idx2_in{q}") for q in range(2)]
        self.found_ready = [sem(f"found_ready{q}") for q in range(2)]
        self.last_in = [sem(f"last_in{j}") for j in range(GROUPS)]
        self.agg2_in = [sem(f"agg2_in{n}") for n in range(len(END_SECTIONS))]
        self.x_in = [sem(f"x_in{n}") for n in range(len(SETUP_SECTIONS))]
        self.agg_in = [sem(f"agg_in{n}") for n in range(len(SECTIONS))]


class Dram:

    def __init__(self, nc, x, src, dst_ext, dst_rows, rbf_t, ef_t, W1, b1, W2, b2, W3, b3, wlin_t, b_lin, wout_t, b_out, out):
        self.x = x
        self.src_rows = src.rearrange("(p t) -> p t", t=T)
        self.dst_ext = dst_ext
        self.dst_rows = dst_rows
        self.rbf_t = rbf_t
        self.ef_t = ef_t
        self.W1 = W1
        self.b1 = b1
        self.W2 = W2
        self.b2 = b2
        self.W3 = W3
        self.b3 = b3
        self.wlin_t = wlin_t
        self.b_lin = b_lin
        self.wout_t = wout_t
        self.b_out = b_out
        self.out = out
        self.h1_tab = nc.dram_tensor("h1_tab", [NODES_PAD, C], fp32).ap()
        self.cnt_tab = nc.dram_tensor("cnt_tab", [NODES_PAD + 1, 1], fp32).ap()
        self.s1 = nc.dram_tensor("s1", [EDGES_PAD, C], fp32).ap()
        self.v = nc.dram_tensor("v", [EDGES_PAD, C], fp32).ap()
        self.tab2 = nc.dram_tensor("tab2", [NODES_PAD, 2 * C], fp32).ap()
        self.s2 = nc.dram_tensor("s2", [EDGES_PAD, 2 * C], fp32).ap()


class Resident:

    def __init__(self, sb):
        self.x = sb("x_sb", [P, NB, C])
        self.node_i = sb("node_i", [P, NB], i32)
        self.same = sb("same", [P, T])
        self.ident = sb("ident", [P, P])
        self.ident_i = sb("ident_i", [P, P], i32)
        self.node = sb("node", [P, NB])
        self.cnt = sb("cnt", [P, NB])
        self.start = sb("start", [P, NB])
        self.has = sb("has", [P, NB])
        self.tmp = sb("tmp", [P, NB])
        self.last_i = sb("last_i", [P, NB], i32)
        self.start_i = sb("start_i", [P, NB], i32)
        self.d0 = sb("d0", [P, 1])
        self.d0_i = sb("d0_i", [P, 1], i32)
        self.turn_node = sb("turn_node", [P, WB, P])
        self.first = sb("first", [P, T])
        self.carried = sb("carried", [P, 1])
        self.carry1 = sb("carry1", [P, C + 1])
        self.keep = sb("keep", [P, NB])
        self.keep2 = sb("keep2", [P, NB])
        self.seg_m = sb("seg_m", [P, C])
        self.idx2 = [sb(f"idx2_{q}", [P, K], i32) for q in range(2)]
        self.bo = sb("bo", [P, C])
        self.fix = sb("fix", [P, 3, C])
        self.link = sb("link", [P, 1])
        self.tail2 = sb("tail2", [P, 3, C])
        self.w1h = sb("w1h", [RBF, C])
        self.b1h = sb("b1h", [C, 1])
        self.w23 = sb("w23", [P, 2 * C])
        self.w1_raw = sb("w1_raw", [RBF, C])
        self.w2_raw = sb("w2_raw", [C, C])
        self.b1_raw = sb("b1_raw", [C, 1])
        self.b23_f = sb("b23_f", [3, 2 * C])
        self.b23_hi = sb("b23_hi", [3, 2 * C], bf16)
        self.b23_mid = sb("b23_mid", [3, 2 * C], bf16)
        self.b23_lo = sb("b23_lo", [3, 2 * C], bf16)
        self.b23_r = sb("b23_r", [3, 2 * C])
        self.b23_s = sb("b23_s", [3, 2 * C])
        self.bias_ones = sb("bias_ones", [3, P], bf16)
        self.bias_rows = sb("bias_rows", [3, GROUP * 2 * C], bf16)


class Early:

    def __init__(self, sb):
        self.dst_i = sb("dst_i", [P, T + 2], i32)
        self.dst_f = sb("dst_f", [P, T + 2])
        self.ends = sb("ends", [P, 1])
        self.table_i = sb("table_i", [RP, RC + 1, ROW], i32)
        self.table = sb("table", [RP, RC, ROW + 1])
        self.table_hi = sb("table_hi", [RP, RC, ROW + 1], bf16)
        self.table_lo = sb("table_lo", [RP, RC, ROW + 1], bf16)
        self.table_first = sb("table_first", [RP, RC])
        self.table_row_i = sb("table_row_i", [RP, RC], i32)
        self.turn_i = sb("turn_i", [P, WB, P], i32)
        self.search_node = sb("search_node", [P, WB])


def gnn_kernel(nc, x, src, dst_ext, dst_rows, rbf_t, ef_t, W1, b1, W2, b2, W3, b3, wlin_t, b_lin, wout_t,
               b_out, out):
    d = Dram(nc, x, src, dst_ext, dst_rows, rbf_t, ef_t, W1, b1, W2, b2, W3, b3, wlin_t, b_lin, wout_t, b_out, out)
    with ExitStack() as ctx:
        sb = lambda name, shape, dt=fp32: ctx.enter_context(nc.sbuf_tensor(name, shape, dt))
        s = Semaphores(lambda name: ctx.enter_context(nc.semaphore(name)))
        m = Resident(sb)
        with ExitStack() as early:
            m.early = Early(lambda name, shape, dt=fp32: early.enter_context(nc.sbuf_tensor(name, shape, dt)))
            setup_phase(nc, d, s, m)
            sum_phase(nc, d, s, m)
        node_phase(nc, d, s, m)
        softmax_phase(nc, d, s, m)
        end_phase(nc, d, s, m)


def kernel(x, src, dst, edge_attr_128, edge_attr_64, L0_gnn_W1, L0_gnn_b1, L0_gnn_W2, L0_gnn_b2, L0_gnn_W3,
           L0_gnn_b3, L1_gnn_W_lin, L1_gnn_b_lin, L1_gnn_W_out, L1_gnn_b_out):
    import numpy as np
    import concourse.bacc as bacc
    from concourse.bass_utils import run_bass_kernel_spmd

    def padded(a, rows, fill=0):
        a = np.asarray(a)
        return np.concatenate([a, np.full((rows - a.shape[0],) + a.shape[1:], fill, a.dtype)])

    def by_column(a):
        return np.ascontiguousarray(padded(a, EDGES_PAD).reshape(P, T, -1).transpose(2, 1, 0)).reshape(-1, T * P)

    dst_pad = padded(dst, EDGES_PAD, NODES)
    before = np.concatenate([np.full((1,), -1, dst_pad.dtype), dst_pad[:-1]])
    after = np.concatenate([dst_pad[1:], np.full((1,), -1, dst_pad.dtype)])
    arrays = {
        "in_x": padded(x, NODES_PAD),
        "in_src": padded(src, EDGES_PAD),
        "in_dst_ext": np.concatenate([before.reshape(P, T)[:, :1], dst_pad.reshape(P, T), after.reshape(P, T)[:, -1:]], axis=1),
        "in_dst_rows": dst_pad.reshape(ROWS, ROW),
        "in_rbf_t": by_column(edge_attr_128),
        "in_ef_t": by_column(edge_attr_64),
        "in_W1": np.asarray(L0_gnn_W1), "in_b1": np.asarray(L0_gnn_b1),
        "in_W2": np.asarray(L0_gnn_W2), "in_b2": np.asarray(L0_gnn_b2),
        "in_W3": np.asarray(L0_gnn_W3), "in_b3": np.asarray(L0_gnn_b3),
        "in_wlin_t": np.ascontiguousarray(np.asarray(L1_gnn_W_lin).T), "in_b_lin": np.asarray(L1_gnn_b_lin),
        "in_wout_t": np.ascontiguousarray(np.asarray(L1_gnn_W_out).T), "in_b_out": np.asarray(L1_gnn_b_out),
    }
    nc = bacc.Bacc("TRN2", target_bir_lowering=False, num_devices=1)
    args = [nc.dram_tensor(n, a.shape, mybir.dt.from_np(a.dtype), kind="ExternalInput").ap() for n, a in arrays.items()]
    args.append(nc.dram_tensor("out_x", (NODES_PAD, C), fp32, kind="ExternalOutput").ap())
    gnn_kernel(nc, *args)
    r = run_bass_kernel_spmd(nc, [arrays], core_ids=[0])
    return r.results[0]["out_x"][:NODES]
```
